# Optimizing a Trainium2 kernel written in Bass

```python
import numpy as np
import jax
import jax.numpy as jnp

def _softmax(x, axis=-1):
    return jax.nn.softmax(x, axis=axis)

def _gelu(x):
    return jax.nn.gelu(x, approximate=True)

def _silu(x):
    return jax.nn.silu(x)

def _sigmoid(x):
    return jax.nn.sigmoid(x)

def _layernorm(x, axis=-1, eps=1e-05):
    m = jnp.mean(x, axis=axis, keepdims=True)
    v = jnp.var(x, axis=axis, keepdims=True)
    return (x - m) / jnp.sqrt(v + eps)

def _scatter_add(tgt, idx, src, axis=0):
    return tgt.at[idx].add(src)

def _segment_sum(src, seg, n):
    return jax.ops.segment_sum(src, seg, n)
kernel_name = 'mk_decoder_preln_d2_seqx_r4_6cd10b'

def setup_inputs(seed: int=0):
    np.random.seed(seed)
    _w = jnp.asarray

    def _rec_inputs():
        import jax
        import jax.numpy as jnp
        _rk = jax.random.key(seed)
        x = -0.0005857 + 0.9999 * jax.random.normal(jax.random.fold_in(_rk, 1), (32, 112, 256), jnp.float32)
        _lenS = 112 - jax.random.randint(jax.random.fold_in(_rk, 7), (32,), 0, max(1, 112 // 4) + 1, jnp.int32)
        _lenS2 = 375 - jax.random.randint(jax.random.fold_in(_rk, 8), (32,), 0, max(1, 375 // 4) + 1, jnp.int32)
        _ctx_1024P = jax.random.normal(jax.random.fold_in(_rk, 11), (32, 16, 256), jnp.float32)
        _ctx_1024c = jax.random.dirichlet(jax.random.fold_in(_rk, 511), 0.3 * jnp.ones((16,), jnp.float32), (32, 375))
        _ctx_1024t = jnp.einsum('bsk,bkd->bsd', _ctx_1024c, _ctx_1024P)
        _ctx_1024t = _ctx_1024t * jax.lax.rsqrt(jnp.mean(jnp.square(_ctx_1024t)) + 1e-12) * 0.953939
        ctx_1024 = -0.000264403 + 1.00002 * (_ctx_1024t + 0.3 * jax.random.normal(jax.random.fold_in(_rk, 611), (32, 375, 256), jnp.float32))
        _validS = jnp.arange(112)[None, :] < _lenS[:, None]
        _validS2 = jnp.arange(375)[None, :] < _lenS2[:, None]
        _causal = jnp.tril(jnp.ones((112, 112), dtype=bool))
        mask_1x1xSxS2_if1 = jnp.where(jnp.ones((1, 1, 112, 375), dtype=bool), 1, 0).astype(jnp.int32)
        mask_BxS2_bf1 = jnp.ones((32, 375), dtype=bool)
        return (x, ctx_1024, mask_1x1xSxS2_if1, mask_BxS2_bf1)
    x, ctx_1024, mask_1x1xSxS2_if1, mask_BxS2_bf1 = _rec_inputs()

    def _L0_attn_setup():
        import jax, jax.numpy as jnp
        import numpy as np
        B, L, D_MODEL = (2, 512, 256)
        D_STATE, D_CONV, EXPAND = (8, 4, 2)
        D_INNER = EXPAND * D_MODEL
        DT_RANK = (D_MODEL + 15) // 16
        key = jax.random.key(seed)
        ks = jax.random.split(key, 8)
        s = 0.02
        x = jax.random.normal(ks[0], (B, L, D_MODEL), dtype=jnp.float32)
        W_in = jax.random.normal(ks[1], (D_MODEL, 2 * D_INNER), dtype=jnp.float32) * s
        dw_kernel = jax.random.normal(ks[2], (D_CONV, D_INNER), dtype=jnp.float32) * s
        pw_kernel = jax.random.normal(ks[3], (D_INNER, D_INNER), dtype=jnp.float32) * s
        conv_bias = jnp.zeros((D_INNER,), dtype=jnp.float32)
        W_x = jax.random.normal(ks[4], (D_INNER, DT_RANK + 2 * D_STATE), dtype=jnp.float32) * s
        W_dt = jax.random.normal(ks[5], (DT_RANK, D_INNER), dtype=jnp.float32) * s
        b_dt = jnp.zeros((D_INNER,), dtype=jnp.float32)
        A_init = np.repeat(np.arange(1, D_STATE + 1, dtype=np.float32), D_INNER).reshape(D_INNER, D_STATE)
        A_log = jnp.asarray(np.log(A_init))
        D = jnp.ones((D_INNER,), dtype=jnp.float32)
        W_out = jax.random.normal(ks[6], (D_INNER, D_MODEL), dtype=jnp.float32) * s
        return {'x': x, 'W_in': W_in, 'dw_kernel': dw_kernel, 'pw_kernel': pw_kernel, 'conv_bias': conv_bias, 'W_x': W_x, 'W_dt': W_dt, 'b_dt': b_dt, 'A_log': A_log, 'D': D, 'W_out': W_out}
    _L0_attn_all = _L0_attn_setup()
    _L0_attn_in = {k: v for k, v in _L0_attn_all.items() if k in ('W_in', 'dw_kernel', 'pw_kernel', 'conv_bias', 'W_x', 'W_dt', 'b_dt', 'A_log', 'D', 'W_out')}
    del _L0_attn_all

    def _L0_xattn_setup():
        import jax, jax.numpy as jnp
        import numpy as np
        B, S, D, H = (2, 512, 256, 16)
        DK = D // H
        key = jax.random.key(seed)
        ks = jax.random.split(key, 8)

        def lin(k):
            kw, kb = jax.random.split(k)
            w = jax.random.normal(kw, (D, D), dtype=jnp.float32) / np.sqrt(D)
            b = jax.random.normal(kb, (D,), dtype=jnp.float32) * 0.01
            return (w, b)
        wq, bq = lin(ks[0])
        wk, bk = lin(ks[1])
        wv, bv = lin(ks[2])
        wo, bo = lin(ks[3])
        return {'q': jax.random.normal(ks[4], (B, S, D), dtype=jnp.float32), 'k': jax.random.normal(ks[5], (B, S, D), dtype=jnp.float32), 'v': jax.random.normal(ks[6], (B, S, D), dtype=jnp.float32), 'mask': jnp.ones((1, 1, S, S), dtype=jnp.int32), 'wq': wq, 'bq': bq, 'wk': wk, 'bk': bk, 'wv': wv, 'bv': bv, 'wo': wo, 'bo': bo}
    _L0_xattn_all = _L0_xattn_setup()
    _L0_xattn_in = {k: v for k, v in _L0_xattn_all.items() if k in ('wq', 'bq', 'wk', 'bk', 'wv', 'bv', 'wo', 'bo')}
    del _L0_xattn_all

    def _L0_ffn_setup():
        import jax, jax.numpy as jnp
        import numpy as np
        B, S, D = (4, 512, 256)
        E = 8
        CF = 1
        key = jax.random.key(seed)
        k_x, k_g, k_w, k_b = jax.random.split(key, 4)
        x = jax.random.normal(k_x, (B, S, D), dtype=jnp.float32)
        Wg = jax.random.normal(k_g, (D, E), dtype=jnp.float32) * (1.0 / np.sqrt(D))
        We = jax.random.normal(k_w, (D, D), dtype=jnp.float32) * (1.0 / np.sqrt(D))
        be = jax.random.normal(k_b, (D,), dtype=jnp.float32) * 0.01
        return {'x': x, 'Wg': Wg, 'We': We, 'be': be}
    _L0_ffn_all = _L0_ffn_setup()
    _L0_ffn_in = {k: v for k, v in _L0_ffn_all.items() if k in ('Wg', 'We', 'be')}
    del _L0_ffn_all

    def _L1_attn_setup():
        import jax, jax.numpy as jnp
        import numpy as np
        B, N, C = (8, 1024, 256)
        key = jax.random.key(seed)
        k1, k2, k3 = jax.random.split(key, 3)
        x = jax.random.normal(k1, (B, N, C), dtype=jnp.float32)
        w_qkv = jax.random.normal(k2, (3 * C, C), dtype=jnp.float32) * C ** (-0.5)
        w_conv1 = jax.random.normal(k3, (C,), dtype=jnp.float32) * C ** (-0.5)
        return {'x': x, 'w_qkv': w_qkv, 'w_conv1': w_conv1}
    _L1_attn_all = _L1_attn_setup()
    _L1_attn_in = {k: v for k, v in _L1_attn_all.items() if k in ('w_qkv', 'w_conv1')}
    del _L1_attn_all

    def _L1_xattn_setup():
        import jax, jax.numpy as jnp
        import numpy as np
        NEG_INF = -10000000000.0
        key = jax.random.key(seed)
        ks = jax.random.split(key, 8)
        B, S, D = (4, 512, 256)
        scale = 1.0 / np.sqrt(D)
        return {'query': jax.random.normal(ks[0], (B, S, D), jnp.float32), 'key': jax.random.normal(ks[1], (B, S, D), jnp.float32), 'value': jax.random.normal(ks[2], (B, S, D), jnp.float32), 'key_padding_mask': jnp.ones((B, S), dtype=bool), 'Wq': jax.random.normal(ks[3], (D, D), jnp.float32) * scale, 'Wk': jax.random.normal(ks[4], (D, D), jnp.float32) * scale, 'Wv': jax.random.normal(ks[5], (D, D), jnp.float32) * scale, 'Wo': jax.random.normal(ks[6], (D, D), jnp.float32) * scale, 'bo': jnp.zeros((D,), jnp.float32)}
    _L1_xattn_all = _L1_xattn_setup()
    _L1_xattn_in = {k: v for k, v in _L1_xattn_all.items() if k in ('Wq', 'Wk', 'Wv', 'Wo', 'bo')}
    del _L1_xattn_all

    def _L1_ffn_setup():
        import jax, jax.numpy as jnp
        import numpy as np
        import math
        D = 256
        H = 16
        E = 8
        TOPK = 2
        LAT = D // 2
        KPH = LAT // H
        HD = D // H

        def _forward(hs, q_w, q_b, k_w, k_b, v_w, v_b, o_w, o_b, router_w, router_b, w1, b1, w2, b2):
            B, S, _ = hs.shape
            Q = (hs @ q_w + q_b).reshape(B, S, H, HD).transpose(0, 2, 1, 3)
            K = (hs @ k_w + k_b).reshape(B, S, H, KPH).transpose(0, 2, 1, 3)
            V = (hs @ v_w + v_b).reshape(B, S, H, KPH).transpose(0, 2, 1, 3)
            scores = jnp.einsum('bhsk,bhtk->bhst', Q[..., :KPH], K) / math.sqrt(KPH)
            attn = jax.nn.softmax(scores, axis=-1)
            ao = jnp.einsum('bhst,bhtv->bhsv', attn, V)
            ao = ao.transpose(0, 2, 1, 3).reshape(B, S, H * KPH)
            ao = jnp.concatenate([ao, jnp.zeros((B, S, D - LAT), ao.dtype)], axis=-1)
            mla_out = ao @ o_w + o_b
            probs = jax.nn.softmax(mla_out @ router_w + router_b, axis=-1)
            topw, topi = jax.lax.top_k(probs, TOPK)
            topw = topw / (topw.sum(-1, keepdims=True) + 1e-08)
            combine = jnp.sum(jax.nn.one_hot(topi, E, dtype=probs.dtype) * topw[..., None], axis=-2)
            h1 = jnp.einsum('bsd,edf->ebsf', mla_out, w1) + b1[:, None, None, :]
            h1 = jax.nn.gelu(h1, approximate=False)
            h2 = jnp.einsum('ebsf,efd->ebsd', h1, w2) + b2[:, None, None, :]
            moe_out = jnp.einsum('bse,ebsd->bsd', combine, h2)
            return hs + 0.3 * moe_out
        key = jax.random.key(seed)
        ks = jax.random.split(key, 16)
        s = 0.02
        inp = {'hidden_states': jax.random.normal(ks[0], (2, 512, D), jnp.float32), 'q_w': jax.random.normal(ks[1], (D, D), jnp.float32) * s, 'q_b': jnp.zeros((D,), jnp.float32), 'k_w': jax.random.normal(ks[2], (D, LAT), jnp.float32) * s, 'k_b': jnp.zeros((LAT,), jnp.float32), 'v_w': jax.random.normal(ks[3], (D, LAT), jnp.float32) * s, 'v_b': jnp.zeros((LAT,), jnp.float32), 'o_w': jax.random.normal(ks[4], (D, D), jnp.float32) * s, 'o_b': jnp.zeros((D,), jnp.float32), 'router_w': jax.random.normal(ks[5], (D, E), jnp.float32) * s, 'router_b': jnp.zeros((E,), jnp.float32), 'w1': jax.random.normal(ks[6], (E, D, 2 * D), jnp.float32) * s, 'b1': jnp.zeros((E, 2 * D), jnp.float32), 'w2': jax.random.normal(ks[7], (E, 2 * D, D), jnp.float32) * s, 'b2': jnp.zeros((E, D), jnp.float32)}
        return inp
    _L1_ffn_all = _L1_ffn_setup()
    _L1_ffn_in = {k: v for k, v in _L1_ffn_all.items() if k in ('q_w', 'q_b', 'k_w', 'k_b', 'v_w', 'v_b', 'o_w', 'o_b', 'router_w', 'router_b', 'w1', 'b1', 'w2', 'b2')}
    del _L1_ffn_all
    return {'x': x, 'ctx_1024': ctx_1024, 'mask_1x1xSxS2_if1': mask_1x1xSxS2_if1, 'mask_BxS2_bf1': mask_BxS2_bf1, 'L0_attn_W_in': _L0_attn_in['W_in'], 'L0_attn_dw_kernel': _L0_attn_in['dw_kernel'], 'L0_attn_pw_kernel': _L0_attn_in['pw_kernel'], 'L0_attn_conv_bias': _L0_attn_in['conv_bias'], 'L0_attn_W_x': _L0_attn_in['W_x'], 'L0_attn_W_dt': _L0_attn_in['W_dt'], 'L0_attn_b_dt': _L0_attn_in['b_dt'], 'L0_attn_A_log': _L0_attn_in['A_log'], 'L0_attn_D': _L0_attn_in['D'], 'L0_attn_W_out': _L0_attn_in['W_out'], 'L0_xattn_wq': _L0_xattn_in['wq'], 'L0_xattn_bq': _L0_xattn_in['bq'], 'L0_xattn_wk': _L0_xattn_in['wk'], 'L0_xattn_bk': _L0_xattn_in['bk'], 'L0_xattn_wv': _L0_xattn_in['wv'], 'L0_xattn_bv': _L0_xattn_in['bv'], 'L0_xattn_wo': _L0_xattn_in['wo'], 'L0_xattn_bo': _L0_xattn_in['bo'], 'L0_ffn_Wg': _L0_ffn_in['Wg'], 'L0_ffn_We': _L0_ffn_in['We'], 'L0_ffn_be': _L0_ffn_in['be'], 'L1_attn_w_qkv': _L1_attn_in['w_qkv'], 'L1_attn_w_conv1': _L1_attn_in['w_conv1'], 'L1_xattn_Wq': _L1_xattn_in['Wq'], 'L1_xattn_Wk': _L1_xattn_in['Wk'], 'L1_xattn_Wv': _L1_xattn_in['Wv'], 'L1_xattn_Wo': _L1_xattn_in['Wo'], 'L1_xattn_bo': _L1_xattn_in['bo'], 'L1_ffn_q_w': _L1_ffn_in['q_w'], 'L1_ffn_q_b': _L1_ffn_in['q_b'], 'L1_ffn_k_w': _L1_ffn_in['k_w'], 'L1_ffn_k_b': _L1_ffn_in['k_b'], 'L1_ffn_v_w': _L1_ffn_in['v_w'], 'L1_ffn_v_b': _L1_ffn_in['v_b'], 'L1_ffn_o_w': _L1_ffn_in['o_w'], 'L1_ffn_o_b': _L1_ffn_in['o_b'], 'L1_ffn_router_w': _L1_ffn_in['router_w'], 'L1_ffn_router_b': _L1_ffn_in['router_b'], 'L1_ffn_w1': _L1_ffn_in['w1'], 'L1_ffn_b1': _L1_ffn_in['b1'], 'L1_ffn_w2': _L1_ffn_in['w2'], 'L1_ffn_b2': _L1_ffn_in['b2']}

def reference(x, ctx_1024, mask_1x1xSxS2_if1, mask_BxS2_bf1, L0_attn_W_in, L0_attn_dw_kernel, L0_attn_pw_kernel, L0_attn_conv_bias, L0_attn_W_x, L0_attn_W_dt, L0_attn_b_dt, L0_attn_A_log, L0_attn_D, L0_attn_W_out, L0_xattn_wq, L0_xattn_bq, L0_xattn_wk, L0_xattn_bk, L0_xattn_wv, L0_xattn_bv, L0_xattn_wo, L0_xattn_bo, L0_ffn_Wg, L0_ffn_We, L0_ffn_be, L1_attn_w_qkv, L1_attn_w_conv1, L1_xattn_Wq, L1_xattn_Wk, L1_xattn_Wv, L1_xattn_Wo, L1_xattn_bo, L1_ffn_q_w, L1_ffn_q_b, L1_ffn_k_w, L1_ffn_k_b, L1_ffn_v_w, L1_ffn_v_b, L1_ffn_o_w, L1_ffn_o_b, L1_ffn_router_w, L1_ffn_router_b, L1_ffn_w1, L1_ffn_b1, L1_ffn_w2, L1_ffn_b2):
    import jax
    import jax.numpy as jnp

    def _L0_attn_ref(x, W_in, dw_kernel, pw_kernel, conv_bias, W_x, W_dt, b_dt, A_log, D, W_out):
        import jax, jax.numpy as jnp
        import numpy as np
        B, L, D_MODEL = (2, 512, 256)
        D_STATE, D_CONV, EXPAND = (8, 4, 2)
        D_INNER = EXPAND * D_MODEL
        DT_RANK = (D_MODEL + 15) // 16
        d_inner, d_state = A_log.shape
        dt_rank = W_dt.shape[0]
        d_conv = dw_kernel.shape[0]
        bsz = x.shape[0]
        xz = x @ W_in
        x_in, z = jnp.split(xz, 2, axis=-1)
        xp = jnp.pad(x_in, ((0, 0), (d_conv - 1, 0), (0, 0)))
        xc = jax.lax.conv_general_dilated(xp, dw_kernel[:, None, :], window_strides=(1,), padding='VALID', dimension_numbers=('NWC', 'WIO', 'NWC'), feature_group_count=d_inner)
        xc = jax.nn.silu(xc @ pw_kernel + conv_bias)
        x_dbl = xc @ W_x
        delta = x_dbl[..., :dt_rank]
        Bm = x_dbl[..., dt_rank:dt_rank + d_state]
        C = x_dbl[..., dt_rank + d_state:]
        delta = jax.nn.softplus(delta @ W_dt + b_dt)
        A = -jnp.exp(A_log)
        deltaA = jnp.exp(jnp.einsum('bld,dn->bldn', delta, A))
        deltaB_u = jnp.einsum('bld,bln,bld->bldn', delta, Bm, xc)

        def step(h, inp):
            dA_t, dBu_t, C_t = inp
            h = dA_t * h + dBu_t
            y_t = jnp.einsum('bn,bdn->bd', C_t, h)
            return (h, y_t)
        h0 = jnp.zeros((bsz, d_inner, d_state), dtype=x.dtype)
        elems = (deltaA.transpose(1, 0, 2, 3), deltaB_u.transpose(1, 0, 2, 3), C.transpose(1, 0, 2))
        _, ys = jax.lax.scan(step, h0, elems)
        y = ys.transpose(1, 0, 2)
        y = y + xc * D
        y = y * jax.nn.silu(z)
        return y @ W_out

    def _L0_xattn_ref(q, k, v, mask, wq, bq, wk, bk, wv, bv, wo, bo):
        import jax, jax.numpy as jnp
        import numpy as np
        B, S, D, H = (2, 512, 256, 16)
        DK = D // H
        b, s, _ = q.shape
        Q = (q @ wq.T + bq).reshape(b, s, H, DK).transpose(0, 2, 1, 3)
        K = (k @ wk.T + bk).reshape(b, -1, H, DK).transpose(0, 2, 1, 3)
        V = (v @ wv.T + bv).reshape(b, -1, H, DK).transpose(0, 2, 1, 3)
        scores = jnp.einsum('bhqd,bhkd->bhqk', Q, K) / np.sqrt(DK)
        scores = jnp.where(mask == 0, jnp.float32(-1e-09), scores)
        att = jax.nn.softmax(scores, axis=-1)
        x = jnp.einsum('bhqk,bhkd->bhqd', att, V)
        x = x.transpose(0, 2, 1, 3).reshape(b, s, H * DK)
        return x @ wo.T + bo

    def _L0_ffn_ref(x, Wg, We, be):
        import jax, jax.numpy as jnp
        import numpy as np
        B, S, D = (4, 512, 256)
        E = 8
        CF = 1
        b, s, d = x.shape
        n = b * s
        cap = n // E * CF
        h = x.reshape(n, d)
        router_logits = h @ Wg
        probs = jax.nn.softmax(router_logits, axis=1)
        best = jnp.argmax(probs, axis=1)
        mask = jax.nn.one_hot(best, E, dtype=probs.dtype)
        gate = jnp.sum(probs * mask, axis=1)
        locations = jnp.cumsum(mask, axis=0) - 1.0
        mask = mask * (locations < cap).astype(mask.dtype)
        loc_idx = jnp.sum(locations * mask, axis=1).astype(jnp.int32)
        new_gate = gate[:, None] * mask
        loc_oh = jax.nn.one_hot(loc_idx, cap, dtype=new_gate.dtype)
        combine = new_gate[:, :, None] * loc_oh[:, None, :]
        dispatch = (combine != 0).astype(h.dtype)
        dispatched = jnp.einsum('nec,nd->ecd', dispatch, h).reshape(E * cap, d)
        expert_out = dispatched @ We + be
        out = combine.reshape(n, E * cap) @ expert_out
        return out.reshape(b, s, d)

    def _L1_attn_ref(x, w_qkv, w_conv1):
        import jax, jax.numpy as jnp
        import numpy as np
        B, N, C = (8, 1024, 256)
        b, n, c = x.shape
        scale = c ** (-0.5)
        qkv = jnp.einsum('bnc,dc->bnd', x, w_qkv)
        q = qkv[..., :c]
        k = qkv[..., c:2 * c]
        v = qkv[..., 2 * c:]
        agent = jnp.einsum('bnc,c->bn', q, w_conv1)
        agent_attn = jax.nn.softmax(jnp.einsum('bn,bnc->bc', agent * scale, k), axis=-1)
        agent_v = jax.nn.softmax(jnp.einsum('bc,bnc->bn', agent_attn, v), axis=-1)
        agent_v = jnp.einsum('bn,bnc->bc', agent_v, v)
        agent_tok = jax.nn.softmax(agent[:, :, None], axis=-1)
        return agent_tok * agent_v[:, None, :]

    def _L1_xattn_ref(query, key, value, key_padding_mask, Wq, Wk, Wv, Wo, bo):
        import jax, jax.numpy as jnp
        import numpy as np
        NEG_INF = -10000000000.0
        nheads = 16
        B, Sq, D = query.shape
        d_k = D // nheads
        scale = 1.0 / jnp.sqrt(jnp.asarray(d_k, query.dtype))
        q = query @ Wq.T
        k = key @ Wk.T
        v = value @ Wv.T
        q = q.reshape(B, Sq, nheads, d_k)
        k = k.reshape(B, -1, nheads, d_k)
        v = v.reshape(B, -1, nheads, d_k)
        scores = jnp.einsum('bqhd,bkhd->bhqk', q, k) * scale
        mask = key_padding_mask[:, None, None, :]
        scores = jnp.where(mask, scores, jnp.asarray(NEG_INF, scores.dtype))
        attn = jax.nn.softmax(scores, axis=-1)
        out = jnp.einsum('bhqk,bkhd->bqhd', attn, v)
        out = out.reshape(B, Sq, D)
        return out @ Wo.T + bo

    def _L1_ffn_ref(hidden_states, q_w, q_b, k_w, k_b, v_w, v_b, o_w, o_b, router_w, router_b, w1, b1, w2, b2):
        import jax, jax.numpy as jnp
        import numpy as np
        import math
        D = 256
        H = 16
        E = 8
        TOPK = 2
        LAT = D // 2
        KPH = LAT // H
        HD = D // H

        def _forward(hs, q_w, q_b, k_w, k_b, v_w, v_b, o_w, o_b, router_w, router_b, w1, b1, w2, b2):
            B, S, _ = hs.shape
            Q = (hs @ q_w + q_b).reshape(B, S, H, HD).transpose(0, 2, 1, 3)
            K = (hs @ k_w + k_b).reshape(B, S, H, KPH).transpose(0, 2, 1, 3)
            V = (hs @ v_w + v_b).reshape(B, S, H, KPH).transpose(0, 2, 1, 3)
            scores = jnp.einsum('bhsk,bhtk->bhst', Q[..., :KPH], K) / math.sqrt(KPH)
            attn = jax.nn.softmax(scores, axis=-1)
            ao = jnp.einsum('bhst,bhtv->bhsv', attn, V)
            ao = ao.transpose(0, 2, 1, 3).reshape(B, S, H * KPH)
            ao = jnp.concatenate([ao, jnp.zeros((B, S, D - LAT), ao.dtype)], axis=-1)
            mla_out = ao @ o_w + o_b
            probs = jax.nn.softmax(mla_out @ router_w + router_b, axis=-1)
            topw, topi = jax.lax.top_k(probs, TOPK)
            topw = topw / (topw.sum(-1, keepdims=True) + 1e-08)
            combine = jnp.sum(jax.nn.one_hot(topi, E, dtype=probs.dtype) * topw[..., None], axis=-2)
            h1 = jnp.einsum('bsd,edf->ebsf', mla_out, w1) + b1[:, None, None, :]
            h1 = jax.nn.gelu(h1, approximate=False)
            h2 = jnp.einsum('ebsf,efd->ebsd', h1, w2) + b2[:, None, None, :]
            moe_out = jnp.einsum('bse,ebsd->bsd', combine, h2)
            return hs + 0.3 * moe_out
        return _forward(hidden_states, q_w, q_b, k_w, k_b, v_w, v_b, o_w, o_b, router_w, router_b, w1, b1, w2, b2)
    x = x + _L0_attn_ref(_layernorm(x, axis=-1), L0_attn_W_in, L0_attn_dw_kernel, L0_attn_pw_kernel, L0_attn_conv_bias, L0_attn_W_x, L0_attn_W_dt, L0_attn_b_dt, L0_attn_A_log, L0_attn_D, L0_attn_W_out)
    x = x + _L0_xattn_ref(_layernorm(x, axis=-1), ctx_1024, ctx_1024, mask_1x1xSxS2_if1, L0_xattn_wq, L0_xattn_bq, L0_xattn_wk, L0_xattn_bk, L0_xattn_wv, L0_xattn_bv, L0_xattn_wo, L0_xattn_bo)
    x = x + _L0_ffn_ref(_layernorm(x, axis=-1), L0_ffn_Wg, L0_ffn_We, L0_ffn_be)
    x = x + _L1_attn_ref(_layernorm(x, axis=-1), L1_attn_w_qkv, L1_attn_w_conv1)
    x = x + _L1_xattn_ref(_layernorm(x, axis=-1), ctx_1024, ctx_1024, mask_BxS2_bf1, L1_xattn_Wq, L1_xattn_Wk, L1_xattn_Wv, L1_xattn_Wo, L1_xattn_bo)
    x = x + _L1_ffn_ref(_layernorm(x, axis=-1), L1_ffn_q_w, L1_ffn_q_b, L1_ffn_k_w, L1_ffn_k_b, L1_ffn_v_w, L1_ffn_v_b, L1_ffn_o_w, L1_ffn_o_b, L1_ffn_router_w, L1_ffn_router_b, L1_ffn_w1, L1_ffn_b1, L1_ffn_w2, L1_ffn_b2)
    return x

_drawn_inputs = setup_inputs


def setup_inputs(seed=0):
    import zlib

    import numpy as np

    out = dict(_drawn_inputs(seed))
    spreads = {'L0_attn_conv_bias': (0.0, 0.1),
     'L0_attn_b_dt': (0.0, 0.1),
     'L0_attn_D': (1.0, 0.2),
     'L1_xattn_bo': (0.0, 0.1),
     'L1_ffn_q_b': (0.0, 0.1),
     'L1_ffn_k_b': (0.0, 0.1),
     'L1_ffn_v_b': (0.0, 0.1),
     'L1_ffn_o_b': (0.0, 0.1),
     'L1_ffn_router_b': (0.0, 0.1),
     'L1_ffn_b1': (0.0, 0.1),
     'L1_ffn_b2': (0.0, 0.1)}
    factors = {}
    for name, (base, spread) in spreads.items():
        noise = np.random.default_rng([zlib.crc32(name.encode()), seed]).standard_normal(out[name].shape)
        drawn = base * np.exp(spread * noise) if base else spread * noise
        out[name] = jnp.asarray(drawn.astype(out[name].dtype))
    for name, factor in factors.items():
        out[name] = (out[name] * factor).astype(out[name].dtype)
    return out
```

```python
from contextlib import ExitStack

import numpy as np

import concourse.bass as bass
from concourse import mybir

F32 = mybir.dt.float32
ALU = mybir.AluOpType
ACT = mybir.ActivationFunctionType
AX_X = mybir.AxisListType.X

B, S, D = 32, 112, 256
SK = 375
KC, KP = 3, 125
DC = D // 128
H, DK = 16, 16
EPS = 1e-5
BIG = 3.0e38


class Scope:

    def __init__(self, nc, stack, prefix):
        self.nc, self.stack, self.prefix = nc, stack, prefix
        self.sems = []
        stack.callback(self.clear)

    def sb(self, name, shape, dt=F32):
        return self.stack.enter_context(self.nc.sbuf_tensor(self.prefix + name, shape, dt))

    def psum(self, name, shape, dt=F32):
        return self.stack.enter_context(self.nc.psum_tensor(self.prefix + name, shape, dt))

    def sem(self, name):
        self.sems.append(self.nc.alloc_semaphore(name=self.prefix + name))
        return self.sems[-1]

    def clear(self):
        if self.sems:
            self.nc.clear_and_free_semaphores(self.sems)
            self.nc.all_engine_barrier()


def reuse(eng, sem, count):
    if not (isinstance(count, int) and count <= 0):
        eng.wait_ge(sem, count)


def row(tensor, b):
    return tensor[:, bass.ds(b, 1), :].rearrange("p o d -> p (o d)")


def normalise(dve, keep, b, out):
    return dve.tensor_scalar(out, row(keep.x, b), keep.moments[:, bass.ds(b, 1), 0], keep.rstd[:, bass.ds(b, 1)],
                             ALU.subtract, ALU.mult)


def load_and_first_stats(nc, keep, x_in):
    with ExitStack() as stack:
        scope = Scope(nc, stack, "ld_")
        x_loaded = [scope.sem(f"x_loaded{n}") for n in range(4)]
        block = stack.enter_context(nc.Block())
        part = B // 4

        @block.sync
        def _(sp):
            for n in range(4):
                sp.dma_start(keep.x[:, n * part:(n + 1) * part, :],
                             x_in[n * part:(n + 1) * part].rearrange("b s d -> s b d")).then_inc(x_loaded[n], 16)
            for n in range(4):
                sp.wait_ge(x_loaded[n], 16)

        @block.vector
        def _(dve):
            for n in range(4):
                dve.wait_ge(x_loaded[n], 16)
                for b in range(n * part, (n + 1) * part):
                    dve.bn_stats(keep.stats[:, b, :], keep.x[:, b, :])


def layernorm_scales(nc, keep, name):
    with ExitStack() as stack:
        scope = Scope(nc, stack, name)
        deviation = scope.sb("deviation", [S, B])
        aggregated = scope.sem("aggregated")
        rooted = scope.sem("rooted")
        block = stack.enter_context(nc.Block())

        @block.vector
        def _(dve):
            for b in range(B):
                last = dve.bn_aggr(keep.moments[:, b, :], keep.stats[:, b, :])
            last.then_inc(aggregated, 1)
            dve.wait_ge(rooted, 1)
            dve.reciprocal(keep.rstd[:, :], deviation[:, :])

        @block.scalar
        def _(act):
            act.wait_ge(aggregated, 1)
            act.activation(deviation[:, :], keep.moments[:, :, 1], ACT.Sqrt, bias=keep.eps[0:S, :]).then_inc(rooted, 1)
KPH = 8
PHASES = (1, 2, 3, 4, 5, 6,)


def mamba(nc, keep, name, w):
    G = 4
    GROUPS = B // G
    T = G * S
    DI, N, R, TAPS = 512, 8, 16, 4
    IC = DI // 128
    FRONT = 18 // 2
    with ExitStack() as stack:
        scope = Scope(nc, stack, name)
        sb, psum, sem = scope.sb, scope.psum, scope.sem
        w_in, pw, w_out = sb("w_in", [128, DC, 2 * DI]), sb("pw", [128, IC, DI]), sb("w_out", [128, IC, D])
        w_x, w_dt = sb("w_x", [128, IC, R + 2 * N]), sb("w_dt", [R, DI])
        conv, conv_bias, b_dt, skip = sb("conv", [128, IC, TAPS]), sb("conv_bias", [128, IC]), sb("b_dt", [128, IC]), sb("skip", [128, IC])
        a_log, decay_rate = sb("a_log", [128, IC, N]), sb("decay_rate", [128, IC, N])
        own_row = sb("own_row", [R + 2 * N, R + 2 * N, 128])
        normed = sb("normed", [S, G, D])
        normed_t = sb("normed_t", [128, DC, T])
        padded = sb("padded", [128, IC, G, TAPS - 1 + S])
        mixed = sb("mixed", [128, IC, T])
        inner = sb("inner", [128, IC, T])
        gates = sb("gates", [128, IC, T])
        low = sb("low", [R + 2 * N, T])
        soft = sb("soft", [128, IC, T])
        delta = sb("delta", [128, IC, T])
        delta_inner = sb("delta_inner", [128, IC, T])
        decay = sb("decay", [128, 2, IC, T])
        drive = sb("drive", [128, IC, T])
        state = sb("state", [128, IC, T])
        read_out = sb("read_out", [128, 2, IC, T])
        y_bank = [psum(f"y_bank{n}", [128, 512]) for n in range(IC)]
        front_bank = [psum(f"front_bank{n}", [128, 512]) for n in range(2)]
        row_bank = [psum(f"row_bank{n}", [128, 512]) for n in range(2)]

        loaded, setup = sem("loaded"), sem("setup")
        normed_ready = sem("normed_ready")
        front_done = [sem(f"front_done{n}") for n in range(2)]
        front_read = [sem(f"front_read{n}") for n in range(2)]
        row_done = [sem(f"row_done{n}") for n in range(2)]
        row_read = [sem(f"row_read{n}") for n in range(2)]
        mixed_ready = sem("mixed_ready")
        relu_ready, abs_ready, log_ready, delta_ready, delta_inner_ready = (
            sem(n) for n in ("relu_ready", "abs_ready", "log_ready", "delta_ready", "delta_inner_ready"))
        decay_ready, cut_ready, drive_ready, state_ready, summed = (
            sem(n) for n in ("decay_ready", "cut_ready", "drive_ready", "state_ready", "summed"))
        skipped, gated = sem("skipped"), sem("gated")
        block = stack.enter_context(nc.Block())

        ROW_USES = (1 + N + 2, N + 2)
        ROW_OF_B, ROW_OF_OUT = 1, (1 + N, N)

        def flat(a):
            return a.rearrange("p c t -> p (c t)")

        @block.sync
        def _(sp):
            for tile, source, k in ((w_in, "w_in", DC), (pw, "pw", IC), (w_out, "w_out", IC), (w_x, "w_x", IC)):
                sp.dma_start(tile[:, :, :], w[source].rearrange("(c p) n -> p c n", c=k)).then_inc(loaded, 16)
            sp.dma_start(w_dt[:, :], w["w_dt"]).then_inc(loaded, 16)
            for tile, source in ((conv, "conv"), (a_log, "a_log")):
                sp.dma_start(tile[:, :, :], w[source]).then_inc(loaded, 16)
            for tile, source in ((conv_bias, "conv_bias"), (b_dt, "b_dt"), (skip, "skip")):
                sp.dma_start(tile[:, :], w[source]).then_inc(loaded, 16)
            sp.dma_start(own_row[:, :, :].rearrange("p r n -> p (r n)"), w["own_row"]).then_inc(loaded, 16)

        LOADED = 16 * 11

        @block.tensor
        def _(pe):
            def front(g, u):
                reuse(pe, front_read[u % 2], FRONT * g + u // 2)
                return front_bank[u % 2]

            def rows(g, k, n):
                reuse(pe, row_read[k], ROW_USES[k] * g + n)
                return row_bank[k]

            def group(g):
                pe.wait_ge(normed_ready, G * (g + 1))
                for c in range(DC):
                    bank = front(g, c)
                    for b in range(G):
                        last = pe.transpose(bank[:, b * S:(b + 1) * S], normed[:, b, c * 128:(c + 1) * 128], keep.ident[0:S, 0:S])
                    last.then_inc(front_done[c % 2], 1)
                for c in range(DC):
                    pe.wait_ge(front_read[c], FRONT * g + 1)
                for m in range(2 * IC):
                    bank = front(g, 2 + m)
                    for c in range(DC):
                        last = pe.matmul(bank[:, 0:T], w_in[:, c, m * 128:(m + 1) * 128], normed_t[:, c, :],
                                         start=c == 0, stop=c == DC - 1)
                    last.then_inc(front_done[m % 2], 1)
                pe.wait_ge(mixed_ready, TAPS * IC * (g + 1))
                for m in range(IC):
                    bank = front(g, 10 + m)
                    for c in range(IC):
                        last = pe.matmul(bank[:, 0:T], pw[:, c, m * 128:(m + 1) * 128], mixed[:, c, :],
                                         start=c == 0, stop=c == IC - 1)
                    last.then_inc(front_done[m % 2], 1)
                for k in range(2):
                    pe.wait_ge(front_read[k], FRONT * g + 7)
                bank = rows(g, 0, 0)
                for c in range(IC):
                    last = pe.matmul(bank[0:R + 2 * N, 0:T], w_x[:, c, :], inner[:, c, :], start=c == 0, stop=c == IC - 1)
                last.then_inc(row_done[0], 1)
                pe.wait_ge(row_read[0], ROW_USES[0] * g + 1)
                for m in range(IC):
                    bank = front(g, 14 + m)
                    pe.matmul(bank[:, 0:T], w_dt[:, m * 128:(m + 1) * 128], low[0:R, :],
                              start=True, stop=True).then_inc(front_done[m % 2], 1)

                def spread(k, n):
                    bank = rows(g, k, (ROW_OF_B if k == 0 else 0) + n)
                    pe.matmul(bank[:, 0:T], own_row[:, R + k * N + n, :], low[:, :], start=True, stop=True).then_inc(row_done[k], 1)

                def add_state(n):
                    pe.wait_ge(row_read[1], ROW_USES[1] * g + n + 1)
                    if n == 0:
                        reuse(pe, skipped, g)
                    for c in range(IC):
                        last = pe.matmul(y_bank[c][:, 0:T], keep.ident[:, :], read_out[:, n % 2, c, :], start=n == 0, stop=n == N - 1)
                    last.then_inc(summed, 1)

                for n in range(N):
                    spread(0, n)
                    spread(1, n)
                    if n >= 1:
                        add_state(n - 1)
                add_state(N - 1)
                pe.wait_ge(gated, g + 1)
                for b in range(G):
                    bank = rows(g, b % 2, ROW_OF_OUT[b % 2] + b // 2)
                    for c in range(IC):
                        last = pe.matmul(bank[0:S, 0:D], mixed[:, c, b * S:(b + 1) * S], w_out[:, c, :], start=c == 0, stop=c == IC - 1)
                    last.then_inc(row_done[b % 2], 1)

            pe.wait_ge(loaded, LOADED)
            group(0)
            with pe.Fori(1, GROUPS) as g:
                group(g)

        @block.scalar
        def _(act):
            def front(g, u):
                act.wait_ge(front_done[u % 2], FRONT * g + u // 2 + 1)
                return front_bank[u % 2]

            def group(g):
                for c in range(DC):
                    act.activation(normed_t[:, c, :], front(g, c)[:, 0:T], ACT.Copy).then_inc(front_read[c % 2], 1)
                for m in range(IC):
                    act.activation(padded[:, m, :, TAPS - 1:], front(g, 2 + m)[:, 0:T].rearrange("p (b s) -> p b s", b=G),
                                   ACT.Copy).then_inc(front_read[m % 2], 1)
                reuse(act, gated, g)
                for m in range(IC):
                    act.activation(gates[:, m, :], front(g, 6 + m)[:, 0:T], ACT.Silu).then_inc(front_read[m % 2], 1)
                for m in range(IC):
                    act.activation(inner[:, m, :], front(g, 10 + m)[:, 0:T], ACT.Silu,
                                   bias=conv_bias[:, m:m + 1]).then_inc(front_read[m % 2], 1)
                act.wait_ge(row_done[0], ROW_USES[0] * g + 1)
                act.activation(low[:, :], row_bank[0][0:R + 2 * N, 0:T], ACT.Copy).then_inc(row_read[0], 1)
                reuse(act, delta_ready, g)
                for m in range(IC):
                    bank = front(g, 14 + m)
                    act.wait_ge(relu_ready, IC * g + m + 1)
                    act.activation(soft[:, m, :], bank[:, 0:T], ACT.Abs, bias=b_dt[:, m:m + 1]).then_inc(front_read[m % 2], 1)
                for k in range(2):
                    act.wait_ge(front_read[k], FRONT * (g + 1))
                act.activation(flat(soft[:, :, :]), flat(soft[:, :, :]), ACT.Exp, scale=-1.0).then_inc(abs_ready, 1)
                act.wait_ge(abs_ready, g + 1)
                act.activation(flat(soft[:, :, :]), flat(soft[:, :, :]), ACT.Ln, bias=keep.one[:, :]).then_inc(log_ready, 1)
                act.wait_ge(delta_ready, g + 1)
                for n in range(N):
                    reuse(act, state_ready, N * g + n - 1)
                    for c in range(IC):
                        last = act.activation(decay[:, n % 2, c, :], delta[:, c, :], ACT.Exp, scale=decay_rate[:, c, n:n + 1])
                    last.then_inc(decay_ready, 1)

            act.wait_ge(loaded, LOADED)
            act.activation(decay_rate[:, :, :], a_log[:, :, :], ACT.Exp).then_inc(setup, 1)
            act.wait_ge(setup, 2)
            group(0)
            with act.Fori(1, GROUPS) as g:
                group(g)

        @block.vector
        def _(dve):
            def group(g):
                reuse(dve, front_done[0], FRONT * g)
                for b in range(G):
                    normalise(dve, keep, G * g + b, normed[:, b, :]).then_inc(normed_ready, 1)
                for tap in range(TAPS):
                    for c in range(IC):
                        taken = padded[:, c, :, tap:tap + S]
                        out = mixed[:, c, :].rearrange("p (b s) -> p b s", b=G)
                        if tap == 0:
                            dve.wait_ge(front_read[c % 2], FRONT * g + 2 + c // 2)
                            dve.tensor_scalar(out, taken, conv[:, c, 0:1], None, ALU.mult).then_inc(mixed_ready, 1)
                        else:
                            dve.wait_ge(mixed_ready, IC * (TAPS * g + tap - 1) + c + 1)
                            dve.scalar_tensor_tensor(out, taken, conv[:, c, tap:tap + 1], out, ALU.mult, ALU.add).then_inc(mixed_ready, 1)
                for m in range(IC):
                    dve.wait_ge(front_done[m % 2], FRONT * g + 7 + m // 2 + 1)
                    dve.tensor_scalar(delta[:, m, :], front_bank[m % 2][:, 0:T], b_dt[:, m:m + 1], 0.0, ALU.add, ALU.max).then_inc(relu_ready, 1)
                dve.wait_ge(log_ready, g + 1)
                dve.wait_ge(relu_ready, IC * (g + 1))
                dve.tensor_tensor(flat(delta[:, :, :]), flat(delta[:, :, :]), flat(soft[:, :, :]), ALU.add).then_inc(delta_ready, 1)
                dve.wait_ge(delta_ready, g + 1)
                dve.tensor_tensor(flat(delta_inner[:, :, :]), flat(delta[:, :, :]), flat(inner[:, :, :]), ALU.mult).then_inc(delta_inner_ready, 1)
                dve.wait_ge(delta_inner_ready, g + 1)
                for n in range(N):
                    k = N * g + n
                    dve.wait_ge(decay_ready, k + 1)
                    dve.memset(decay[:, n % 2, :, :].rearrange("p c (b s) -> p c b s", b=G)[:, :, :, 0], 0.0).then_inc(cut_ready, 1)
                    dve.wait_ge(row_done[0], ROW_USES[0] * g + ROW_OF_B + n + 1)
                    dve.tensor_tensor(drive[:, :, :], delta_inner[:, :, :],
                                      row_bank[0][:, 0:T].unsqueeze(1).broadcast_to([128, IC, T]), ALU.mult).then_inc(row_read[0], 1)
                    dve.wait_ge(cut_ready, k + 1)
                    dve.wait_ge(row_read[0], ROW_USES[0] * g + ROW_OF_B + n + 1)
                    dve.tensor_tensor_scan(flat(state[:, :, :]), flat(decay[:, n % 2, :, :]), flat(drive[:, :, :]), 0.0,
                                           ALU.mult, ALU.add).then_inc(state_ready, 1)
                    dve.wait_ge(state_ready, k + 1)
                    dve.wait_ge(row_done[1], ROW_USES[1] * g + n + 1)
                    reuse(dve, summed, k - 1)
                    dve.tensor_tensor(read_out[:, n % 2, :, :], state[:, :, :],
                                      row_bank[1][:, 0:T].unsqueeze(1).broadcast_to([128, IC, T]), ALU.mult).then_inc(row_read[1], 1)
                dve.wait_ge(summed, N * (g + 1))
                for c in range(IC):
                    last = dve.scalar_tensor_tensor(delta_inner[:, c, :], inner[:, c, :], skip[:, c:c + 1], y_bank[c][:, 0:T],
                                                    ALU.mult, ALU.add)
                last.then_inc(skipped, 1)
                dve.wait_ge(skipped, g + 1)
                dve.tensor_tensor(flat(mixed[:, :, :]), flat(delta_inner[:, :, :]), flat(gates[:, :, :]), ALU.mult).then_inc(gated, 1)
                for b in range(G):
                    t = G * g + b
                    dve.wait_ge(row_done[b % 2], ROW_USES[b % 2] * g + ROW_OF_OUT[b % 2] + b // 2 + 1)
                    dve.tensor_tensor(row(keep.x, t), row_bank[b % 2][0:S, 0:D], row(keep.x, t), ALU.add).then_inc(row_read[b % 2], 1)
                for b in range(G):
                    t = G * g + b
                    dve.wait_ge(row_read[b % 2], ROW_USES[b % 2] * g + ROW_OF_OUT[b % 2] + b // 2 + 1)
                    dve.bn_stats(row(keep.stats, t), row(keep.x, t))

            dve.wait_ge(setup, 1)
            dve.tensor_scalar(decay_rate[:, :, :], decay_rate[:, :, :], -1.0, None, ALU.mult).then_inc(setup, 1)
            dve.memset(padded[:, :, :, 0:TAPS - 1], 0.0)
            group(0)
            with dve.Fori(1, GROUPS) as g:
                group(g)


def cross_attention(nc, keep, name, ctx_t, w_q, w_k, w_v, w_o, b_q, b_k, b_v, b_o, query_scale, mask, masked_t, key_mask):
    replaced = mask is not None
    USES = 7 if replaced else 6
    VW = DK + 1
    with ExitStack() as stack:
        scope = Scope(nc, stack, name)
        sb, psum, sem = scope.sb, scope.psum, scope.sem
        wq, wk, wv, wo = (sb(n, [128, DC, D]) for n in ("wq", "wk", "wv", "wo"))
        bq, bk = sb("bq", [128, DC]), sb("bk", [128, DC])
        bv, bo = sb("bv", [KP, D]), sb("bo", [1, D])
        ones = sb("ones", [1, S])
        q_scale = sb("q_scale", [128, 2])
        q_bias = sb("q_bias", [128, DC, 2])
        context = [sb(f"context{n}", [128, DC, SK]) for n in range(2)]
        normed = sb("normed", [S, D])
        normed_t = sb("normed_t", [128, DC, S])
        queries = [sb(f"queries{n}", [128, 2, DC, S]) for n in range(2)]
        keys = [sb(f"keys{n}", [128, DC, SK]) for n in range(2)]
        values = [sb(f"values{n}", [KP, KC, H, VW]) for n in range(2)]
        scores = sb("scores", [S, 4, SK])
        row_max = sb("row_max", [S, 4])
        negmax = [sb(f"negmax{n}", [S, H]) for n in range(2)]
        floor = sb("floor", [S, 1])
        probs = sb("probs", [S, 2, SK])
        probs_t = sb("probs_t", [KP, 2, KC, S])
        heads_sum = sb("heads_sum", [S, H, VW])
        inverse = sb("inverse", [S, H])
        heads_out = sb("heads_out", [S, H, DK])
        heads_t = sb("heads_t", [128, DC, S])
        if replaced:
            mask_raw = sb("mask_raw", [S, SK], mybir.dt.int32)
            masked_raw = sb("masked_raw", [KP, KC, S], mybir.dt.int32)
            masked = sb("masked", [S, SK])
            masked_on_keys = sb("masked_on_keys", [KP, KC, S])
            added = [sb("added", [S, SK])] * 2
            any_masked = sb("any_masked", [S, 1])
            masked_values = [sb(f"masked_values{n}", [S, H, VW]) for n in range(2)]
            masked_exp = sb("masked_exp", [S, H])
            masked_part = sb("masked_part", [S, H, VW])
        else:
            mask_raw = sb("mask_raw", [S, B, SK], mybir.dt.uint8)
            key_row = sb("key_row", [S, 2, SK])
            added = [sb(f"added{n}", [S, SK]) for n in range(2)]
        score_bank = [psum(f"score_bank{n}", [128, 512]) for n in range(2)]
        turn_bank = [psum(f"turn_bank{n}", [128, 512]) for n in range(2)]
        proj_bank = [psum(f"proj_bank{n}", [128, 512]) for n in range(2)]
        heads_bank = psum("heads_bank", [128, 512])
        out_bank = psum("out_bank", [128, 512])
        heads_psum = heads_bank[0:S, 0:H * VW].rearrange("p (h v) -> p h v", h=H)
        heads_t_psum = out_bank[:, 0:DC * S].rearrange("p (c s) -> p c s", c=DC)
        out_psum = out_bank[0:S, 256:256 + D]

        weights_in = sem("weights_in")
        context_in = [sem(f"context_in{n}") for n in range(2)]
        constants = sem("constants")
        masks = sem("masks")
        key_row_ready = sem("key_row_ready")
        key_mask_started = sem("key_mask_started")
        key_mask_added = sem("key_mask_added")
        normed_ready = sem("normed_ready")
        proj_done = [sem(f"proj_done{n}") for n in range(2)]
        proj_read = [sem(f"proj_read{n}") for n in range(2)]
        scores_done = sem("scores_done")
        max_started = sem("max_started")
        max_ready = sem("max_ready")
        negmax_ready = sem("negmax_ready")
        probs_ready = sem("probs_ready")
        turned = sem("turned")
        turned_read = [sem(f"turned_read{n}") for n in range(2)]
        head_summed = sem("head_summed")
        masked_exp_ready = sem("masked_exp_ready")
        masked_part_ready = sem("masked_part_ready")
        heads_read = sem("heads_read")
        inverse_ready = sem("inverse_ready")
        heads_out_ready = sem("heads_out_ready")
        heads_turned = sem("heads_turned")
        heads_t_ready = sem("heads_t_ready")
        out_done = sem("out_done")
        x_ready = sem("x_ready")

        N_WEIGHTS = 16 * (4 + 3 * (b_q is not None) + (b_o is not None) + 1 + (2 if replaced else 1))

        def use(i, s, u):
            n = USES * s + u
            return n % 2, USES * i + n // 2

        block = stack.enter_context(nc.Block())

        @block.sync
        def _(sp):
            for tile, w in ((wq, w_q), (wk, w_k), (wv, w_v), (wo, w_o)):
                sp.dma_start(tile[:, :, :], w.rearrange("(c p) n -> p c n", p=128)).then_inc(weights_in, 16)
            if b_q is not None:
                sp.dma_start(bq[:, :], b_q).then_inc(weights_in, 16)
                sp.dma_start(bk[:, :], b_k).then_inc(weights_in, 16)
                sp.dma_start(bv[:, :], b_v.rearrange("(o n) -> o n", o=1).broadcast_to([KP, D])).then_inc(weights_in, 16)
            if b_o is not None:
                sp.dma_start(bo[:, :], b_o.rearrange("(o n) -> o n", o=1)).then_inc(weights_in, 16)
            sp.dma_start(q_scale[:, :], query_scale).then_inc(weights_in, 16)
            if replaced:
                sp.dma_start(mask_raw[:, :], mask).then_inc(weights_in, 16)
                sp.dma_start(masked_raw[:, :, :], masked_t.rearrange("(c p) s -> p c s", c=KC)).then_inc(weights_in, 16)
            else:
                sp.dma_start(mask_raw[:, :, :].rearrange("p b k -> p (b k)"),
                             key_mask.rearrange("(o b) k -> o (b k)", o=1).broadcast_to([S, B * SK])).then_inc(weights_in, 16)

            def context_load(t, s):
                sp.dma_start(context[s][:, :, :], ctx_t[t].rearrange("(c p) k -> p c k", p=128)).then_inc(context_in[s], 16)

            context_load(0, 0)
            context_load(1, 1)
            with sp.Fori(1, B // 2) as i:
                for s in range(2):
                    k, before = use(i - 1, s, 5)
                    sp.wait_ge(proj_done[k], before + 1)
                    sp.dma_start(context[s][:, :, :],
                                 ctx_t[bass.ds(2 * i + s, 1)].rearrange("o (c p) k -> p (o c) k", p=128)
                                 ).then_inc(context_in[s], 16)

        @block.gpsimd
        def _(pool):
            pool.wait_ge(weights_in, N_WEIGHTS)
            if replaced:
                pool.tensor_scalar(masked[:, :], mask_raw[:, :], 0.0, None, ALU.is_equal).then_inc(masks, 1)
                pool.tensor_scalar(masked_on_keys[:, :, :], masked_raw[:, :, :], 0.0, None, ALU.is_equal).then_inc(masks, 1)
                pool.wait_ge(masks, 1)
                pool.tensor_scalar(added[0][:, :], masked[:, :], -BIG, None, ALU.mult).then_inc(masks, 1)
            else:
                def add_key_mask(i, s):
                    pool.tensor_copy(key_row[:, s, :], mask_raw[:, bass.ds(2 * i + s, 1), :].rearrange("p o k -> p (o k)")
                                     ).then_inc(key_row_ready, 1)
                    pool.wait_ge(key_row_ready, 2 * i + s + 1)
                    pool.sem_inc(key_mask_started, 1)
                    pool.tensor_scalar(added[s][:, :], key_row[:, s, :], -1.0, 1e10, ALU.add, ALU.mult).then_inc(key_mask_added, 1)

                add_key_mask(0, 0)
                add_key_mask(0, 1)
                with pool.Fori(1, B // 2) as i:
                    for s in range(2):
                        pool.wait_ge(key_mask_added, 2 * i + s - 1)
                        pool.wait_ge(max_ready, H * (2 * i + s - 1))
                        add_key_mask(i, s)

        @block.tensor
        def _(pe):
            def project(i, s, u):
                k, before = use(i, s, u)
                bank = proj_bank[k]
                pe.wait_ge(proj_read[k], before)
                if u == 0:
                    pe.wait_ge(normed_ready, 2 * i + s + 1)
                    for c in range(DC):
                        last = pe.transpose(bank[:, c * S:(c + 1) * S], normed[:, c * 128:(c + 1) * 128],
                                            keep.ident[0:S, 0:S])
                elif u in (1, 2):
                    if u == 1:
                        pe.wait_ge(context_in[s], 16 * (i + 1))
                    m = u - 1
                    for c in range(DC):
                        last = pe.matmul(bank[:, 0:SK], wk[:, c, m * 128:(m + 1) * 128], context[s][:, c, :],
                                         start=c == 0, stop=c == DC - 1)
                elif u == 3:
                    k0, b0 = use(i, s, 0)
                    pe.wait_ge(proj_read[k0], b0 + 1)
                    for m in range(DC):
                        for c in range(DC):
                            last = pe.matmul(bank[:, m * S:(m + 1) * S], wq[:, c, m * 128:(m + 1) * 128],
                                             normed_t[:, c, :], start=c == 0, stop=c == DC - 1)
                elif u in (4, 5):
                    for j, kc in enumerate((0, 1) if u == 4 else (2,)):
                        for c in range(DC):
                            last = pe.matmul(bank[0:KP, j * D:(j + 1) * D], context[s][:, c, kc * KP:(kc + 1) * KP],
                                             wv[:, c, :], start=c == 0, stop=c == DC - 1)
                    last.then_inc(proj_done[k], 1)
                    return
                else:
                    for uv in (4, 5):
                        kv, bv_ = use(i, s, uv)
                        pe.wait_ge(proj_read[kv], bv_ + 1)
                    for kc in range(KC):
                        last = pe.matmul(bank[0:S, 0:H * VW], masked_on_keys[:, kc, :],
                                         values[s][:, kc, :, :].rearrange("p h v -> p (h v)"),
                                         start=kc == 0, stop=kc == KC - 1)
                last.then_inc(proj_done[k], 1)

            def score(i, s, h):
                m, rows, parity = h // 8, 32 * (h % 8 // 2), h % 2
                if h == 0:
                    for u in (1, 2, 3):
                        k, before = use(i, s, u)
                        pe.wait_ge(proj_read[k], before + 1)
                n = H * (2 * i + s) + h
                if not (isinstance(i, int) and i == 0 and s == 0 and h < 2):
                    pe.wait_ge(max_ready, n - 1)
                pe.matmul(score_bank[h % 2][0:S, 0:SK], queries[s][rows:rows + 32, parity, m, :],
                          keys[s][rows:rows + 32, m, :], start=True, stop=True).then_inc(scores_done, 1)

            def turn(i, s, h):
                n = H * (2 * i + s) + h
                pe.wait_ge(probs_ready, n + 1)
                pe.wait_ge(turned_read[h % 2], 8 * (2 * i + s) + h // 2)
                for kc in range(KC):
                    last = pe.transpose(turn_bank[h % 2][0:KP, kc * S:(kc + 1) * S],
                                        probs[:, h % 2, kc * KP:(kc + 1) * KP], keep.ident[0:S, 0:S])
                last.then_inc(turned, 1)

            def weigh(i, s, h):
                if h == 0:
                    pe.wait_ge(heads_read, 2 * i + s)
                    for u in (4, 5):
                        k, before = use(i, s, u)
                        pe.wait_ge(proj_read[k], before + 1)
                pe.wait_ge(turned_read[h % 2], 8 * (2 * i + s) + h // 2 + 1)
                for kc in range(KC):
                    last = pe.matmul(heads_psum[:, h, :], probs_t[:, h % 2, kc, :], values[s][:, kc, h, :],
                                     start=kc == 0, stop=kc == KC - 1)
                last.then_inc(head_summed, 1)

            def turn_heads(t):
                pe.wait_ge(heads_out_ready, t)
                pe.wait_ge(x_ready, t - 1)
                for c in range(DC):
                    last = pe.transpose(heads_t_psum[:, c, :],
                                        heads_out[:, 8 * c:8 * c + 8, :].rearrange("p h v -> p (h v)"),
                                        keep.ident[0:S, 0:S])
                last.then_inc(heads_turned, 1)

            def project_out(t):
                pe.wait_ge(heads_t_ready, t)
                if b_o is not None:
                    pe.matmul(out_psum, ones[:, :], bo[:, :], start=True, stop=False)
                for c in range(DC):
                    last = pe.matmul(out_psum, heads_t[:, c, :], wo[:, c, :],
                                     start=c == 0 and b_o is None, stop=c == DC - 1)
                last.then_inc(out_done, 1)

            def batch(i, s, first=False, final=False):
                t = 2 * i + s
                following = (i, 1) if s == 0 else (i + 1, 0)
                for h in range(H):
                    if h + 2 < H:
                        score(i, s, h + 2)
                    elif not final:
                        score(*following, h + 2 - H)
                    turn(i, s, h)
                    if h == 4 and not first:
                        turn_heads(t)
                    if h == 6 and not first:
                        project_out(t)
                    if h % 2 == 1 and h // 2 < USES and not final:
                        project(*following, h // 2)
                    if h >= 2:
                        weigh(i, s, h - 2)
                weigh(i, s, H - 2)
                weigh(i, s, H - 1)

            pe.wait_ge(weights_in, N_WEIGHTS)
            pe.wait_ge(constants, 3)
            if replaced:
                pe.wait_ge(masks, 3)
            for u in range(USES):
                project(0, 0, u)
            score(0, 0, 0)
            score(0, 0, 1)
            batch(0, 0, first=True)
            batch(0, 1)
            with pe.Fori(1, B // 2 - 1) as i:
                batch(i, 0)
                batch(i, 1)
            batch(B // 2 - 1, 0)
            batch(B // 2 - 1, 1, final=True)
            turn_heads(B)
            project_out(B)

        def copy_out_turned(eng, copy, i, s, h):
            n = H * (2 * i + s) + h
            eng.wait_ge(turned, n + 1)
            if not (isinstance(i, int) and i == 0 and s == 0 and h < 2):
                eng.wait_ge(head_summed, n - 1)
            copy(probs_t[:, h % 2, :, :].rearrange("p c s -> p (c s)"),
                 turn_bank[h % 2][0:KP, 0:KC * S]).then_inc(turned_read[h % 2], 1)

        @block.vector
        def _(dve):
            def normalise(i, s):
                t = 2 * i + s
                if not (isinstance(t, int) and t == 0):
                    k, before = use(i, 0, 0) if s else use(i - 1, 1, 0)
                    dve.wait_ge(proj_done[k], before + 1)
                dve.tensor_scalar(normed[:, :], keep.x[:, bass.ds(t, 1), :].rearrange("p o d -> p (o d)"),
                                  keep.moments[:, bass.ds(t, 1), 0], keep.rstd[:, bass.ds(t, 1)],
                                  ALU.subtract, ALU.mult).then_inc(normed_ready, 1)

            def read_projection(i, s, u):
                k, before = use(i, s, u)
                bank = proj_bank[k]
                if u == 3:
                    dve.wait_ge(proj_done[k], before + 1)
                    dve.wait_ge(scores_done, H * (2 * i + s - 1)) if not (isinstance(i, int) and 2 * i + s < 2) else None
                    for parity in range(2):
                        for m in range(DC):
                            if b_q is not None:
                                last = dve.tensor_scalar(queries[s][:, parity, m, :], bank[:, m * S:(m + 1) * S],
                                                         q_scale[:, parity:parity + 1], q_bias[:, m, parity:parity + 1],
                                                         ALU.mult, ALU.add)
                            else:
                                last = dve.tensor_scalar(queries[s][:, parity, m, :], bank[:, m * S:(m + 1) * S],
                                                         q_scale[:, parity:parity + 1], None, ALU.mult)
                    last.then_inc(proj_read[k], 1)
                if u in (4, 5):
                    dve.wait_ge(proj_done[k], before + 1)
                    dve.wait_ge(head_summed, H * (2 * i + s - 1)) if not (isinstance(i, int) and 2 * i + s < 2) else None
                    for j, kc in enumerate((0, 1) if u == 4 else (2,)):
                        out = values[s][:, kc, :, 0:DK]
                        got = bank[0:KP, j * D:(j + 1) * D].rearrange("p (h v) -> p h v", h=H)
                        if b_v is not None:
                            last = dve.tensor_tensor(out, got, bv[:, :].rearrange("p (h v) -> p h v", h=H), ALU.add)
                        else:
                            last = dve.tensor_copy(out, got)
                    last.then_inc(proj_read[k], 1)

            def add_mask_and_max(i, s, h):
                n = H * (2 * i + s) + h
                first = isinstance(i, int) and i == 0 and s == 0
                if h == 0 and not replaced:
                    dve.wait_ge(key_mask_added, 2 * i + s + 1)
                dve.wait_ge(scores_done, n + 1)
                if not (first and h < 4):
                    dve.wait_ge(probs_ready, n - 3)
                dve.sem_inc(max_started, 1)
                dve.tensor_tensor_reduce(scores[:, h % 4, :], score_bank[h % 2][0:S, 0:SK], added[s][:, :], 1.0, -BIG,
                                         ALU.add, ALU.max, row_max[:, h % 4:h % 4 + 1]).then_inc(max_ready, 1)
                dve.wait_ge(max_ready, n + 1)
                dve.tensor_scalar(negmax[s][:, h:h + 1], row_max[:, h % 4:h % 4 + 1], floor[:, :], -1.0,
                                  ALU.max, ALU.mult).then_inc(negmax_ready, 1)

            def sum_heads(t, s):
                dve.wait_ge(head_summed, H * t)
                if replaced:
                    dve.wait_ge(masked_exp_ready, t)
                    dve.tensor_tensor(masked_part[:, :, :], masked_values[s][:, :, :],
                                      masked_exp[:, :].unsqueeze(2).broadcast_to([S, H, VW]), ALU.mult).then_inc(masked_part_ready, 1)
                    dve.wait_ge(masked_part_ready, t)
                    dve.tensor_tensor(heads_sum[:, :, :], heads_psum, masked_part[:, :, :], ALU.add).then_inc(heads_read, 1)
                else:
                    dve.tensor_copy(heads_sum[:, :, :], heads_psum).then_inc(heads_read, 1)
                dve.wait_ge(heads_read, t)
                dve.reciprocal(inverse[:, :], heads_sum[:, :, DK]).then_inc(inverse_ready, 1)

            def normalise_heads(t):
                dve.wait_ge(inverse_ready, t)
                dve.wait_ge(heads_turned, t - 1)
                dve.tensor_tensor(heads_out[:, :, :], heads_sum[:, :, 0:DK],
                                  inverse[:, :].unsqueeze(2).broadcast_to([S, H, DK]), ALU.mult).then_inc(heads_out_ready, 1)

            def update_x(t):
                dve.wait_ge(out_done, t)
                row = keep.x[:, bass.ds(t - 1, 1), :].rearrange("p o d -> p (o d)")
                dve.tensor_tensor(row, out_psum, row, ALU.add).then_inc(x_ready, 1)
                dve.wait_ge(x_ready, t)
                dve.bn_stats(keep.stats[:, bass.ds(t - 1, 1), :].rearrange("p o d -> p (o d)"), row)

            def batch(i, s, first=False, final=False):
                t = 2 * i + s
                following = (i, 1) if s == 0 else (i + 1, 0)
                for h in range(H):
                    if h + 2 < H:
                        add_mask_and_max(i, s, h + 2)
                    elif not final:
                        add_mask_and_max(*following, h + 2 - H)
                    if h % 2 == 1:
                        copy_out_turned(dve, dve.tensor_copy, i, s, h)
                    if h == 0 and not first:
                        sum_heads(t, 1 - s)
                    if h == 0 and not final:
                        normalise(*following)
                    if h == 2 and not first:
                        normalise_heads(t)
                    if h == 6 and not first:
                        update_x(t)
                    if h % 2 == 1 and h // 2 < USES and not final:
                        read_projection(*following, h // 2)

            dve.memset(ones[:, :], 1.0).then_inc(constants, 1)
            for s in range(2):
                dve.memset(values[s][:, :, :, DK:VW], 1.0).then_inc(constants, 1)
            dve.wait_ge(weights_in, N_WEIGHTS)
            if replaced:
                dve.wait_ge(masks, 3)
                dve.reduce_max(any_masked[:, :], masked[:, :], AX_X).then_inc(constants, 1)
                dve.wait_ge(constants, 4)
                dve.tensor_scalar(any_masked[:, :], any_masked[:, :], -1.0, BIG, ALU.add, ALU.mult).then_inc(constants, 1)
                dve.wait_ge(constants, 5)
                dve.tensor_scalar(floor[:, :], any_masked[:, :], -1e-9, None, ALU.add).then_inc(constants, 1)
            else:
                dve.memset(floor[:, :], -BIG).then_inc(constants, 1)
            ready = 6 if replaced else 4
            if b_q is not None:
                for m in range(DC):
                    last = dve.tensor_scalar(q_bias[:, m, :], q_scale[:, :], bq[:, m:m + 1], None, ALU.mult)
                last.then_inc(constants, 1)
                ready += 1
            dve.wait_ge(constants, ready)
            normalise(0, 0)
            for u in range(USES):
                read_projection(0, 0, u)
            add_mask_and_max(0, 0, 0)
            add_mask_and_max(0, 0, 1)
            batch(0, 0, first=True)
            batch(0, 1)
            with dve.Fori(1, B // 2 - 1) as i:
                batch(i, 0)
                batch(i, 1)
            batch(B // 2 - 1, 0)
            batch(B // 2 - 1, 1, final=True)
            sum_heads(B, 1)
            normalise_heads(B)
            update_x(B)

        @block.scalar
        def _(act):
            def copy(out, in_):
                return act.activation(out, in_, ACT.Copy)

            def read_projection(i, s, u):
                k, before = use(i, s, u)
                bank = proj_bank[k]
                if u == 0:
                    act.wait_ge(proj_done[k], before + 1)
                    if not (isinstance(i, int) and 2 * i + s == 0):
                        kq, bq_ = use(i, s - 1, 3) if s else use(i - 1, 1, 3)
                        act.wait_ge(proj_done[kq], bq_ + 1)
                    copy(normed_t[:, :, :].rearrange("p c s -> p (c s)"), bank[:, 0:DC * S]).then_inc(proj_read[k], 1)
                if u in (1, 2):
                    act.wait_ge(proj_done[k], before + 1)
                    if not (isinstance(i, int) and 2 * i + s < 2):
                        act.wait_ge(scores_done, H * (2 * i + s - 1))
                    if b_k is not None:
                        act.activation(keys[s][:, u - 1, :], bank[:, 0:SK], ACT.Identity,
                                       bias=bk[:, u - 1:u]).then_inc(proj_read[k], 1)
                    else:
                        copy(keys[s][:, u - 1, :], bank[:, 0:SK]).then_inc(proj_read[k], 1)
                if u == 6:
                    act.wait_ge(proj_done[k], before + 1)
                    if not (isinstance(i, int) and 2 * i + s < 2):
                        act.wait_ge(masked_part_ready, 2 * i + s - 1)
                    copy(masked_values[s][:, :, :].rearrange("p h v -> p (h v)"), bank[0:S, 0:H * VW]).then_inc(proj_read[k], 1)

            def exponentials(i, s, h):
                n = H * (2 * i + s) + h
                act.wait_ge(negmax_ready, n + 1)
                if not (isinstance(i, int) and i == 0 and s == 0 and h < 2):
                    act.wait_ge(turned, n - 1)
                act.activation(probs[:, h % 2, :], scores[:, h % 4, :], ACT.Exp,
                               bias=negmax[s][:, h:h + 1]).then_inc(probs_ready, 1)

            def masked_exponentials(t, s):
                if replaced:
                    act.wait_ge(negmax_ready, H * t)
                    act.wait_ge(masked_part_ready, t - 1)
                    act.activation(masked_exp[:, :], negmax[s][:, :], ACT.Exp, bias=keep.masked_score[0:S, :]).then_inc(masked_exp_ready, 1)

            def read_heads(t):
                act.wait_ge(heads_turned, t)
                act.wait_ge(out_done, t - 1)
                copy(heads_t[:, :, :], heads_t_psum).then_inc(heads_t_ready, 1)

            def batch(i, s, first=False, final=False):
                t = 2 * i + s
                following = (i, 1) if s == 0 else (i + 1, 0)
                for h in range(H):
                    if h == 0 and not first:
                        masked_exponentials(t, 1 - s)
                    if h + 2 < H:
                        exponentials(i, s, h + 2)
                    elif not final:
                        exponentials(*following, h + 2 - H)
                    if h % 2 == 0:
                        copy_out_turned(act, copy, i, s, h)
                    if h == 4 and not first:
                        read_heads(t)
                    if h % 2 == 1 and h // 2 < USES and not final:
                        read_projection(*following, h // 2)

            act.wait_ge(weights_in, N_WEIGHTS)
            for u in range(USES):
                read_projection(0, 0, u)
            exponentials(0, 0, 0)
            exponentials(0, 0, 1)
            batch(0, 0, first=True)
            batch(0, 1)
            with act.Fori(1, B // 2 - 1) as i:
                batch(i, 0)
                batch(i, 1)
            batch(B // 2 - 1, 0)
            batch(B // 2 - 1, 1, final=True)
            masked_exponentials(B, 1)
            read_heads(B)


def switch_ffn(nc, keep, name, w):
    E = 8
    CAP = B * S // E
    G = 4
    with ExitStack() as stack:
        scope = Scope(nc, stack, name)
        sb, psum, sem = scope.sb, scope.psum, scope.sem
        gate_w, expert_w, expert_b = sb("gate_w", [128, DC, E]), sb("expert_w", [128, DC, D]), sb("expert_b", [1, D])
        upto, ones, preference = sb("upto", [S, S]), sb("ones", [S, S]), sb("preference", [S, E])
        normed = sb("normed", [S, G, D])
        normed_t = sb("normed_t", [128, G, DC, S])
        expert_out = sb("expert_out", [S, B, D])
        logits = sb("logits", [S, B, E])
        shifted, exps, chosen = sb("shifted", [S, B, E]), sb("exps", [S, B, E]), sb("chosen", [S, B, E])
        kept, before_here = sb("kept", [S, B, E]), sb("before_here", [S, B + 1, E])
        top, total, gate, weight = sb("top", [S, B]), sb("total", [S, B]), sb("gate", [S, B]), sb("weight", [S, B])
        turn_bank = [psum(f"turn_bank{n}", [128, 512]) for n in range(G)]
        rows_bank = [psum(f"rows_bank{n}", [128, 512]) for n in range(G)]

        loaded, ones_ready = sem("loaded"), sem("ones_ready")
        normed_ready, turned, turned_read = sem("normed_ready"), sem("turned"), sem("turned_read")
        rows_done, logits_read, expert_read = sem("rows_done"), sem("logits_read"), sem("expert_read")
        gating = sem("gating")
        exps_ready, places_done = sem("exps_ready"), sem("places_done")
        updated = sem("updated")
        block = stack.enter_context(nc.Block())

        @block.sync
        def _(sp):
            sp.dma_start(gate_w[:, :, :], w["gate"].rearrange("(c p) e -> p c e", p=128)).then_inc(loaded, 16)
            sp.dma_start(expert_w[:, :, :], w["expert"].rearrange("(c p) n -> p c n", p=128)).then_inc(loaded, 16)
            sp.dma_start(expert_b[:, :], w["expert_bias"].rearrange("(o n) -> o n", o=1)).then_inc(loaded, 16)
            sp.dma_start(upto[:, :], w["upto"]).then_inc(loaded, 16)

        @block.tensor
        def _(pe):
            def step(i):
                for s in range(G):
                    t = G * i + s
                    pe.wait_ge(normed_ready, t + 1)
                    reuse(pe, turned_read, t + 1 - G)
                    for c in range(DC):
                        last = pe.transpose(turn_bank[s][:, c * S:(c + 1) * S], normed[:, s, c * 128:(c + 1) * 128],
                                            keep.ident[0:S, 0:S])
                    last.then_inc(turned, 1)
                for s in range(G):
                    t = G * i + s
                    pe.wait_ge(turned_read, t + 1)
                    reuse(pe, logits_read, t + 1 - G)
                    reuse(pe, expert_read, t + 1 - G)
                    for c in range(DC):
                        pe.matmul(rows_bank[s][0:S, 0:E], normed_t[:, s, c, :], gate_w[:, c, :], start=c == 0, stop=c == DC - 1)
                    out = rows_bank[s][0:S, D:2 * D]
                    pe.matmul(out, ones[0:1, :], expert_b[:, :], start=True, stop=False)
                    for c in range(DC):
                        last = pe.matmul(out, normed_t[:, s, c, :], expert_w[:, c, :], start=False, stop=c == DC - 1)
                    last.then_inc(rows_done, 1)

            pe.wait_ge(loaded, 64)
            pe.wait_ge(ones_ready, 1)
            step(0)
            with pe.Fori(1, B // G) as i:
                step(i)
            pe.wait_ge(gating, 13)
            places = rows_bank[0][0:S, 0:B * E]
            pe.wait_ge(logits_read, B)
            pe.wait_ge(expert_read, B)
            pe.matmul(places, upto[:, :], chosen[:, :, :].rearrange("p b e -> p (b e)"), start=True, stop=False)
            pe.matmul(places, ones[:, :], before_here[:, 0:B, :].rearrange("p b e -> p (b e)"),
                      start=False, stop=True).then_inc(places_done, 1)

        @block.scalar
        def _(act):
            def step(i):
                for s in range(G):
                    t = G * i + s
                    act.wait_ge(turned, t + 1)
                    reuse(act, rows_done, t + 1 - G)
                    act.activation(normed_t[:, s, :, :].rearrange("p c s -> p (c s)"), turn_bank[s][:, 0:DC * S],
                                   ACT.Copy).then_inc(turned_read, 1)
                for s in range(G):
                    t = G * i + s
                    act.wait_ge(rows_done, t + 1)
                    act.wait_ge(logits_read, t + 1)
                    act.activation(row(expert_out, t), rows_bank[s][0:S, D:2 * D], ACT.Copy).then_inc(expert_read, 1)

            step(0)
            with act.Fori(1, B // G) as i:
                step(i)
            act.wait_ge(gating, 2)
            act.activation(exps[:, :, :], shifted[:, :, :], ACT.Exp).then_inc(exps_ready, 1)

        @block.vector
        def _(dve):
            def step(i):
                for s in range(G):
                    t = G * i + s
                    reuse(dve, turned, t + 1 - G)
                    normalise(dve, keep, t, normed[:, s, :]).then_inc(normed_ready, 1)
                for s in range(G):
                    t = G * i + s
                    dve.wait_ge(rows_done, t + 1)
                    dve.tensor_copy(row(logits, t), rows_bank[s][0:S, 0:E]).then_inc(logits_read, 1)

            def wide(column):
                return column[:, :].unsqueeze(2).broadcast_to([S, B, E])

            dve.memset(ones[:, :], 1.0).then_inc(ones_ready, 1)
            dve.memset(before_here[:, 0, :], 0.0)
            for e in range(E):
                last = dve.memset(preference[:, e:e + 1], float(E - e))
            last.then_inc(ones_ready, 1)
            step(0)
            with dve.Fori(1, B // G) as i:
                step(i)
            dve.wait_ge(logits_read, B)
            dve.wait_ge(ones_ready, 2)
            dve.reduce_max(top[:, :], logits[:, :, :], AX_X).then_inc(gating, 1)
            dve.wait_ge(gating, 1)
            dve.tensor_tensor(shifted[:, :, :], logits[:, :, :], wide(top), ALU.subtract).then_inc(gating, 1)
            dve.wait_ge(gating, 2)
            dve.scalar_tensor_tensor(kept[:, :, :], shifted[:, :, :], 0.0, preference[:, :].unsqueeze(1).broadcast_to([S, B, E]),
                                     ALU.is_ge, ALU.mult).then_inc(gating, 1)
            dve.wait_ge(gating, 3)
            dve.reduce_max(top[:, :], kept[:, :, :], AX_X).then_inc(gating, 1)
            dve.wait_ge(gating, 4)
            dve.tensor_tensor(chosen[:, :, :], kept[:, :, :], wide(top), ALU.is_equal).then_inc(gating, 1)
            dve.wait_ge(gating, 5)
            for e in range(E):
                dve.tensor_tensor_scan(before_here[:, 1:B + 1, e], ones[:, 0:B], chosen[:, :, e], 0.0,
                                       ALU.mult, ALU.add).then_inc(gating, 1)
            dve.wait_ge(exps_ready, 1)
            dve.reduce_sum(total[:, :], exps[:, :, :], AX_X).then_inc(gating, 1)
            dve.wait_ge(gating, 14)
            dve.reciprocal(gate[:, :], total[:, :]).then_inc(gating, 1)
            dve.wait_ge(places_done, 1)
            dve.scalar_tensor_tensor(kept[:, :, :], rows_bank[0][0:S, 0:B * E].rearrange("p (b e) -> p b e", b=B), float(CAP),
                                     chosen[:, :, :], ALU.is_le, ALU.mult).then_inc(gating, 1)
            dve.wait_ge(gating, 16)
            dve.reduce_sum(total[:, :], kept[:, :, :], AX_X).then_inc(gating, 1)
            dve.wait_ge(gating, 17)
            dve.tensor_tensor(weight[:, :], gate[:, :], total[:, :], ALU.mult).then_inc(gating, 1)
            dve.wait_ge(gating, 18)
            dve.wait_ge(expert_read, B)

            def update(b):
                dve.scalar_tensor_tensor(row(keep.x, b), row(expert_out, b), weight[:, bass.ds(b, 1)], row(keep.x, b),
                                         ALU.mult, ALU.add).then_inc(updated, 1)

            update(0)
            with dve.Fori(1, B) as b:
                update(b)
                dve.wait_ge(updated, b)
                dve.bn_stats(row(keep.stats, b - 1), row(keep.x, b - 1))
            dve.wait_ge(updated, B)
            dve.bn_stats(keep.stats[:, B - 1, :], keep.x[:, B - 1, :])


def agent_attention(nc, keep, name, w):
    G = 4
    with ExitStack() as stack:
        scope = Scope(nc, stack, name)
        sb, psum, sem = scope.sb, scope.psum, scope.sem
        wq, wv = sb("wq", [128, DC, D]), sb("wv", [128, DC, D])
        wk_t, wv_t = sb("wk_t", [128, DC, D]), sb("wv_t", [128, DC, D])
        conv1, agent_w = sb("conv1", [128, DC]), sb("agent_w", [128, DC])
        normed, normed_t = sb("normed", [S, G, D]), sb("normed_t", [128, G, DC, S])
        agent, agents = sb("agent", [S, G]), sb("agents", [S, B])
        token_sum, channel_w = sb("token_sum", [128, DC, B]), sb("channel_w", [128, DC, B])
        key_sum, key_exp, key_probs = sb("key_sum", [B, D]), sb("key_exp", [B, D]), sb("key_probs", [B, D])
        key_probs_t = sb("key_probs_t", [128, DC, B])
        token_scores, token_rows = sb("token_scores", [S, B]), sb("token_rows", [B, S])
        token_exp, token_probs, token_weights = sb("token_exp", [B, S]), sb("token_probs", [B, S]), sb("token_weights", [S, B])
        stat = sb("stat", [B, 8])
        gathered = sb("gathered", [128, G, DC])
        own, own_exp, own_inverse, own_probs = (sb(n, [S, B]) for n in ("own", "own_exp", "own_inverse", "own_probs"))
        bank_a = [psum(f"bank_a{n}", [128, 512]) for n in range(G)]
        bank_b = [psum(f"bank_b{n}", [128, 512]) for n in range(G)]

        loaded = sem("loaded")
        agent_w_done, agent_w_ready = sem("agent_w_done"), sem("agent_w_ready")
        normed_ready, turned, turned_read = sem("normed_ready"), sem("turned"), sem("turned_read")
        agent_done, agent_ready, token_sum_done, token_sum_read = (
            sem(n) for n in ("agent_done", "agent_ready", "token_sum_done", "token_sum_read"))
        scores_done, scores_read = sem("scores_done"), sem("scores_read")
        gather_done, gather_read, value_done, updated = (sem(n) for n in ("gather_done", "gather_read", "value_done", "updated"))
        pe_step, dve_step, act_step, small_step = (sem(n) for n in ("pe_step", "dve_step", "act_step", "small_step"))
        block = stack.enter_context(nc.Block())

        @block.sync
        def _(sp):
            qkv, qkv_t = w["qkv"], w["qkv_t"]
            sp.dma_start(wq[:, :, :], qkv[0:D, :].rearrange("(c p) n -> p c n", p=128)).then_inc(loaded, 16)
            sp.dma_start(wv[:, :, :], qkv[2 * D:3 * D, :].rearrange("(c p) n -> p c n", p=128)).then_inc(loaded, 16)
            sp.dma_start(wk_t[:, :, :], qkv_t[:, D:2 * D].rearrange("(c p) n -> p c n", p=128)).then_inc(loaded, 16)
            sp.dma_start(wv_t[:, :, :], qkv_t[:, 2 * D:3 * D].rearrange("(c p) n -> p c n", p=128)).then_inc(loaded, 16)
            sp.dma_start(conv1[:, :], w["conv1"]).then_inc(loaded, 16)

        @block.tensor
        def _(pe):
            def turn(n, i, s):
                t = n * B + G * i + s
                pe.wait_ge(normed_ready, t + 1)
                reuse(pe, turned_read, t + 1 - G)
                for c in range(DC):
                    last = pe.transpose(bank_a[s][:, c * S:(c + 1) * S], normed[:, s, c * 128:(c + 1) * 128],
                                        keep.ident[0:S, 0:S])
                last.then_inc(turned, 1)

            def first_pass(i):
                for s in range(G):
                    turn(0, i, s)
                for s in range(G):
                    t = G * i + s
                    pe.wait_ge(turned_read, t + 1)
                    reuse(pe, token_sum_read, t + 1 - G)
                    for c in range(DC):
                        last = pe.matmul(bank_b[s][0:S, 0:1], normed_t[:, s, c, :], agent_w[:, c:c + 1], start=c == 0, stop=c == DC - 1)
                    last.then_inc(agent_done, 1)
                for s in range(G):
                    t = G * i + s
                    pe.wait_ge(agent_ready, t + 1)
                    for c in range(DC):
                        last = pe.matmul(bank_b[s][:, 8 + c:9 + c], normed[:, s, c * 128:(c + 1) * 128], agent[:, s:s + 1],
                                         start=True, stop=True)
                    last.then_inc(token_sum_done, 1)

            def second_pass(i):
                for s in range(G):
                    turn(1, i, s)
                for s in range(G):
                    t = G * i + s
                    pe.wait_ge(turned_read, B + t + 1)
                    reuse(pe, scores_read, t + 1 - G)
                    for c in range(DC):
                        last = pe.matmul(bank_b[s][0:S, 0:1], normed_t[:, s, c, :], channel_w[:, c, bass.ds(G * i + s, 1)],
                                         start=c == 0, stop=c == DC - 1)
                    last.then_inc(scores_done, 1)

            def third_pass(i):
                for s in range(G):
                    t = G * i + s
                    pe.wait_ge(normed_ready, 2 * B + t + 1)
                    reuse(pe, gather_read, t + 1 - G)
                    for c in range(DC):
                        last = pe.matmul(bank_a[s][:, c:c + 1], normed[:, s, c * 128:(c + 1) * 128],
                                         token_weights[:, bass.ds(G * i + s, 1)], start=True, stop=True)
                    last.then_inc(gather_done, 1)
                for s in range(G):
                    t = G * i + s
                    pe.wait_ge(gather_read, t + 1)
                    reuse(pe, updated, t + 1 - G)
                    for c in range(DC):
                        last = pe.matmul(bank_b[s][0:S, 0:D], gathered[:, s, c:c + 1].broadcast_to([128, S]), wv_t[:, c, :],
                                         start=c == 0, stop=c == DC - 1)
                    last.then_inc(value_done, 1)

            pe.wait_ge(loaded, 80)
            for m in range(DC):
                for c in range(DC):
                    last = pe.matmul(bank_a[0][:, m:m + 1], wq[:, c, m * 128:(m + 1) * 128], conv1[:, c:c + 1],
                                     start=c == 0, stop=c == DC - 1)
            last.then_inc(agent_w_done, 1)
            pe.wait_ge(agent_w_ready, 1)
            first_pass(0)
            with pe.Fori(1, B // G) as i:
                first_pass(i)

            pe.wait_ge(token_sum_read, B)
            for c in range(DC):
                last = pe.matmul(bank_a[0][0:B, 0:D], token_sum[:, c, :], wk_t[:, c, :], start=c == 0, stop=c == DC - 1)
            last.then_inc(pe_step, 1)
            pe.wait_ge(dve_step, 2)
            for c in range(DC):
                last = pe.transpose(bank_a[1][:, c * B:(c + 1) * B], key_probs[:, c * 128:(c + 1) * 128], keep.ident[0:B, 0:B])
            last.then_inc(pe_step, 1)
            pe.wait_ge(act_step, 2)
            for m in range(DC):
                for c in range(DC):
                    last = pe.matmul(bank_a[2][:, m * B:(m + 1) * B], wv[:, c, m * 128:(m + 1) * 128], key_probs_t[:, c, :],
                                     start=c == 0, stop=c == DC - 1)
            last.then_inc(pe_step, 1)
            pe.wait_ge(act_step, 3)
            second_pass(0)
            with pe.Fori(1, B // G) as i:
                second_pass(i)

            pe.wait_ge(scores_read, B)
            pe.transpose(bank_a[0][0:B, 0:S], token_scores[:, :], keep.ident[0:S, 0:S]).then_inc(pe_step, 1)
            pe.wait_ge(dve_step, 4)
            pe.transpose(bank_a[1][0:S, 0:B], token_probs[:, :], keep.ident[0:B, 0:B]).then_inc(pe_step, 1)
            pe.wait_ge(act_step, 5)
            third_pass(0)
            with pe.Fori(1, B // G) as i:
                third_pass(i)

        @block.scalar
        def _(act):
            def read_turned(n, i, s):
                t = n * B + G * i + s
                act.wait_ge(turned, t + 1)
                if n == 0:
                    reuse(act, agent_done, t + 1 - G)
                else:
                    act.wait_ge(agent_done, B)
                    reuse(act, scores_done, G * i + s + 1 - G)
                act.activation(normed_t[:, s, :, :].rearrange("p c s -> p (c s)"), bank_a[s][:, 0:DC * S],
                               ACT.Copy).then_inc(turned_read, 1)

            def first_pass(i):
                for s in range(G):
                    read_turned(0, i, s)
                for s in range(G):
                    t = G * i + s
                    act.wait_ge(agent_done, t + 1)
                    reuse(act, token_sum_done, t + 1 - G)
                    act.activation(agent[:, s:s + 1], bank_b[s][0:S, 0:1], ACT.Copy, scale=float(D) ** -0.5).then_inc(agent_ready, 1)
                for s in range(G):
                    t = G * i + s
                    act.wait_ge(token_sum_done, t + 1)
                    act.activation(agents[:, bass.ds(t, 1)], agent[:, s:s + 1], ACT.Copy)
                    act.activation(token_sum[:, :, bass.ds(t, 1)].rearrange("p c o -> p (c o)"), bank_b[s][:, 8:8 + DC],
                                   ACT.Copy).then_inc(token_sum_read, 1)

            def second_pass(i):
                for s in range(G):
                    read_turned(1, i, s)
                for s in range(G):
                    t = G * i + s
                    act.wait_ge(scores_done, t + 1)
                    act.activation(token_scores[:, bass.ds(t, 1)], bank_b[s][0:S, 0:1], ACT.Copy).then_inc(scores_read, 1)

            def third_pass(i):
                for s in range(G):
                    t = G * i + s
                    act.wait_ge(gather_done, t + 1)
                    reuse(act, value_done, t + 1 - G)
                    act.activation(gathered[:, s, :], bank_a[s][:, 0:DC], ACT.Copy).then_inc(gather_read, 1)

            act.wait_ge(agent_w_done, 1)
            act.activation(agent_w[:, :], bank_a[0][:, 0:DC], ACT.Copy).then_inc(agent_w_ready, 1)
            first_pass(0)
            with act.Fori(1, B // G) as i:
                first_pass(i)
            act.wait_ge(dve_step, 1)
            act.activation(key_exp[:, :], key_sum[:, :], ACT.Exp, bias=stat[:, 0:1], accum_out=stat[:, 1:2]).then_inc(act_step, 1)
            act.wait_ge(pe_step, 2)
            act.activation(key_probs_t[:, :, :].rearrange("p c b -> p (c b)"), bank_a[1][:, 0:DC * B], ACT.Copy).then_inc(act_step, 1)
            act.wait_ge(pe_step, 3)
            act.activation(channel_w[:, :, :].rearrange("p c b -> p (c b)"), bank_a[2][:, 0:DC * B], ACT.Copy).then_inc(act_step, 1)
            second_pass(0)
            with act.Fori(1, B // G) as i:
                second_pass(i)
            act.wait_ge(dve_step, 3)
            act.activation(token_exp[:, :], token_rows[:, :], ACT.Exp, bias=stat[:, 4:5], accum_out=stat[:, 5:6]).then_inc(act_step, 1)
            act.wait_ge(pe_step, 5)
            act.activation(token_weights[:, :], bank_a[1][0:S, 0:B], ACT.Copy).then_inc(act_step, 1)
            act.wait_ge(dve_step, 5)
            act.activation(own_exp[:, :], own[:, :], ACT.Exp).then_inc(act_step, 1)
            third_pass(0)
            with act.Fori(1, B // G) as i:
                third_pass(i)

        @block.vector
        def _(dve):
            def rows_in(n, i, s):
                t = n * B + G * i + s
                if n == 0:
                    reuse(dve, token_sum_done, t + 1 - G)
                elif n == 1:
                    if isinstance(i, int):
                        dve.wait_ge(token_sum_done, B)
                    reuse(dve, turned, t + 1 - G)
                else:
                    if isinstance(i, int):
                        dve.wait_ge(turned, 2 * B)
                    reuse(dve, gather_done, G * i + s + 1 - G)
                normalise(dve, keep, G * i + s, normed[:, s, :]).then_inc(normed_ready, 1)

            def rows_of(n, i):
                for s in range(G):
                    rows_in(n, i, s)

            def update(i):
                for s in range(G):
                    t = G * i + s
                    dve.wait_ge(value_done, t + 1)
                    dve.scalar_tensor_tensor(row(keep.x, t), bank_b[s][0:S, 0:D], own_probs[:, bass.ds(t, 1)], row(keep.x, t),
                                             ALU.mult, ALU.add).then_inc(updated, 1)
                for s in range(G):
                    t = G * i + s
                    dve.wait_ge(updated, t + 1)
                    dve.bn_stats(row(keep.stats, t), row(keep.x, t))

            rows_of(0, 0)
            with dve.Fori(1, B // G) as i:
                rows_of(0, i)

            def softmax(source, kept, exps, probs, at):
                dve.wait_ge(pe_step, 1 if at == 0 else 4)
                dve.reduce_max(stat[:, at + 2:at + 3], source, AX_X).then_inc(small_step, 1)
                dve.tensor_copy(kept, source).then_inc(small_step, 1)
                dve.wait_ge(small_step, 3 * (at > 0) + 2)
                dve.tensor_scalar(stat[:, at:at + 1], stat[:, at + 2:at + 3], -1.0, None, ALU.mult).then_inc(dve_step, 1)
                dve.wait_ge(act_step, 1 if at == 0 else 4)
                dve.reciprocal(stat[:, at + 3:at + 4], stat[:, at + 1:at + 2]).then_inc(small_step, 1)
                dve.wait_ge(small_step, 3 * (at > 0) + 3)
                dve.tensor_scalar(probs, exps, stat[:, at + 3:at + 4], None, ALU.mult).then_inc(dve_step, 1)

            softmax(bank_a[0][0:B, 0:D], key_sum[:, :], key_exp[:, :], key_probs[:, :], 0)
            rows_of(1, 0)
            with dve.Fori(1, B // G) as i:
                rows_of(1, i)
            softmax(bank_a[0][0:B, 0:S], token_rows[:, :], token_exp[:, :], token_probs[:, :], 4)
            dve.wait_ge(token_sum_read, B)
            dve.tensor_tensor(own[:, :], agents[:, :], agents[:, :], ALU.subtract).then_inc(dve_step, 1)
            dve.wait_ge(act_step, 6)
            dve.reciprocal(own_inverse[:, :], own_exp[:, :]).then_inc(small_step, 1)
            dve.wait_ge(small_step, 7)
            dve.tensor_tensor(own_probs[:, :], own_exp[:, :], own_inverse[:, :], ALU.mult).then_inc(small_step, 1)
            dve.wait_ge(small_step, 8)
            rows_of(2, 0)
            update(0)
            with dve.Fori(1, B // G) as i:
                rows_of(2, i)
                update(i)


def latent_moe(nc, keep, name, w):
    with ExitStack() as stack:
        scope = Scope(nc, stack, name)
        latent_t = scope.sb("latent_t", [128, DC, B, S])
        combine = scope.sb("combine", [S, B, 8])
        latent_attention(nc, keep, name + "a_", w, latent_t, combine)
        experts(nc, keep, name + "e_", w, latent_t, combine)


def latent_attention(nc, keep, name, w, latent_t, combine):
    E = 8
    LAT = H * KPH
    QUADS = H // 4
    VW = KPH + 1
    UNITS = 2 * QUADS
    with ExitStack() as stack:
        scope = Scope(nc, stack, name)
        sb, psum, sem = scope.sb, scope.psum, scope.sem
        wq, wk, wv = (sb(n, [128, DC, LAT]) for n in ("wq", "wk", "wv"))
        wo, router = sb("wo", [LAT, D]), sb("router", [128, DC, E])
        bq, bk, bv, bo = sb("bq", [LAT, 1]), sb("bk", [LAT, 1]), sb("bv", [S, LAT]), sb("bo", [128, DC])
        router_b, ones, preference = sb("router_b", [1, E]), sb("ones", [1, S]), sb("preference", [S, E])
        own_rows, k_bias = sb("own_rows", [LAT, 4]), sb("k_bias", [LAT, 4])
        normed = sb("normed", [S, 2, D])
        normed_t = sb("normed_t", [128, 2, DC, S])
        queries = sb("queries", [LAT, 2, S])
        keys = sb("keys", [LAT, 2, 4, S])
        values = sb("values", [S, 2, H, VW])
        top4 = sb("top4", [S, 2, 4])
        shifted, probs, probs_t = sb("shifted", [S, 2, 4, S]), sb("probs", [S, 2, 4, S]), sb("probs_t", [S, 2, 4, S])
        inverse, heads_out, heads_t = sb("inverse", [S, 2, H]), sb("heads_out", [S, 2, H, KPH]), sb("heads_t", [LAT, 2, S])
        latent = sb("latent", [128, 2, DC, S])
        logits = sb("logits", [S, B, E])
        exps, left, picked, first = (sb(n, [S, B, E]) for n in ("exps", "left", "picked", "first"))
        top, total = sb("top", [S, B]), sb("total", [S, B])
        qkv_bank = [psum(f"qkv_bank{n}", [128, 512]) for n in range(2)]
        score_bank = [psum(f"score_bank{n}", [128, 512]) for n in range(2)]
        turn_bank = [psum(f"turn_bank{n}", [128, 512]) for n in range(2)]
        heads_bank = [psum(f"heads_bank{n}", [128, 512]) for n in range(2)]
        heads_psum = [b[0:S, 0:H * VW].rearrange("p (h v) -> p h v", h=H) for b in heads_bank]
        heads_t_psum = [b[0:LAT, 160:160 + S] for b in heads_bank]
        latent_psum = [b[:, 272:272 + DC * S] for b in heads_bank]
        logits_psum = [b[0:S, 496:496 + E] for b in heads_bank]

        loaded, constants = sem("loaded"), sem("constants")
        normed_ready, turned, turned_read, residual_added = (sem(n) for n in ("normed_ready", "turned", "turned_read", "residual_added"))
        qkv_done, queries_ready, keys_ready = (sem(n) for n in ("qkv_done", "queries_ready", "keys_ready"))
        inverse_ready, heads_out_ready, heads_turned, heads_t_ready = (
            sem(n) for n in ("inverse_ready", "heads_out_ready", "heads_turned", "heads_t_ready"))
        latent_done, latent_ready, latent_kept, logits_done, logits_read = (
            sem(n) for n in ("latent_done", "latent_ready", "latent_kept", "logits_done", "logits_read"))
        scores_done, max_ready, shifted_ready, probs_ready, probs_turned, probs_t_ready, weighed = (
            sem(n) for n in ("scores_done", "max_ready", "shifted_ready", "probs_ready", "probs_turned", "probs_t_ready", "weighed"))
        routing, exps_ready = sem("routing"), sem("exps_ready")
        block = stack.enter_context(nc.Block())
        LOADED = 16 * 11

        @block.sync
        def _(sp):
            for tile, source in ((wq, "m_wq"), (wk, "m_wk"), (wv, "m_wv"), (router, "m_router")):
                sp.dma_start(tile[:, :, :], w[source].rearrange("(c p) n -> p c n", p=128)).then_inc(loaded, 16)
            sp.dma_start(wo[:, :], w["m_wo"][0:LAT, :]).then_inc(loaded, 16)
            for tile, source in ((bq, "m_bq"), (bk, "m_bk"), (bo, "m_bo"), (own_rows, "head_quarter")):
                sp.dma_start(tile[:, :], w[source]).then_inc(loaded, 16)
            sp.dma_start(bv[:, :], w["m_bv"].rearrange("(o n) -> o n", o=1).broadcast_to([S, LAT])).then_inc(loaded, 16)
            sp.dma_start(router_b[:, :], w["m_router_b"].rearrange("(o n) -> o n", o=1)).then_inc(loaded, 16)

        @block.gpsimd
        def _(pool):
            def keep_latent(i):
                for s in range(2):
                    t = 2 * i + s
                    pool.wait_ge(latent_ready, t + 1)
                    pool.tensor_copy(latent_t[:, :, bass.ds(t, 1), :].rearrange("p c o s -> p c (o s)"),
                                     latent[:, s, :, :]).then_inc(latent_kept, 1)

            keep_latent(0)
            with pool.Fori(1, B // 2) as i:
                keep_latent(i)

        @block.tensor
        def _(pe):
            def score(i, k):
                s, j = k % 2, k // 2
                t, n = 2 * i + s, UNITS * i + k
                if j == 0:
                    pe.wait_ge(queries_ready, t + 1)
                    pe.wait_ge(keys_ready, t + 1)
                reuse(pe, shifted_ready, n - 1)
                pe.matmul(score_bank[s][0:S, 0:4 * S], queries[32 * j:32 * j + 32, s, :],
                          keys[32 * j:32 * j + 32, s, :, :].rearrange("p r s -> p (r s)"), start=True, stop=True).then_inc(scores_done, 1)

            def turn(i, k):
                s, n = k % 2, UNITS * i + k
                pe.wait_ge(probs_ready, n + 1)
                reuse(pe, probs_t_ready, n - 1)
                for r in range(4):
                    last = pe.transpose(turn_bank[s][0:S, r * S:(r + 1) * S], probs[:, s, r, :], keep.ident[0:S, 0:S])
                last.then_inc(probs_turned, 1)

            def weigh(i, k):
                s, j, n = k % 2, k // 2, UNITS * i + k
                if j == 0:
                    reuse(pe, logits_read, 2 * i + s - 1)
                pe.wait_ge(probs_t_ready, n + 1)
                for r in range(4):
                    last = pe.matmul(heads_psum[s][:, 4 * j + r, :], probs_t[:, s, r, :], values[:, s, 4 * j + r, :],
                                     start=True, stop=True)
                last.then_inc(weighed, 1)

            def pair(i):
                for s in range(2):
                    t = 2 * i + s
                    pe.wait_ge(normed_ready, t + 1)
                    reuse(pe, keys_ready, t - 1)
                    for c in range(DC):
                        last = pe.transpose(qkv_bank[s][:, c * S:(c + 1) * S], normed[:, s, c * 128:(c + 1) * 128], keep.ident[0:S, 0:S])
                    last.then_inc(turned, 1)
                for s in range(2):
                    pe.wait_ge(turned_read, 2 * i + s + 1)
                    for n, weights in enumerate((wq, wk)):
                        for c in range(DC):
                            pe.matmul(qkv_bank[s][:, n * S:(n + 1) * S], weights[:, c, :], normed_t[:, s, c, :], start=c == 0, stop=c == DC - 1)
                    for c in range(DC):
                        last = pe.matmul(qkv_bank[s][0:S, 256:256 + LAT], normed_t[:, s, c, :], wv[:, c, :], start=c == 0, stop=c == DC - 1)
                    last.then_inc(qkv_done, 1)
                score(i, 0)
                for k in range(UNITS):
                    if k + 1 < UNITS:
                        score(i, k + 1)
                    turn(i, k)
                    if k >= 1:
                        weigh(i, k - 1)
                weigh(i, UNITS - 1)
                for s in range(2):
                    pe.wait_ge(heads_out_ready, 2 * i + s + 1)
                    pe.transpose(heads_t_psum[s], heads_out[:, s, :, :].rearrange("p h v -> p (h v)"), keep.ident[0:S, 0:S]).then_inc(heads_turned, 1)
                for s in range(2):
                    pe.wait_ge(heads_t_ready, 2 * i + s + 1)
                    for c in range(DC):
                        last = pe.matmul(latent_psum[s][:, c * S:(c + 1) * S], wo[:, c * 128:(c + 1) * 128], heads_t[:, s, :],
                                         start=True, stop=True)
                    last.then_inc(latent_done, 1)
                for s in range(2):
                    pe.wait_ge(latent_ready, 2 * i + s + 1)
                    pe.matmul(logits_psum[s], ones[:, :], router_b[:, :], start=True, stop=False)
                    for c in range(DC):
                        last = pe.matmul(logits_psum[s], latent[:, s, c, :], router[:, c, :], start=False, stop=c == DC - 1)
                    last.then_inc(logits_done, 1)

            pe.wait_ge(loaded, LOADED)
            pe.wait_ge(constants, 2)
            pair(0)
            with pe.Fori(1, B // 2) as i:
                pair(i)

        @block.scalar
        def _(act):
            def exponentials(i, k):
                s, n = k % 2, UNITS * i + k
                act.wait_ge(shifted_ready, n + 1)
                reuse(act, probs_turned, n - 1)
                act.activation(probs[:, s, :, :], shifted[:, s, :, :], ACT.Exp).then_inc(probs_ready, 1)

            def read_turned(i, k):
                s, n = k % 2, UNITS * i + k
                act.wait_ge(probs_turned, n + 1)
                reuse(act, weighed, n - 1)
                act.activation(probs_t[:, s, :, :].rearrange("p r s -> p (r s)"), turn_bank[s][0:S, 0:4 * S],
                               ACT.Copy).then_inc(probs_t_ready, 1)

            def pair(i):
                for s in range(2):
                    t = 2 * i + s
                    act.wait_ge(turned, t + 1)
                    reuse(act, qkv_done, t - 1)
                    act.activation(normed_t[:, s, :, :].rearrange("p c s -> p (c s)"), qkv_bank[s][:, 0:DC * S], ACT.Copy).then_inc(turned_read, 1)
                for s in range(2):
                    t = 2 * i + s
                    act.wait_ge(qkv_done, t + 1)
                    reuse(act, scores_done, UNITS * i)
                    act.activation(queries[:, s, :], qkv_bank[s][:, 0:S], ACT.Identity, bias=bq[:, :]).then_inc(queries_ready, 1)
                exponentials(i, 0)
                for k in range(UNITS):
                    if k + 1 < UNITS:
                        exponentials(i, k + 1)
                    read_turned(i, k)
                for s in range(2):
                    t = 2 * i + s
                    act.wait_ge(heads_turned, t + 1)
                    reuse(act, latent_done, t - 1)
                    act.activation(heads_t[:, s, :], heads_t_psum[s], ACT.Copy).then_inc(heads_t_ready, 1)
                for s in range(2):
                    t = 2 * i + s
                    act.wait_ge(latent_done, t + 1)
                    reuse(act, latent_kept, t - 1)
                    reuse(act, logits_done, t - 1)
                    for c in range(DC):
                        last = act.activation(latent[:, s, c, :], latent_psum[s][:, c * S:(c + 1) * S], ACT.Identity, bias=bo[:, c:c + 1])
                    last.then_inc(latent_ready, 1)

            act.wait_ge(loaded, LOADED)
            pair(0)
            with act.Fori(1, B // 2) as i:
                pair(i)
            act.wait_ge(routing, 2)
            act.activation(exps[:, :, :], exps[:, :, :], ACT.Exp).then_inc(exps_ready, 1)

        @block.vector
        def _(dve):
            def shift(i, k):
                s, n = k % 2, UNITS * i + k
                bank = score_bank[s][0:S, 0:4 * S].rearrange("p (r s) -> p r s", r=4)
                dve.wait_ge(scores_done, n + 1)
                dve.reduce_max(top4[:, s, :], bank, AX_X).then_inc(max_ready, 1)
                dve.wait_ge(max_ready, n + 1)
                reuse(dve, probs_ready, n - 1)
                dve.tensor_tensor(shifted[:, s, :, :], bank, top4[:, s, :].unsqueeze(2).broadcast_to([S, 4, S]),
                                  ALU.subtract).then_inc(shifted_ready, 1)

            def pair(i):
                for s in range(2):
                    t = 2 * i + s
                    reuse(dve, turned, t - 1)
                    normalise(dve, keep, t, normed[:, s, :]).then_inc(normed_ready, 1)
                for s in range(2):
                    t = 2 * i + s
                    dve.wait_ge(normed_ready, t + 1)
                    dve.tensor_tensor(row(keep.x, t), row(keep.x, t), normed[:, s, :], ALU.add)
                for s in range(2):
                    t = 2 * i + s
                    dve.wait_ge(queries_ready, t + 1)
                    reuse(dve, weighed, UNITS * i)
                    for r in range(4):
                        dve.tensor_scalar(keys[:, s, r, :], qkv_bank[s][:, S:2 * S], own_rows[:, r:r + 1], k_bias[:, r:r + 1], ALU.mult, ALU.add)
                    dve.tensor_tensor(values[:, s, :, 0:KPH], qkv_bank[s][0:S, 256:256 + LAT].rearrange("p (h v) -> p h v", h=H),
                                      bv[:, :].rearrange("p (h v) -> p h v", h=H), ALU.add).then_inc(keys_ready, 1)
                for k in range(UNITS):
                    shift(i, k)
                for s in range(2):
                    t = 2 * i + s
                    dve.wait_ge(weighed, UNITS * i + UNITS - 1 + s)
                    dve.reciprocal(inverse[:, s, :], heads_psum[s][:, :, KPH]).then_inc(inverse_ready, 1)
                    dve.wait_ge(inverse_ready, t + 1)
                    reuse(dve, heads_turned, t - 1)
                    dve.tensor_tensor(heads_out[:, s, :, :], heads_psum[s][:, :, 0:KPH],
                                      inverse[:, s, :].unsqueeze(2).broadcast_to([S, H, KPH]), ALU.mult).then_inc(heads_out_ready, 1)
                for s in range(2):
                    t = 2 * i + s
                    dve.wait_ge(logits_done, t + 1)
                    dve.tensor_copy(row(logits, t), logits_psum[s]).then_inc(logits_read, 1)

            def wide(column):
                return column[:, :].unsqueeze(2).broadcast_to([S, B, E])

            def pick_best(source, out, steps):
                dve.reduce_max(top[:, :], source[:, :, :], AX_X).then_inc(routing, 1)
                dve.wait_ge(routing, steps + 1)
                dve.tensor_tensor(out[:, :, :], source[:, :, :], wide(top), ALU.is_ge).then_inc(routing, 1)
                dve.wait_ge(routing, steps + 2)
                dve.tensor_tensor(out[:, :, :], out[:, :, :], preference[:, :].unsqueeze(1).broadcast_to([S, B, E]), ALU.mult).then_inc(routing, 1)
                dve.wait_ge(routing, steps + 3)
                dve.reduce_max(top[:, :], out[:, :, :], AX_X).then_inc(routing, 1)
                dve.wait_ge(routing, steps + 4)
                dve.tensor_tensor(out[:, :, :], out[:, :, :], wide(top), ALU.is_equal).then_inc(routing, 1)
                dve.wait_ge(routing, steps + 5)

            dve.memset(ones[:, :], 1.0).then_inc(constants, 1)
            dve.memset(values[:, :, :, KPH:VW], 1.0).then_inc(constants, 1)
            for e in range(E):
                last = dve.memset(preference[:, e:e + 1], float(E - e))
            last.then_inc(constants, 1)
            dve.wait_ge(loaded, LOADED)
            dve.tensor_scalar(own_rows[:, :], own_rows[:, :], float(KPH) ** -0.5, None, ALU.mult).then_inc(constants, 1)
            dve.wait_ge(constants, 4)
            dve.tensor_scalar(k_bias[:, :], own_rows[:, :], bk[:, :], None, ALU.mult).then_inc(constants, 1)
            dve.wait_ge(constants, 5)
            pair(0)
            with dve.Fori(1, B // 2) as i:
                pair(i)
            dve.wait_ge(logits_read, B)
            dve.reduce_max(top[:, :], logits[:, :, :], AX_X).then_inc(routing, 1)
            dve.wait_ge(routing, 1)
            dve.tensor_tensor(exps[:, :, :], logits[:, :, :], wide(top), ALU.subtract).then_inc(routing, 1)
            dve.wait_ge(exps_ready, 1)
            dve.reduce_sum(total[:, :], exps[:, :, :], AX_X).then_inc(routing, 1)
            dve.wait_ge(routing, 3)
            dve.reciprocal(total[:, :], total[:, :]).then_inc(routing, 1)
            dve.wait_ge(routing, 4)
            dve.tensor_tensor(exps[:, :, :], exps[:, :, :], wide(total), ALU.mult).then_inc(routing, 1)
            dve.wait_ge(routing, 5)
            pick_best(exps, first, 5)
            dve.scalar_tensor_tensor(left[:, :, :], first[:, :, :], -2.0, exps[:, :, :], ALU.mult, ALU.add).then_inc(routing, 1)
            dve.wait_ge(routing, 11)
            pick_best(left, picked, 11)
            dve.tensor_tensor(picked[:, :, :], picked[:, :, :], first[:, :, :], ALU.add).then_inc(routing, 1)
            dve.wait_ge(routing, 17)
            dve.tensor_tensor(picked[:, :, :], picked[:, :, :], exps[:, :, :], ALU.mult).then_inc(routing, 1)
            dve.wait_ge(routing, 18)
            dve.reduce_sum(total[:, :], picked[:, :, :], AX_X).then_inc(routing, 1)
            dve.wait_ge(routing, 19)
            dve.tensor_scalar(total[:, :], total[:, :], 1e-8, None, ALU.add).then_inc(routing, 1)
            dve.wait_ge(routing, 20)
            dve.reciprocal(total[:, :], total[:, :]).then_inc(routing, 1)
            dve.wait_ge(routing, 21)
            dve.tensor_tensor(picked[:, :, :], picked[:, :, :], wide(total), ALU.mult).then_inc(routing, 1)
            dve.wait_ge(routing, 22)
            dve.tensor_scalar(combine[:, :, :], picked[:, :, :], 0.3, None, ALU.mult)


def experts(nc, keep, name, w, latent_t, combine):
    E, G = 8, 4
    GROUPS = B // G
    T = G * S
    F = 512
    FC = F // 128
    with ExitStack() as stack:
        scope = Scope(nc, stack, name)
        sb, psum, sem = scope.sb, scope.psum, scope.sem
        w1, w2 = sb("w1", [128, E, DC, F]), sb("w2", [128, E, FC, D])
        b1, b2 = sb("b1", [128, E, FC]), sb("b2", [E, D])
        hidden = sb("hidden", [128, 2, FC, T])
        combine_here, combine_t = sb("combine_here", [S, G, E]), sb("combine_t", [E, G, S])
        hidden_bank = [psum(f"hidden_bank{n}", [128, 512]) for n in range(FC)]
        out_bank = [psum(f"out_bank{n}", [128, 512]) for n in range(G)]
        small_loaded = sem("small_loaded")
        expert_loaded = [sem(f"expert_loaded{e}") for e in range(E)]
        here_ready, combine_turned, combine_t_ready = sem("here_ready"), sem("combine_turned"), sem("combine_t_ready")
        hidden_done, hidden_ready = sem("hidden_done"), sem("hidden_ready")
        out_done = [sem(f"out_done{n}") for n in range(G)]
        out_read = [sem(f"out_read{n}") for n in range(G)]
        block = stack.enter_context(nc.Block())
        USES = E + 1

        @block.sync
        def _(sp):
            sp.dma_start(b1[:, :, :], w["m_b1"]).then_inc(small_loaded, 16)
            sp.dma_start(b2[:, :], w["m_b2"]).then_inc(small_loaded, 16)
            for e in range(E):
                sp.dma_start(w1[:, e, :, :], w["m_w1"][e].rearrange("(c p) n -> p c n", p=128)).then_inc(expert_loaded[e], 16)
                sp.dma_start(w2[:, e, :, :], w["m_w2"][e].rearrange("(c p) n -> p c n", p=128)).then_inc(expert_loaded[e], 16)

        @block.tensor
        def _(pe):
            def hide(g, e):
                if isinstance(g, int):
                    pe.wait_ge(expert_loaded[e], 32)
                for m in range(FC):
                    n = FC * (E * g + e) + m
                    reuse(pe, hidden_ready, n + 1 - FC)
                    for c in range(DC):
                        last = pe.matmul(hidden_bank[m][:, 0:T], w1[:, e, c, m * 128:(m + 1) * 128],
                                         latent_t[:, c, bass.ds(G * g, G), :].rearrange("p b s -> p (b s)"),
                                         start=c == 0, stop=c == DC - 1)
                    last.then_inc(hidden_done, 1)

            def unhide(g, e):
                for m in range(FC):
                    pe.wait_ge(hidden_ready, FC * (E * g + e) + m + 1)
                for b in range(G):
                    reuse(pe, out_read[b], USES * g + 1 + e)
                    for m in range(FC):
                        last = pe.matmul(out_bank[b][0:S, 0:D], hidden[:, e % 2, m, b * S:(b + 1) * S], w2[:, e, m, :],
                                         start=m == 0, stop=m == FC - 1)
                    last.then_inc(out_done[b], 1)

            def group(g):
                hide(g, 0)
                pe.wait_ge(here_ready, g + 1)
                for b in range(G):
                    reuse(pe, out_read[b], USES * g)
                    last = pe.transpose(out_bank[b][0:E, D:D + S], combine_here[:, b, :], keep.ident[0:S, 0:S])
                last.then_inc(combine_turned, 1)
                pe.wait_ge(combine_t_ready, g + 1)
                for b in range(G):
                    pe.matmul(out_bank[b][0:S, 0:D], combine_t[:, b, :], b2[:, :], start=True, stop=True).then_inc(out_done[b], 1)
                for e in range(E):
                    if e + 1 < E:
                        hide(g, e + 1)
                    unhide(g, e)

            pe.wait_ge(small_loaded, 32)
            group(0)
            with pe.Fori(1, GROUPS) as g:
                group(g)

        @block.scalar
        def _(act):
            def gelu(g, e):
                for m in range(FC):
                    n = FC * (E * g + e) + m
                    act.wait_ge(hidden_done, n + 1)
                    if e >= 2:
                        act.wait_ge(out_done[G - 1], USES * g + e)
                    else:
                        reuse(act, out_done[G - 1], 0 if isinstance(g, int) and g == 0 else USES * g - 1 + e)
                    act.activation(hidden[:, e % 2, m, :], hidden_bank[m][:, 0:T], ACT.Gelu, bias=b1[:, e, m:m + 1]).then_inc(hidden_ready, 1)

            def group(g):
                gelu(g, 0)
                act.wait_ge(combine_turned, g + 1)
                for b in range(G):
                    last = act.activation(combine_t[:, b, :], out_bank[b][0:E, D:D + S], ACT.Copy)
                last.then_inc(combine_t_ready, 1)
                for e in range(1, E):
                    gelu(g, e)

            act.wait_ge(small_loaded, 32)
            group(0)
            with act.Fori(1, GROUPS) as g:
                group(g)

        @block.vector
        def _(dve):
            def group(g):
                reuse(dve, combine_turned, g)
                for b in range(G):
                    reuse(dve, out_read[b], USES * g)
                dve.tensor_copy(combine_here[:, :, :], combine[:, bass.ds(G * g, G), :]).then_inc(here_ready, 1)
                for use in range(USES):
                    for b in range(G):
                        x_row = row(keep.x, G * g + b)
                        out = out_bank[b][0:S, 0:D]
                        dve.wait_ge(out_done[b], USES * g + use + 1)
                        reuse(dve, out_read[b], USES * g + use)
                        if use == 0:
                            dve.tensor_tensor(x_row, out, x_row, ALU.add).then_inc(out_read[b], 1)
                        else:
                            dve.scalar_tensor_tensor(x_row, out, combine_here[:, b, use - 1:use], x_row,
                                                     ALU.mult, ALU.add).then_inc(out_read[b], 1)

            group(0)
            with dve.Fori(1, GROUPS) as g:
                group(g)


def store_x(nc, keep, out):
    with ExitStack() as stack:
        stored = stack.enter_context(nc.semaphore("x_stored"))
        block = stack.enter_context(nc.Block())

        @block.sync
        def _(sp):
            sp.dma_start(out.rearrange("b s d -> s b d"), keep.x[:, :, :]).then_inc(stored, 16)
            sp.wait_ge(stored, 16)


class Keep:

    def __init__(self, nc, stack, ident_in):
        scope = Scope(nc, stack, "keep_")
        self.x = scope.sb("x", [S, B, D])
        self.stats = scope.sb("stats", [S, B, 6])
        self.moments = scope.sb("moments", [S, B, 2])
        self.rstd = scope.sb("rstd", [S, B])
        self.ident = scope.sb("ident", [128, 128])
        self.eps = scope.sb("eps", [128, 1])
        self.masked_score = scope.sb("masked_score", [128, 1])
        self.one = scope.sb("one", [128, 1])
        loaded = scope.sem("loaded")
        with nc.Block() as block:
            @block.sync
            def _(sp):
                sp.dma_start(self.ident[:, :], ident_in).then_inc(loaded, 16)
                sp.wait_ge(loaded, 16)

            @block.vector
            def _(dve):
                dve.memset(self.eps[:, :], EPS)
                dve.memset(self.one[:, :], 1.0)
                dve.memset(self.masked_score[:, :], -1e-9)


def decoder(nc, t, out):
    with ExitStack() as stack:
        keep = Keep(nc, stack, t["ident"])
        load_and_first_stats(nc, keep, t["x"])
        if 1 in PHASES:
            layernorm_scales(nc, keep, "n1_")
            mamba(nc, keep, "mb_", t)
        if 2 in PHASES:
            layernorm_scales(nc, keep, "n2_")
            cross_attention(nc, keep, "xa0_", t["ctx_t"], t["x0_wq_t"], t["x0_wk_t"], t["x0_wv_t"], t["x0_wo_t"],
                            t["x0_bq_cols"], t["x0_bk_cols"], t["x0_bv"], t["x0_bo"], t["head_parity"],
                            t["mask"], t["mask_t"], None)
        if 3 in PHASES:
            layernorm_scales(nc, keep, "n3_")
            switch_ffn(nc, keep, "sf_", t)
        if 4 in PHASES:
            layernorm_scales(nc, keep, "n4_")
            agent_attention(nc, keep, "ag_", t)
        if 5 in PHASES:
            layernorm_scales(nc, keep, "n5_")
            cross_attention(nc, keep, "xa1_", t["ctx_t"], t["x1_wq_t"], t["x1_wk_t"], t["x1_wv_t"], t["x1_wo_t"],
                            None, None, None, t["x1_bo"], t["head_parity"], None, None, t["key_mask"])
        if 6 in PHASES:
            layernorm_scales(nc, keep, "n6_")
            latent_moe(nc, keep, "lm_", t)
        store_x(nc, keep, out)


def kernel(**inputs):
    import concourse.bacc as bacc
    from concourse.bass_utils import run_bass_kernel_spmd

    a = {n: np.ascontiguousarray(v) for n, v in inputs.items()}

    def t_(v):
        return np.ascontiguousarray(np.swapaxes(v, -1, -2))

    def cols(v):
        return np.ascontiguousarray(v.reshape(-1, 128).T)

    parity = np.zeros((128, 2), np.float32)
    for p in range(128):
        parity[p, p // DK % 2] = DK ** -0.5
    quarter = np.zeros((128, 4), np.float32)
    for p in range(128):
        quarter[p, p // KPH % 4] = 1.0
    arrays = {
        "x": a["x"], "ident": np.eye(128, dtype=np.float32), "head_parity": parity, "head_quarter": quarter,
        "upto": np.triu(np.ones((S, S), np.float32)),
        "own_row": np.kron(np.eye(32, dtype=np.float32), np.ones((1, 128), np.float32)),
        "ctx_t": t_(a["ctx_1024"]),
        "mask": a["mask_1x1xSxS2_if1"].reshape(S, SK), "mask_t": t_(a["mask_1x1xSxS2_if1"].reshape(S, SK)),
        "key_mask": a["mask_BxS2_bf1"].view(np.uint8),
        "x0_wq_t": t_(a["L0_xattn_wq"]), "x0_wk_t": t_(a["L0_xattn_wk"]), "x0_wv_t": t_(a["L0_xattn_wv"]),
        "x0_wo_t": t_(a["L0_xattn_wo"]), "x0_bq_cols": cols(a["L0_xattn_bq"]), "x0_bk_cols": cols(a["L0_xattn_bk"]),
        "x0_bv": a["L0_xattn_bv"], "x0_bo": a["L0_xattn_bo"],
        "x1_wq_t": t_(a["L1_xattn_Wq"]), "x1_wk_t": t_(a["L1_xattn_Wk"]), "x1_wv_t": t_(a["L1_xattn_Wv"]),
        "x1_wo_t": t_(a["L1_xattn_Wo"]), "x1_bo": a["L1_xattn_bo"],
        "w_in": a["L0_attn_W_in"], "conv": np.ascontiguousarray(a["L0_attn_dw_kernel"].reshape(4, 4, 128).transpose(2, 1, 0)),
        "pw": a["L0_attn_pw_kernel"], "conv_bias": cols(a["L0_attn_conv_bias"]),
        "w_x": a["L0_attn_W_x"], "w_dt": a["L0_attn_W_dt"], "b_dt": cols(a["L0_attn_b_dt"]),
        "a_log": np.ascontiguousarray(a["L0_attn_A_log"].reshape(4, 128, 8).transpose(1, 0, 2)),
        "skip": cols(a["L0_attn_D"]), "w_out": a["L0_attn_W_out"],
        "gate": a["L0_ffn_Wg"], "expert": a["L0_ffn_We"], "expert_bias": a["L0_ffn_be"],
        "qkv": a["L1_attn_w_qkv"], "qkv_t": t_(a["L1_attn_w_qkv"]), "conv1": cols(a["L1_attn_w_conv1"]),
        "m_wq": np.ascontiguousarray(a["L1_ffn_q_w"].reshape(D, H, DK)[:, :, :KPH].reshape(D, H * KPH)),
        "m_bq": np.ascontiguousarray(a["L1_ffn_q_b"].reshape(H, DK)[:, :KPH].reshape(H * KPH, 1)),
        "m_wk": a["L1_ffn_k_w"], "m_bk": cols(a["L1_ffn_k_b"]), "m_wv": a["L1_ffn_v_w"], "m_bv": a["L1_ffn_v_b"],
        "m_wo": a["L1_ffn_o_w"], "m_bo": cols(a["L1_ffn_o_b"]), "m_router": a["L1_ffn_router_w"],
        "m_router_b": a["L1_ffn_router_b"], "m_w1": a["L1_ffn_w1"],
        "m_b1": np.ascontiguousarray(a["L1_ffn_b1"].reshape(8, 4, 128).transpose(2, 0, 1)),
        "m_w2": a["L1_ffn_w2"], "m_b2": a["L1_ffn_b2"],
    }
    nc = bacc.Bacc("TRN2", target_bir_lowering=False, num_devices=1)
    tensors = {n: nc.dram_tensor(f"in_{n}", v.shape, mybir.dt.from_np(v.dtype), kind="ExternalInput").ap()
               for n, v in arrays.items()}
    out = nc.dram_tensor("out_x", (B, S, D), F32, kind="ExternalOutput").ap()
    decoder(nc, tensors, out)
    result = run_bass_kernel_spmd(nc, [{f"in_{n}": v for n, v in arrays.items()}], core_ids=[0])
    return result.results[0]["out_x"]
```

```python
from contextlib import ExitStack

import numpy as np

import concourse.bass as bass
from concourse import mybir

F32 = mybir.dt.float32
BF16 = mybir.dt.bfloat16
ALU = mybir.AluOpType
ACT = mybir.ActivationFunctionType
AX_X = mybir.AxisListType.X

B, S, D = 32, 112, 256
SK = 375
KC, KP = 3, 125
DC = D // 128
H, DK = 16, 16
EPS = 1e-5
BIG = 3.0e38


class Scope:

    def __init__(self, nc, stack, prefix):
        self.nc, self.stack, self.prefix = nc, stack, prefix
        self.sems = []
        stack.callback(self.clear)

    def sb(self, name, shape, dt=F32):
        return self.stack.enter_context(self.nc.sbuf_tensor(self.prefix + name, shape, dt))

    def psum(self, name, shape, dt=F32):
        return self.stack.enter_context(self.nc.psum_tensor(self.prefix + name, shape, dt))

    def sem(self, name):
        self.sems.append(self.nc.alloc_semaphore(name=self.prefix + name))
        return self.sems[-1]

    def clear(self):
        if self.sems:
            self.nc.clear_and_free_semaphores(self.sems)
            self.nc.all_engine_barrier()


def reuse(eng, sem, count):
    if not (isinstance(count, int) and count <= 0):
        eng.wait_ge(sem, count)


def row(tensor, b):
    return tensor[:, bass.ds(b, 1), :].rearrange("p o d -> p (o d)")


def normalise(dve, keep, b, out):
    return dve.tensor_scalar(out, row(keep.x, b), keep.moments[:, bass.ds(b, 1), 0], keep.rstd[:, bass.ds(b, 1)],
                             ALU.subtract, ALU.mult)


def load_and_first_stats(nc, keep, x_in):
    with ExitStack() as stack:
        scope = Scope(nc, stack, "ld_")
        x_loaded = [scope.sem(f"x_loaded{n}") for n in range(4)]
        block = stack.enter_context(nc.Block())
        part = B // 4

        @block.sync
        def _(sp):
            for n in range(4):
                sp.dma_start(keep.x[:, n * part:(n + 1) * part, :],
                             x_in[n * part:(n + 1) * part].rearrange("b s d -> s b d")).then_inc(x_loaded[n], 16)
            for n in range(4):
                sp.wait_ge(x_loaded[n], 16)

        @block.vector
        def _(dve):
            for n in range(4):
                dve.wait_ge(x_loaded[n], 16)
                for b in range(n * part, (n + 1) * part):
                    dve.bn_stats(keep.stats[:, b, :], keep.x[:, b, :])


def layernorm_scales(nc, keep, name):
    with ExitStack() as stack:
        scope = Scope(nc, stack, name)
        deviation = scope.sb("deviation", [S, B])
        aggregated = scope.sem("aggregated")
        rooted = scope.sem("rooted")
        block = stack.enter_context(nc.Block())

        @block.vector
        def _(dve):
            for b in range(B):
                last = dve.bn_aggr(keep.moments[:, b, :], keep.stats[:, b, :])
            last.then_inc(aggregated, 1)
            dve.wait_ge(rooted, 1)
            dve.reciprocal(keep.rstd[:, :], deviation[:, :])

        @block.scalar
        def _(act):
            act.wait_ge(aggregated, 1)
            act.activation(deviation[:, :], keep.moments[:, :, 1], ACT.Sqrt, bias=keep.eps[0:S, :]).then_inc(rooted, 1)
KPH = 8
PHASES = (1, 2, 3, 4, 5, 6,)


def mamba(nc, keep, name, w):
    G = 4
    GROUPS = B // G
    T = G * S
    DI, N, R, TAPS = 512, 8, 16, 4
    IC = DI // 128
    STEPS = 2 * TAPS - 1
    LOW = R + 2 * N
    FRONT = 18 // 2
    with ExitStack() as stack:
        scope = Scope(nc, stack, name)
        sb, psum, sem = scope.sb, scope.psum, scope.sem
        w_in, pw, w_out = sb("w_in", [128, DC, 2 * DI]), sb("pw", [128, IC, DI]), sb("w_out", [128, IC, D])
        w_x, w_dt = sb("w_x", [128, IC, R + 2 * N]), sb("w_dt", [R, DI])
        conv, conv_bias, b_dt, skip_w = sb("conv", [128, IC, TAPS]), sb("conv_bias", [128, IC]), sb("b_dt", [128, IC]), sb("skip", [128, IC])
        a_log, decay_rate = sb("a_log", [128, IC, N]), sb("decay_rate", [128, IC, N])
        own_row_f32 = sb("own_row_f32", [3 * LOW, 2 * N, 128])
        own_row = sb("own_row", [3 * LOW, 2 * N, 128], BF16)
        normed = sb("normed", [S, G, D])
        normed_t = sb("normed_t", [128, DC, T])
        padded = sb("padded", [128, IC, G, TAPS - 1 + S])
        mixed = sb("mixed", [128, IC, T])
        tap_product = sb("tap_product", [128, IC, T])
        inner = sb("inner", [128, IC, T])
        gates = sb("gates", [128, IC, T])
        low = sb("low", [LOW, T])
        part1, part2, rest1, rest2 = (sb("part1", [LOW, T], BF16), sb("part2", [LOW, T], BF16),
                                      sb("rest1", [LOW, T]), sb("rest2", [LOW, T]))
        low_parts = sb("low_parts", [3 * LOW, T], BF16)
        skip_term = sb("skip_term", [128, IC, T])
        gated_y = sb("gated_y", [128, IC, T])
        soft = sb("soft", [128, IC, T])
        delta = sb("delta", [128, IC, T])
        delta_inner = sb("delta_inner", [128, IC, T])
        decay = sb("decay", [128, 2, IC, T])
        drive = sb("drive", [128, IC, T])
        state = sb("state", [128, IC, T])
        read_out = sb("read_out", [128, 2, IC, T])
        y_bank = [psum(f"y_bank{n}", [128, 512]) for n in range(IC)]
        front_bank = [psum(f"front_bank{n}", [128, 512]) for n in range(2)]
        row_bank = [psum(f"row_bank{n}", [128, 512]) for n in range(2)]

        loaded, setup, negated = sem("loaded"), sem("setup"), sem("negated")
        normed_ready = sem("normed_ready")
        front_done = [sem(f"front_done{n}") for n in range(2)]
        front_read = [sem(f"front_read{n}") for n in range(2)]
        row_done = [sem(f"row_done{n}") for n in range(2)]
        row_read = [sem(f"row_read{n}") for n in range(2)]
        mixed_ready = sem("mixed_ready")
        mixed_started = sem("mixed_started")
        relu_ready, abs_ready, log_ready, delta_ready, delta_inner_ready = (
            sem(n) for n in ("relu_ready", "abs_ready", "log_ready", "delta_ready", "delta_inner_ready"))
        decay_ready, cut_ready, drive_ready, state_ready, summed = (
            sem(n) for n in ("decay_ready", "cut_ready", "drive_ready", "state_ready", "summed"))
        skip_ready, skipped, gated = sem("skip_ready"), sem("skipped"), sem("gated")
        split = sem("split")
        stacked = sem("stacked")
        block = stack.enter_context(nc.Block())
        LOADED = 16 * 11

        ROW_USES = (N + 1 + G // 2, N + G // 2)

        def use_of_low(g):
            return 0 if isinstance(g, int) and g == 0 else 1 + ROW_USES[0] * (g - 1) + N

        def use_of_row(g, k, n):
            return ROW_USES[k] * g + n + (k == 0)

        def use_of_out(g, b, final):
            return use_of_row(g, b % 2, N + b // 2) + (b % 2 == 0 and not final)

        def all_groups(eng, group):
            group(0)
            with eng.Fori(1, GROUPS - 1) as g:
                group(g)
            group(GROUPS - 1, final=True)

        def flat(a):
            return a.rearrange("p c t -> p (c t)")

        @block.sync
        def _(sp):
            for tile, source, k in ((w_in, "w_in", DC), (pw, "pw", IC), (w_out, "w_out", IC), (w_x, "w_x", IC)):
                sp.dma_start(tile[:, :, :], w[source].rearrange("(c p) n -> p c n", c=k)).then_inc(loaded, 16)
            sp.dma_start(w_dt[:, :], w["w_dt"]).then_inc(loaded, 16)
            for tile, source in ((conv, "conv"), (a_log, "a_log")):
                sp.dma_start(tile[:, :, :], w[source]).then_inc(loaded, 16)
            for tile, source in ((conv_bias, "conv_bias"), (b_dt, "b_dt"), (skip_w, "skip")):
                sp.dma_start(tile[:, :], w[source]).then_inc(loaded, 16)
            sp.dma_start(own_row_f32[:, :, :].rearrange("p r n -> p (r n)"), w["own_row"]).then_inc(loaded, 16)

        Z = 7

        @block.gpsimd
        def _(pool):
            def convolve(g):
                for k in range(2):
                    pool.wait_ge(front_read[k], FRONT * g + 3)
                    reuse(pool, front_done[k], FRONT * (g - 1) + 5)
                out = mixed[:, :, :].rearrange("p c (b s) -> p c b s", b=G)
                part = tap_product[:, :, :].rearrange("p c (b s) -> p c b s", b=G)
                for tap in range(TAPS):
                    before = STEPS * g + max(0, 2 * tap - 1)
                    reuse(pool, mixed_ready, before)
                    pool.sem_inc(mixed_started, 1)
                    pool.tensor_tensor(out if tap == 0 else part, padded[:, :, :, tap:tap + S],
                                       conv[:, :, tap:tap + 1].unsqueeze(3).broadcast_to([128, IC, G, S]), ALU.mult).then_inc(mixed_ready, 1)
                    if tap > 0:
                        pool.wait_ge(mixed_ready, before + 1)
                        pool.sem_inc(mixed_started, 1)
                        pool.tensor_tensor(out, out, part, ALU.add).then_inc(mixed_ready, 1)

            def group(g, final=False):
                if not final:
                    convolve(g + 1)

            pool.wait_ge(loaded, LOADED)
            pool.wait_ge(setup, 3)
            convolve(0)
            all_groups(pool, group)

        @block.tensor
        def _(pe):
            def front(g, u):
                reuse(pe, front_read[u % 2], FRONT * g + u // 2)
                return front_bank[u % 2]

            def turn_rows(g):
                pe.wait_ge(normed_ready, G * (g + 1))
                for c in range(DC):
                    bank = front(g, c)
                    for b in range(G):
                        last = pe.transpose(bank[:, b * S:(b + 1) * S], normed[:, b, c * 128:(c + 1) * 128], keep.ident[0:S, 0:S])
                    last.then_inc(front_done[c % 2], 1)

            def project_in(g, u, chunks):
                for c in range(DC):
                    pe.wait_ge(front_read[c], FRONT * g + 1)
                for m in chunks:
                    bank = front(g, u + m % IC)
                    for c in range(DC):
                        last = pe.matmul(bank[:, 0:T], w_in[:, c, m * 128:(m + 1) * 128], normed_t[:, c, :],
                                         start=c == 0, stop=c == DC - 1)
                    last.then_inc(front_done[m % 2], 1)

            def pointwise(g):
                pe.wait_ge(mixed_ready, STEPS * (g + 1))
                for m in range(IC):
                    bank = front(g, 6 + m)
                    for c in range(IC):
                        last = pe.matmul(bank[:, 0:T], pw[:, c, m * 128:(m + 1) * 128], mixed[:, c, :],
                                         start=c == 0, stop=c == IC - 1)
                    last.then_inc(front_done[m % 2], 1)

            def low_rank(g):
                for k in range(2):
                    pe.wait_ge(front_read[k], FRONT * g + 5)
                reuse(pe, row_read[0], use_of_low(g))
                for c in range(IC):
                    last = pe.matmul(row_bank[0][0:LOW, 0:T], w_x[:, c, :], inner[:, c, :], start=c == 0, stop=c == IC - 1)
                last.then_inc(row_done[0], 1)

            def deltas(g):
                pe.wait_ge(row_read[0], use_of_low(g) + 1)
                for m in range(IC):
                    bank = front(g, 10 + m)
                    pe.matmul(bank[:, 0:T], w_dt[:, m * 128:(m + 1) * 128], low[0:R, :],
                              start=True, stop=True).then_inc(front_done[m % 2], 1)

            def spread(g, k, n):
                reuse(pe, row_read[k], use_of_row(g, k, n))
                pe.matmul(row_bank[k][:, 0:T], own_row[:, k * N + n, :], low_parts[:, :], start=True, stop=True).then_inc(row_done[k], 1)

            def add_state(g, n):
                pe.wait_ge(row_read[1], use_of_row(g, 1, n) + 1)
                if n == 0:
                    reuse(pe, skipped, g)
                for c in range(IC):
                    last = pe.matmul(y_bank[c][:, 0:T], keep.ident[:, :], read_out[:, n % 2, c, :], start=n == 0, stop=n == N - 1)
                last.then_inc(summed, 1)

            def group(g, final=False):
                pe.wait_ge(stacked, 3 * (g + 1))
                for n in range(N):
                    spread(g, 0, n)
                    spread(g, 1, n)
                    if n >= 1:
                        add_state(g, n - 1)
                    if n == 0:
                        project_in(g, 2 * Z, range(IC, 2 * IC))
                    if n == 1 and not final:
                        turn_rows(g + 1)
                    if n == 2 and not final:
                        project_in(g + 1, 2, range(IC))
                    if n == 6 and not final:
                        pointwise(g + 1)
                if not final:
                    low_rank(g + 1)
                    deltas(g + 1)
                add_state(g, N - 1)
                pe.wait_ge(gated, g + 1)
                for b in range(G):
                    reuse(pe, row_read[b % 2], use_of_out(g, b, final))
                    for c in range(IC):
                        last = pe.matmul(row_bank[b % 2][0:S, 0:D], gated_y[:, c, b * S:(b + 1) * S], w_out[:, c, :],
                                         start=c == 0, stop=c == IC - 1)
                    last.then_inc(row_done[b % 2], 1)

            pe.wait_ge(loaded, LOADED)
            pe.wait_ge(setup, 3)
            turn_rows(0)
            project_in(0, 2, range(IC))
            pointwise(0)
            low_rank(0)
            deltas(0)
            all_groups(pe, group)

        @block.scalar
        def _(act):
            def front(g, u):
                act.wait_ge(front_done[u % 2], FRONT * g + u // 2 + 1)
                return front_bank[u % 2]

            def read_rows(g):
                if not (isinstance(g, int) and g == 0):
                    for k in range(2):
                        act.wait_ge(front_done[k], FRONT * g)
                for c in range(DC):
                    act.activation(normed_t[:, c, :], front(g, c)[:, 0:T], ACT.Copy).then_inc(front_read[c % 2], 1)

            def read_inner_half(g):
                reuse(act, mixed_ready, STEPS * g)
                for m in range(IC):
                    act.activation(padded[:, m, :, TAPS - 1:], front(g, 2 + m)[:, 0:T].rearrange("p (b s) -> p b s", b=G),
                                   ACT.Copy).then_inc(front_read[m % 2], 1)

            def read_gates(g):
                reuse(act, gated, g)
                for m in range(IC):
                    act.activation(gates[:, m, :], front(g, 2 * Z + m)[:, 0:T], ACT.Silu).then_inc(front_read[m % 2], 1)

            def read_inner(g):
                reuse(act, skip_ready, g)
                reuse(act, delta_inner_ready, g)
                for m in range(IC):
                    act.activation(inner[:, m, :], front(g, 6 + m)[:, 0:T], ACT.Silu,
                                   bias=conv_bias[:, m:m + 1]).then_inc(front_read[m % 2], 1)

            def skip(g):
                reuse(act, gated, g)
                for c in range(IC):
                    last = act.activation(skip_term[:, c, :], inner[:, c, :], ACT.Copy, scale=skip_w[:, c:c + 1])
                last.then_inc(skip_ready, 1)

            def read_low(g):
                act.wait_ge(row_done[0], use_of_low(g) + 1)
                reuse(act, split, 5 * g)
                act.activation(low[:, :], row_bank[0][0:LOW, 0:T], ACT.Copy).then_inc(row_read[0], 1)

            def stack_parts(g):
                for k in range(2):
                    reuse(act, row_done[k], use_of_row(g - 1, k, N))
                for k, (part, made) in enumerate(((part1, 1), (part2, 3), (rest2, 4))):
                    act.wait_ge(split, 5 * g + made)
                    act.activation(low_parts[k * LOW:(k + 1) * LOW, :], part[:, :], ACT.Copy).then_inc(stacked, 1)

            def softplus(g):
                reuse(act, delta_ready, g)
                for m in range(IC):
                    bank = front(g, 10 + m)
                    act.wait_ge(relu_ready, IC * g + m + 1)
                    act.activation(soft[:, m, :], bank[:, 0:T], ACT.Abs, bias=b_dt[:, m:m + 1]).then_inc(front_read[m % 2], 1)
                for k in range(2):
                    act.wait_ge(front_read[k], FRONT * g + Z)
                act.activation(flat(soft[:, :, :]), flat(soft[:, :, :]), ACT.Exp, scale=-1.0).then_inc(abs_ready, 1)
                act.wait_ge(abs_ready, g + 1)
                act.activation(flat(soft[:, :, :]), flat(soft[:, :, :]), ACT.Ln, bias=keep.one[:, :]).then_inc(log_ready, 1)

            def decays(g, n):
                if n == 0:
                    act.wait_ge(negated, 1)
                    act.wait_ge(delta_ready, g + 1)
                reuse(act, state_ready, N * g + n - 1)
                for c in range(IC):
                    last = act.activation(decay[:, n % 2, c, :], delta[:, c, :], ACT.Exp, scale=decay_rate[:, c, n:n + 1])
                last.then_inc(decay_ready, 1)

            def group(g, final=False):
                decays(g, 0)
                decays(g, 1)
                skip(g)
                for n in range(N):
                    if n == 0:
                        read_gates(g)
                    if n == 1 and not final:
                        read_rows(g + 1)
                    if n == 2 and not final:
                        read_inner_half(g + 1)
                    if n + 2 < N:
                        decays(g, n + 2)
                if not final:
                    read_inner(g + 1)
                    read_low(g + 1)
                    stack_parts(g + 1)
                    softplus(g + 1)

            act.wait_ge(loaded, LOADED)
            act.activation(own_row[:, :, :], own_row_f32[:, :, :], ACT.Copy).then_inc(setup, 1)
            act.activation(decay_rate[:, :, :], a_log[:, :, :], ACT.Exp).then_inc(setup, 1)
            read_rows(0)
            read_inner_half(0)
            read_inner(0)
            read_low(0)
            stack_parts(0)
            softplus(0)
            all_groups(act, group)

        @block.vector
        def _(dve):
            def rows(g):
                for k in range(2):
                    reuse(dve, front_done[k], FRONT * (g - 1) + 1)
                for b in range(G):
                    normalise(dve, keep, G * g + b, normed[:, b, :]).then_inc(normed_ready, 1)

            def split_low(g):
                reuse(dve, stacked, 3 * g)
                dve.wait_ge(row_read[0], use_of_low(g) + 1)
                dve.tensor_copy(part1[:, :], low[:, :]).then_inc(split, 1)
                dve.wait_ge(split, 5 * g + 1)
                dve.tensor_tensor(rest1[:, :], low[:, :], part1[:, :], ALU.subtract).then_inc(split, 1)
                dve.wait_ge(split, 5 * g + 2)
                dve.tensor_copy(part2[:, :], rest1[:, :]).then_inc(split, 1)
                dve.wait_ge(split, 5 * g + 3)
                dve.tensor_tensor(rest2[:, :], rest1[:, :], part2[:, :], ALU.subtract).then_inc(split, 2)

            def relu(g):
                reuse(dve, decay_ready, N * g)
                for m in range(IC):
                    dve.wait_ge(front_done[m % 2], FRONT * g + 5 + m // 2 + 1)
                    dve.tensor_scalar(delta[:, m, :], front_bank[m % 2][:, 0:T], b_dt[:, m:m + 1], 0.0, ALU.add, ALU.max).then_inc(relu_ready, 1)

            def make_delta(g):
                dve.wait_ge(log_ready, g + 1)
                dve.wait_ge(relu_ready, IC * (g + 1))
                dve.tensor_tensor(flat(delta[:, :, :]), flat(delta[:, :, :]), flat(soft[:, :, :]), ALU.add).then_inc(delta_ready, 1)
                dve.wait_ge(delta_ready, g + 1)
                dve.tensor_tensor(flat(delta_inner[:, :, :]), flat(delta[:, :, :]), flat(inner[:, :, :]), ALU.mult).then_inc(delta_inner_ready, 1)

            def state_of(g, n):
                k = N * g + n
                dve.wait_ge(decay_ready, k + 1)
                dve.memset(decay[:, n % 2, :, :].rearrange("p c (b s) -> p c b s", b=G)[:, :, :, 0], 0.0).then_inc(cut_ready, 1)
                dve.wait_ge(row_done[0], use_of_row(g, 0, n) + 1)
                if n == 0:
                    dve.wait_ge(delta_inner_ready, g + 1)
                dve.tensor_tensor(drive[:, :, :], delta_inner[:, :, :],
                                  row_bank[0][:, 0:T].unsqueeze(1).broadcast_to([128, IC, T]), ALU.mult).then_inc(row_read[0], 1)
                dve.wait_ge(cut_ready, k + 1)
                dve.wait_ge(row_read[0], use_of_row(g, 0, n) + 1)
                dve.tensor_tensor_scan(flat(state[:, :, :]), flat(decay[:, n % 2, :, :]), flat(drive[:, :, :]), 0.0,
                                       ALU.mult, ALU.add).then_inc(state_ready, 1)
                dve.wait_ge(state_ready, k + 1)
                dve.wait_ge(row_done[1], use_of_row(g, 1, n) + 1)
                reuse(dve, summed, k - 1)
                dve.tensor_tensor(read_out[:, n % 2, :, :], state[:, :, :],
                                  row_bank[1][:, 0:T].unsqueeze(1).broadcast_to([128, IC, T]), ALU.mult).then_inc(row_read[1], 1)

            def finish(g, final):
                dve.wait_ge(summed, N * (g + 1))
                dve.wait_ge(skip_ready, g + 1)
                for c in range(IC):
                    last = dve.tensor_tensor(skip_term[:, c, :], skip_term[:, c, :], y_bank[c][:, 0:T], ALU.add)
                last.then_inc(skipped, 1)
                dve.wait_ge(skipped, g + 1)
                dve.tensor_tensor(flat(gated_y[:, :, :]), flat(skip_term[:, :, :]), flat(gates[:, :, :]), ALU.mult).then_inc(gated, 1)
                if not final:
                    make_delta(g + 1)
                for b in range(G):
                    t = G * g + b
                    dve.wait_ge(row_done[b % 2], use_of_out(g, b, final) + 1)
                    dve.tensor_tensor(row(keep.x, t), row_bank[b % 2][0:S, 0:D], row(keep.x, t), ALU.add).then_inc(row_read[b % 2], 1)
                for b in range(G):
                    t = G * g + b
                    dve.wait_ge(row_read[b % 2], use_of_out(g, b, final) + 1)
                    dve.bn_stats(row(keep.stats, t), row(keep.x, t))

            def group(g, final=False):
                if not final:
                    rows(g + 1)
                for n in range(N):
                    state_of(g, n)
                if not final:
                    split_low(g + 1)
                    relu(g + 1)
                finish(g, final)

            dve.memset(padded[:, :, :, 0:TAPS - 1], 0.0).then_inc(setup, 1)
            rows(0)
            dve.wait_ge(setup, 3)
            dve.tensor_scalar(decay_rate[:, :, :], decay_rate[:, :, :], -1.0, None, ALU.mult).then_inc(negated, 1)
            split_low(0)
            relu(0)
            make_delta(0)
            all_groups(dve, group)


def cross_attention(nc, keep, name, ctx_t, w_q, w_k, w_v, w_o, b_q, b_k, b_v, b_o, head_rows, mask, masked_t, key_mask):
    replaced = mask is not None
    USES = 7 if replaced else 6
    VW = DK + 1
    HC = 128 // DK
    with ExitStack() as stack:
        scope = Scope(nc, stack, name)
        sb, psum, sem = scope.sb, scope.psum, scope.sem
        wq, wk, wv, wo = (sb(n, [128, DC, D]) for n in ("wq", "wk", "wv", "wo"))
        bq, bk = sb("bq", [128, DC]), sb("bk", [128, DC])
        bv, bo = sb("bv", [KP, D]), sb("bo", [1, D])
        ones = sb("ones", [1, S])
        own_head = sb("own_head", [128, HC])
        plain_queries = sb("plain_queries", [128, DC, S])
        context = [sb(f"context{n}", [128, DC, SK]) for n in range(2)]
        normed = sb("normed", [S, D])
        normed_t = sb("normed_t", [128, DC, S])
        queries = [sb(f"queries{n}", [128, HC, DC, S]) for n in range(2)]
        keys = [sb(f"keys{n}", [128, DC, SK]) for n in range(2)]
        values = [sb(f"values{n}", [KP, KC, H, VW]) for n in range(2)]
        scores = sb("scores", [S, 4, SK])
        row_max = sb("row_max", [S, 4])
        negmax = [sb(f"negmax{n}", [S, H]) for n in range(2)]
        floor = sb("floor", [S, 1])
        probs = sb("probs", [S, 2, SK])
        probs_t = sb("probs_t", [KP, 2, KC, S])
        heads_sum = sb("heads_sum", [S, H, VW])
        inverse = sb("inverse", [S, H])
        heads_out = sb("heads_out", [S, H, DK])
        heads_t = sb("heads_t", [128, DC, S])
        if replaced:
            mask_raw = sb("mask_raw", [S, SK], mybir.dt.int32)
            masked_raw = sb("masked_raw", [KP, KC, S], mybir.dt.int32)
            masked = sb("masked", [S, SK])
            masked_on_keys = sb("masked_on_keys", [KP, KC, S])
            added = [sb("added", [S, SK])] * 2
            any_masked = sb("any_masked", [S, 1])
            masked_values = [sb(f"masked_values{n}", [S, H, VW]) for n in range(2)]
            masked_exp = sb("masked_exp", [S, H])
            masked_part = sb("masked_part", [S, H, VW])
        else:
            mask_raw = sb("mask_raw", [S, B, SK], mybir.dt.uint8)
            key_row = sb("key_row", [S, 2, SK])
            added = [sb(f"added{n}", [S, SK]) for n in range(2)]
        score_bank = [psum(f"score_bank{n}", [128, 512]) for n in range(2)]
        turn_bank = [psum(f"turn_bank{n}", [128, 512]) for n in range(2)]
        proj_bank = [psum(f"proj_bank{n}", [128, 512]) for n in range(2)]
        heads_bank = psum("heads_bank", [128, 512])
        out_bank = psum("out_bank", [128, 512])
        heads_psum = heads_bank[0:S, 0:H * VW].rearrange("p (h v) -> p h v", h=H)
        heads_t_psum = out_bank[:, 0:DC * S].rearrange("p (c s) -> p c s", c=DC)
        out_psum = out_bank[0:S, 256:256 + D]

        weights_in = sem("weights_in")
        context_in = [sem(f"context_in{n}") for n in range(2)]
        constants = sem("constants")
        masks = sem("masks")
        key_row_ready = sem("key_row_ready")
        key_mask_started = sem("key_mask_started")
        key_mask_added = sem("key_mask_added")
        normed_ready = sem("normed_ready")
        proj_done = [sem(f"proj_done{n}") for n in range(2)]
        proj_read = [sem(f"proj_read{n}") for n in range(2)]
        scores_done = sem("scores_done")
        max_started = sem("max_started")
        max_ready = sem("max_ready")
        negmax_ready = sem("negmax_ready")
        queries_ready = sem("queries_ready")
        probs_ready = sem("probs_ready")
        turned = sem("turned")
        turned_read = [sem(f"turned_read{n}") for n in range(2)]
        head_summed = sem("head_summed")
        masked_exp_ready = sem("masked_exp_ready")
        masked_part_ready = sem("masked_part_ready")
        heads_read = sem("heads_read")
        inverse_ready = sem("inverse_ready")
        heads_out_ready = sem("heads_out_ready")
        heads_turned = sem("heads_turned")
        heads_t_ready = sem("heads_t_ready")
        out_done = sem("out_done")
        x_ready = sem("x_ready")

        N_WEIGHTS = 16 * (4 + 3 * (b_q is not None) + (b_o is not None) + 1 + (2 if replaced else 1))

        def use(i, s, u):
            n = USES * s + u
            return n % 2, USES * i + n // 2

        block = stack.enter_context(nc.Block())

        @block.sync
        def _(sp):
            for tile, w in ((wq, w_q), (wk, w_k), (wv, w_v), (wo, w_o)):
                sp.dma_start(tile[:, :, :], w.rearrange("(c p) n -> p c n", p=128)).then_inc(weights_in, 16)
            if b_q is not None:
                sp.dma_start(bq[:, :], b_q).then_inc(weights_in, 16)
                sp.dma_start(bk[:, :], b_k).then_inc(weights_in, 16)
                sp.dma_start(bv[:, :], b_v.rearrange("(o n) -> o n", o=1).broadcast_to([KP, D])).then_inc(weights_in, 16)
            if b_o is not None:
                sp.dma_start(bo[:, :], b_o.rearrange("(o n) -> o n", o=1)).then_inc(weights_in, 16)
            sp.dma_start(own_head[:, :], head_rows).then_inc(weights_in, 16)
            if replaced:
                sp.dma_start(mask_raw[:, :], mask).then_inc(weights_in, 16)
                sp.dma_start(masked_raw[:, :, :], masked_t.rearrange("(c p) s -> p c s", c=KC)).then_inc(weights_in, 16)
            else:
                sp.dma_start(mask_raw[:, :, :].rearrange("p b k -> p (b k)"),
                             key_mask.rearrange("(o b) k -> o (b k)", o=1).broadcast_to([S, B * SK])).then_inc(weights_in, 16)

            def context_load(t, s):
                sp.dma_start(context[s][:, :, :], ctx_t[t].rearrange("(c p) k -> p c k", p=128)).then_inc(context_in[s], 16)

            context_load(0, 0)
            context_load(1, 1)
            with sp.Fori(1, B // 2) as i:
                for s in range(2):
                    k, before = use(i - 1, s, 5)
                    sp.wait_ge(proj_done[k], before + 1)
                    sp.dma_start(context[s][:, :, :],
                                 ctx_t[bass.ds(2 * i + s, 1)].rearrange("o (c p) k -> p (o c) k", p=128)
                                 ).then_inc(context_in[s], 16)

        @block.gpsimd
        def _(pool):
            pool.wait_ge(weights_in, N_WEIGHTS)
            if replaced:
                pool.tensor_scalar(masked[:, :], mask_raw[:, :], 0.0, None, ALU.is_equal).then_inc(masks, 1)
                pool.tensor_scalar(masked_on_keys[:, :, :], masked_raw[:, :, :], 0.0, None, ALU.is_equal).then_inc(masks, 1)
                pool.wait_ge(masks, 1)
                pool.tensor_scalar(added[0][:, :], masked[:, :], -BIG, None, ALU.mult).then_inc(masks, 1)
            if not replaced:
                def add_key_mask(i, s):
                    reuse(pool, key_mask_added, 2 * i + s - 1)
                    reuse(pool, max_ready, H * (2 * i + s - 1))
                    pool.tensor_copy(key_row[:, s, :], mask_raw[:, bass.ds(2 * i + s, 1), :].rearrange("p o k -> p (o k)")
                                     ).then_inc(key_row_ready, 1)
                    pool.wait_ge(key_row_ready, 2 * i + s + 1)
                    pool.sem_inc(key_mask_started, 1)
                    pool.tensor_scalar(added[s][:, :], key_row[:, s, :], -1.0, 1e10, ALU.add, ALU.mult).then_inc(key_mask_added, 1)

            def spread_queries(i, s):
                k, before = use(i, s, 3)
                pool.wait_ge(proj_read[k], before + 1)
                reuse(pool, scores_done, H * (2 * i + s - 1))
                for m in range(DC):
                    last = pool.tensor_tensor(queries[s][:, :, m, :], plain_queries[:, m, :].unsqueeze(1).broadcast_to([128, HC, S]),
                                              own_head[:, :].unsqueeze(2).broadcast_to([128, HC, S]), ALU.mult)
                last.then_inc(queries_ready, 1)

            def batch(i, s):
                if not replaced:
                    add_key_mask(i, s)
                spread_queries(i, s)

            batch(0, 0)
            batch(0, 1)
            with pool.Fori(1, B // 2) as i:
                batch(i, 0)
                batch(i, 1)

        @block.tensor
        def _(pe):
            def project(i, s, u):
                k, before = use(i, s, u)
                bank = proj_bank[k]
                pe.wait_ge(proj_read[k], before)
                if u == 0:
                    pe.wait_ge(normed_ready, 2 * i + s + 1)
                    for c in range(DC):
                        last = pe.transpose(bank[:, c * S:(c + 1) * S], normed[:, c * 128:(c + 1) * 128],
                                            keep.ident[0:S, 0:S])
                elif u in (1, 2):
                    if u == 1:
                        pe.wait_ge(context_in[s], 16 * (i + 1))
                    m = u - 1
                    for c in range(DC):
                        last = pe.matmul(bank[:, 0:SK], wk[:, c, m * 128:(m + 1) * 128], context[s][:, c, :],
                                         start=c == 0, stop=c == DC - 1)
                elif u == 3:
                    k0, b0 = use(i, s, 0)
                    pe.wait_ge(proj_read[k0], b0 + 1)
                    for m in range(DC):
                        for c in range(DC):
                            last = pe.matmul(bank[:, m * S:(m + 1) * S], wq[:, c, m * 128:(m + 1) * 128],
                                             normed_t[:, c, :], start=c == 0, stop=c == DC - 1)
                elif u in (4, 5):
                    for j, kc in enumerate((0, 1) if u == 4 else (2,)):
                        for c in range(DC):
                            last = pe.matmul(bank[0:KP, j * D:(j + 1) * D], context[s][:, c, kc * KP:(kc + 1) * KP],
                                             wv[:, c, :], start=c == 0, stop=c == DC - 1)
                    last.then_inc(proj_done[k], 1)
                    return
                else:
                    for uv in (4, 5):
                        kv, bv_ = use(i, s, uv)
                        pe.wait_ge(proj_read[kv], bv_ + 1)
                    for kc in range(KC):
                        last = pe.matmul(bank[0:S, 0:H * VW], masked_on_keys[:, kc, :],
                                         values[s][:, kc, :, :].rearrange("p h v -> p (h v)"),
                                         start=kc == 0, stop=kc == KC - 1)
                last.then_inc(proj_done[k], 1)

            def score(i, s, h):
                m = h // HC
                if h == 0:
                    for u in (1, 2):
                        k, before = use(i, s, u)
                        pe.wait_ge(proj_read[k], before + 1)
                    pe.wait_ge(queries_ready, 2 * i + s + 1)
                n = H * (2 * i + s) + h
                if not (isinstance(i, int) and i == 0 and s == 0 and h < 2):
                    pe.wait_ge(max_ready, n - 1)
                pe.matmul(score_bank[h % 2][0:S, 0:SK], queries[s][:, h % HC, m, :],
                          keys[s][:, m, :], start=True, stop=True).then_inc(scores_done, 1)

            def turn(i, s, h):
                n = H * (2 * i + s) + h
                pe.wait_ge(probs_ready, n + 1)
                pe.wait_ge(turned_read[h % 2], 8 * (2 * i + s) + h // 2)
                for kc in range(KC):
                    last = pe.transpose(turn_bank[h % 2][0:KP, kc * S:(kc + 1) * S],
                                        probs[:, h % 2, kc * KP:(kc + 1) * KP], keep.ident[0:S, 0:S])
                last.then_inc(turned, 1)

            def weigh(i, s, h):
                if h == 0:
                    pe.wait_ge(heads_read, 2 * i + s)
                    for u in (4, 5):
                        k, before = use(i, s, u)
                        pe.wait_ge(proj_read[k], before + 1)
                pe.wait_ge(turned_read[h % 2], 8 * (2 * i + s) + h // 2 + 1)
                for kc in range(KC):
                    last = pe.matmul(heads_psum[:, h, :], probs_t[:, h % 2, kc, :], values[s][:, kc, h, :],
                                     start=kc == 0, stop=kc == KC - 1)
                last.then_inc(head_summed, 1)

            def turn_heads(t):
                pe.wait_ge(heads_out_ready, t)
                pe.wait_ge(x_ready, t - 1)
                for c in range(DC):
                    last = pe.transpose(heads_t_psum[:, c, :],
                                        heads_out[:, 8 * c:8 * c + 8, :].rearrange("p h v -> p (h v)"),
                                        keep.ident[0:S, 0:S])
                last.then_inc(heads_turned, 1)

            def project_out(t):
                pe.wait_ge(heads_t_ready, t)
                if b_o is not None:
                    pe.matmul(out_psum, ones[:, :], bo[:, :], start=True, stop=False)
                for c in range(DC):
                    last = pe.matmul(out_psum, heads_t[:, c, :], wo[:, c, :],
                                     start=c == 0 and b_o is None, stop=c == DC - 1)
                last.then_inc(out_done, 1)

            def batch(i, s, first=False, final=False):
                t = 2 * i + s
                following = (i, 1) if s == 0 else (i + 1, 0)
                for h in range(H):
                    if h + 2 < H:
                        score(i, s, h + 2)
                    elif not final:
                        score(*following, h + 2 - H)
                    turn(i, s, h)
                    if h == 4 and not first:
                        turn_heads(t)
                    if h == 6 and not first:
                        project_out(t)
                    if h % 2 == 1 and h // 2 < USES and not final:
                        project(*following, h // 2)
                    if h >= 2:
                        weigh(i, s, h - 2)
                weigh(i, s, H - 2)
                weigh(i, s, H - 1)

            pe.wait_ge(weights_in, N_WEIGHTS)
            pe.wait_ge(constants, 3)
            if replaced:
                pe.wait_ge(masks, 3)
            for u in range(USES):
                project(0, 0, u)
            score(0, 0, 0)
            score(0, 0, 1)
            batch(0, 0, first=True)
            batch(0, 1)
            with pe.Fori(1, B // 2 - 1) as i:
                batch(i, 0)
                batch(i, 1)
            batch(B // 2 - 1, 0)
            batch(B // 2 - 1, 1, final=True)
            turn_heads(B)
            project_out(B)

        def copy_out_turned(eng, copy, i, s, h):
            n = H * (2 * i + s) + h
            eng.wait_ge(turned, n + 1)
            if not (isinstance(i, int) and i == 0 and s == 0 and h < 2):
                eng.wait_ge(head_summed, n - 1)
            copy(probs_t[:, h % 2, :, :].rearrange("p c s -> p (c s)"),
                 turn_bank[h % 2][0:KP, 0:KC * S]).then_inc(turned_read[h % 2], 1)

        @block.vector
        def _(dve):
            def normalise(i, s):
                t = 2 * i + s
                if not (isinstance(t, int) and t == 0):
                    k, before = use(i, 0, 0) if s else use(i - 1, 1, 0)
                    dve.wait_ge(proj_done[k], before + 1)
                dve.tensor_scalar(normed[:, :], keep.x[:, bass.ds(t, 1), :].rearrange("p o d -> p (o d)"),
                                  keep.moments[:, bass.ds(t, 1), 0], keep.rstd[:, bass.ds(t, 1)],
                                  ALU.subtract, ALU.mult).then_inc(normed_ready, 1)

            def read_projection(i, s, u):
                k, before = use(i, s, u)
                bank = proj_bank[k]
                if u in (4, 5):
                    dve.wait_ge(proj_done[k], before + 1)
                    dve.wait_ge(head_summed, H * (2 * i + s - 1)) if not (isinstance(i, int) and 2 * i + s < 2) else None
                    for j, kc in enumerate((0, 1) if u == 4 else (2,)):
                        out = values[s][:, kc, :, 0:DK]
                        got = bank[0:KP, j * D:(j + 1) * D].rearrange("p (h v) -> p h v", h=H)
                        if b_v is not None:
                            last = dve.tensor_tensor(out, got, bv[:, :].rearrange("p (h v) -> p h v", h=H), ALU.add)
                        else:
                            last = dve.tensor_copy(out, got)
                    last.then_inc(proj_read[k], 1)

            def add_mask_and_max(i, s, h):
                n = H * (2 * i + s) + h
                first = isinstance(i, int) and i == 0 and s == 0
                if h == 0 and not replaced:
                    dve.wait_ge(key_mask_added, 2 * i + s + 1)
                dve.wait_ge(scores_done, n + 1)
                if not (first and h < 4):
                    dve.wait_ge(probs_ready, n - 3)
                dve.sem_inc(max_started, 1)
                dve.tensor_tensor_reduce(scores[:, h % 4, :], score_bank[h % 2][0:S, 0:SK], added[s][:, :], 1.0, -BIG,
                                         ALU.add, ALU.max, row_max[:, h % 4:h % 4 + 1]).then_inc(max_ready, 1)
                dve.wait_ge(max_ready, n + 1)
                dve.tensor_scalar(negmax[s][:, h:h + 1], row_max[:, h % 4:h % 4 + 1], floor[:, :], -1.0,
                                  ALU.max, ALU.mult).then_inc(negmax_ready, 1)

            def sum_heads(t, s):
                dve.wait_ge(head_summed, H * t)
                if replaced:
                    dve.wait_ge(masked_exp_ready, t)
                    dve.tensor_tensor(masked_part[:, :, :], masked_values[s][:, :, :],
                                      masked_exp[:, :].unsqueeze(2).broadcast_to([S, H, VW]), ALU.mult).then_inc(masked_part_ready, 1)
                    dve.wait_ge(masked_part_ready, t)
                    dve.tensor_tensor(heads_sum[:, :, :], heads_psum, masked_part[:, :, :], ALU.add).then_inc(heads_read, 1)
                else:
                    dve.tensor_copy(heads_sum[:, :, :], heads_psum).then_inc(heads_read, 1)
                dve.wait_ge(heads_read, t)
                dve.reciprocal(inverse[:, :], heads_sum[:, :, DK]).then_inc(inverse_ready, 1)

            def normalise_heads(t):
                dve.wait_ge(inverse_ready, t)
                dve.wait_ge(heads_turned, t - 1)
                dve.tensor_tensor(heads_out[:, :, :], heads_sum[:, :, 0:DK],
                                  inverse[:, :].unsqueeze(2).broadcast_to([S, H, DK]), ALU.mult).then_inc(heads_out_ready, 1)

            def update_x(t):
                dve.wait_ge(out_done, t)
                row = keep.x[:, bass.ds(t - 1, 1), :].rearrange("p o d -> p (o d)")
                dve.tensor_tensor(row, out_psum, row, ALU.add).then_inc(x_ready, 1)
                dve.wait_ge(x_ready, t)
                dve.bn_stats(keep.stats[:, bass.ds(t - 1, 1), :].rearrange("p o d -> p (o d)"), row)

            def batch(i, s, first=False, final=False):
                t = 2 * i + s
                following = (i, 1) if s == 0 else (i + 1, 0)
                for h in range(H):
                    if h + 2 < H:
                        add_mask_and_max(i, s, h + 2)
                    elif not final:
                        add_mask_and_max(*following, h + 2 - H)
                    if h % 2 == 1:
                        copy_out_turned(dve, dve.tensor_copy, i, s, h)
                    if h == 0 and not first:
                        sum_heads(t, 1 - s)
                    if h == 0 and not final:
                        normalise(*following)
                    if h == 2 and not first:
                        normalise_heads(t)
                    if h == 6 and not first:
                        update_x(t)
                    if h % 2 == 1 and h // 2 < USES and not final:
                        read_projection(*following, h // 2)

            dve.memset(ones[:, :], 1.0).then_inc(constants, 1)
            for s in range(2):
                dve.memset(values[s][:, :, :, DK:VW], 1.0).then_inc(constants, 1)
            dve.wait_ge(weights_in, N_WEIGHTS)
            if replaced:
                dve.wait_ge(masks, 3)
                dve.reduce_max(any_masked[:, :], masked[:, :], AX_X).then_inc(constants, 1)
                dve.wait_ge(constants, 4)
                dve.tensor_scalar(any_masked[:, :], any_masked[:, :], -1.0, BIG, ALU.add, ALU.mult).then_inc(constants, 1)
                dve.wait_ge(constants, 5)
                dve.tensor_scalar(floor[:, :], any_masked[:, :], -1e-9, None, ALU.add).then_inc(constants, 1)
            else:
                dve.memset(floor[:, :], -BIG).then_inc(constants, 1)
            dve.wait_ge(constants, 6 if replaced else 4)
            normalise(0, 0)
            for u in range(USES):
                read_projection(0, 0, u)
            add_mask_and_max(0, 0, 0)
            add_mask_and_max(0, 0, 1)
            batch(0, 0, first=True)
            batch(0, 1)
            with dve.Fori(1, B // 2 - 1) as i:
                batch(i, 0)
                batch(i, 1)
            batch(B // 2 - 1, 0)
            batch(B // 2 - 1, 1, final=True)
            sum_heads(B, 1)
            normalise_heads(B)
            update_x(B)

        @block.scalar
        def _(act):
            def copy(out, in_):
                return act.activation(out, in_, ACT.Copy)

            def read_projection(i, s, u):
                k, before = use(i, s, u)
                bank = proj_bank[k]
                if u == 0:
                    act.wait_ge(proj_done[k], before + 1)
                    if not (isinstance(i, int) and 2 * i + s == 0):
                        kq, bq_ = use(i, s - 1, 3) if s else use(i - 1, 1, 3)
                        act.wait_ge(proj_done[kq], bq_ + 1)
                    copy(normed_t[:, :, :].rearrange("p c s -> p (c s)"), bank[:, 0:DC * S]).then_inc(proj_read[k], 1)
                if u == 3:
                    act.wait_ge(proj_done[k], before + 1)
                    reuse(act, queries_ready, 2 * i + s)
                    for m in range(DC):
                        out, got = plain_queries[:, m, :], bank[:, m * S:(m + 1) * S]
                        if b_q is not None:
                            last = act.activation(out, got, ACT.Identity, bias=bq[:, m:m + 1])
                        else:
                            last = act.activation(out, got, ACT.Copy)
                    last.then_inc(proj_read[k], 1)
                if u in (1, 2):
                    act.wait_ge(proj_done[k], before + 1)
                    if not (isinstance(i, int) and 2 * i + s < 2):
                        act.wait_ge(scores_done, H * (2 * i + s - 1))
                    if b_k is not None:
                        act.activation(keys[s][:, u - 1, :], bank[:, 0:SK], ACT.Identity,
                                       bias=bk[:, u - 1:u]).then_inc(proj_read[k], 1)
                    else:
                        copy(keys[s][:, u - 1, :], bank[:, 0:SK]).then_inc(proj_read[k], 1)
                if u == 6:
                    act.wait_ge(proj_done[k], before + 1)
                    if not (isinstance(i, int) and 2 * i + s < 2):
                        act.wait_ge(masked_part_ready, 2 * i + s - 1)
                    copy(masked_values[s][:, :, :].rearrange("p h v -> p (h v)"), bank[0:S, 0:H * VW]).then_inc(proj_read[k], 1)

            def exponentials(i, s, h):
                n = H * (2 * i + s) + h
                act.wait_ge(negmax_ready, n + 1)
                if not (isinstance(i, int) and i == 0 and s == 0 and h < 2):
                    act.wait_ge(turned, n - 1)
                act.activation(probs[:, h % 2, :], scores[:, h % 4, :], ACT.Exp,
                               bias=negmax[s][:, h:h + 1]).then_inc(probs_ready, 1)

            def masked_exponentials(t, s):
                if replaced:
                    act.wait_ge(negmax_ready, H * t)
                    act.wait_ge(masked_part_ready, t - 1)
                    act.activation(masked_exp[:, :], negmax[s][:, :], ACT.Exp, bias=keep.masked_score[0:S, :]).then_inc(masked_exp_ready, 1)

            def read_heads(t):
                act.wait_ge(heads_turned, t)
                act.wait_ge(out_done, t - 1)
                copy(heads_t[:, :, :], heads_t_psum).then_inc(heads_t_ready, 1)

            def batch(i, s, first=False, final=False):
                t = 2 * i + s
                following = (i, 1) if s == 0 else (i + 1, 0)
                for h in range(H):
                    if h == 0 and not first:
                        masked_exponentials(t, 1 - s)
                    if h + 2 < H:
                        exponentials(i, s, h + 2)
                    elif not final:
                        exponentials(*following, h + 2 - H)
                    if h % 2 == 0:
                        copy_out_turned(act, copy, i, s, h)
                    if h == 4 and not first:
                        read_heads(t)
                    if h % 2 == 1 and h // 2 < USES and not final:
                        read_projection(*following, h // 2)

            act.wait_ge(weights_in, N_WEIGHTS)
            for u in range(USES):
                read_projection(0, 0, u)
            exponentials(0, 0, 0)
            exponentials(0, 0, 1)
            batch(0, 0, first=True)
            batch(0, 1)
            with act.Fori(1, B // 2 - 1) as i:
                batch(i, 0)
                batch(i, 1)
            batch(B // 2 - 1, 0)
            batch(B // 2 - 1, 1, final=True)
            masked_exponentials(B, 1)
            read_heads(B)


def switch_ffn(nc, keep, name, w):
    E = 8
    CAP = B * S // E
    G = 4
    with ExitStack() as stack:
        scope = Scope(nc, stack, name)
        sb, psum, sem = scope.sb, scope.psum, scope.sem
        gate_w, expert_w, expert_b = sb("gate_w", [128, DC, E]), sb("expert_w", [128, DC, D]), sb("expert_b", [1, D])
        upto, ones, preference = sb("upto", [S, S]), sb("ones", [S, S]), sb("preference", [S, E])
        normed = sb("normed", [S, G, D])
        normed_t = sb("normed_t", [128, G, DC, S])
        expert_out = sb("expert_out", [S, B, D])
        logits = sb("logits", [S, B, E])
        shifted, exps, chosen = sb("shifted", [S, B, E]), sb("exps", [S, B, E]), sb("chosen", [S, B, E])
        kept, before_here = sb("kept", [S, B, E]), sb("before_here", [S, B + 1, E])
        top, total, gate, weight = sb("top", [S, B]), sb("total", [S, B]), sb("gate", [S, B]), sb("weight", [S, B])
        turn_bank = [psum(f"turn_bank{n}", [128, 512]) for n in range(G)]
        rows_bank = [psum(f"rows_bank{n}", [128, 512]) for n in range(G)]

        loaded, ones_ready = sem("loaded"), sem("ones_ready")
        normed_ready, turned, turned_read = sem("normed_ready"), sem("turned"), sem("turned_read")
        rows_done, logits_read, expert_read = sem("rows_done"), sem("logits_read"), sem("expert_read")
        gating = sem("gating")
        exps_ready, places_done = sem("exps_ready"), sem("places_done")
        updated = sem("updated")
        block = stack.enter_context(nc.Block())

        @block.sync
        def _(sp):
            sp.dma_start(gate_w[:, :, :], w["gate"].rearrange("(c p) e -> p c e", p=128)).then_inc(loaded, 16)
            sp.dma_start(expert_w[:, :, :], w["expert"].rearrange("(c p) n -> p c n", p=128)).then_inc(loaded, 16)
            sp.dma_start(expert_b[:, :], w["expert_bias"].rearrange("(o n) -> o n", o=1)).then_inc(loaded, 16)
            sp.dma_start(upto[:, :], w["upto"]).then_inc(loaded, 16)

        @block.tensor
        def _(pe):
            def step(i):
                for s in range(G):
                    t = G * i + s
                    pe.wait_ge(normed_ready, t + 1)
                    reuse(pe, turned_read, t + 1 - G)
                    for c in range(DC):
                        last = pe.transpose(turn_bank[s][:, c * S:(c + 1) * S], normed[:, s, c * 128:(c + 1) * 128],
                                            keep.ident[0:S, 0:S])
                    last.then_inc(turned, 1)
                for s in range(G):
                    t = G * i + s
                    pe.wait_ge(turned_read, t + 1)
                    reuse(pe, logits_read, t + 1 - G)
                    reuse(pe, expert_read, t + 1 - G)
                    for c in range(DC):
                        pe.matmul(rows_bank[s][0:S, 0:E], normed_t[:, s, c, :], gate_w[:, c, :], start=c == 0, stop=c == DC - 1)
                    out = rows_bank[s][0:S, D:2 * D]
                    pe.matmul(out, ones[0:1, :], expert_b[:, :], start=True, stop=False)
                    for c in range(DC):
                        last = pe.matmul(out, normed_t[:, s, c, :], expert_w[:, c, :], start=False, stop=c == DC - 1)
                    last.then_inc(rows_done, 1)

            pe.wait_ge(loaded, 64)
            pe.wait_ge(ones_ready, 1)
            step(0)
            with pe.Fori(1, B // G) as i:
                step(i)
            pe.wait_ge(gating, 13)
            places = rows_bank[0][0:S, 0:B * E]
            pe.wait_ge(logits_read, B)
            pe.wait_ge(expert_read, B)
            pe.matmul(places, upto[:, :], chosen[:, :, :].rearrange("p b e -> p (b e)"), start=True, stop=False)
            pe.matmul(places, ones[:, :], before_here[:, 0:B, :].rearrange("p b e -> p (b e)"),
                      start=False, stop=True).then_inc(places_done, 1)

        @block.scalar
        def _(act):
            def step(i):
                for s in range(G):
                    t = G * i + s
                    act.wait_ge(turned, t + 1)
                    reuse(act, rows_done, t + 1 - G)
                    act.activation(normed_t[:, s, :, :].rearrange("p c s -> p (c s)"), turn_bank[s][:, 0:DC * S],
                                   ACT.Copy).then_inc(turned_read, 1)
                for s in range(G):
                    t = G * i + s
                    act.wait_ge(rows_done, t + 1)
                    act.wait_ge(logits_read, t + 1)
                    act.activation(row(expert_out, t), rows_bank[s][0:S, D:2 * D], ACT.Copy).then_inc(expert_read, 1)

            step(0)
            with act.Fori(1, B // G) as i:
                step(i)
            act.wait_ge(gating, 2)
            act.activation(exps[:, :, :], shifted[:, :, :], ACT.Exp).then_inc(exps_ready, 1)

        @block.vector
        def _(dve):
            def step(i):
                for s in range(G):
                    t = G * i + s
                    reuse(dve, turned, t + 1 - G)
                    normalise(dve, keep, t, normed[:, s, :]).then_inc(normed_ready, 1)
                for s in range(G):
                    t = G * i + s
                    dve.wait_ge(rows_done, t + 1)
                    dve.tensor_copy(row(logits, t), rows_bank[s][0:S, 0:E]).then_inc(logits_read, 1)

            def wide(column):
                return column[:, :].unsqueeze(2).broadcast_to([S, B, E])

            dve.memset(ones[:, :], 1.0).then_inc(ones_ready, 1)
            dve.memset(before_here[:, 0, :], 0.0)
            for e in range(E):
                last = dve.memset(preference[:, e:e + 1], float(E - e))
            last.then_inc(ones_ready, 1)
            step(0)
            with dve.Fori(1, B // G) as i:
                step(i)
            dve.wait_ge(logits_read, B)
            dve.wait_ge(ones_ready, 2)
            dve.reduce_max(top[:, :], logits[:, :, :], AX_X).then_inc(gating, 1)
            dve.wait_ge(gating, 1)
            dve.tensor_tensor(shifted[:, :, :], logits[:, :, :], wide(top), ALU.subtract).then_inc(gating, 1)
            dve.wait_ge(gating, 2)
            dve.scalar_tensor_tensor(kept[:, :, :], shifted[:, :, :], 0.0, preference[:, :].unsqueeze(1).broadcast_to([S, B, E]),
                                     ALU.is_ge, ALU.mult).then_inc(gating, 1)
            dve.wait_ge(gating, 3)
            dve.reduce_max(top[:, :], kept[:, :, :], AX_X).then_inc(gating, 1)
            dve.wait_ge(gating, 4)
            dve.tensor_tensor(chosen[:, :, :], kept[:, :, :], wide(top), ALU.is_equal).then_inc(gating, 1)
            dve.wait_ge(gating, 5)
            for e in range(E):
                dve.tensor_tensor_scan(before_here[:, 1:B + 1, e], ones[:, 0:B], chosen[:, :, e], 0.0,
                                       ALU.mult, ALU.add).then_inc(gating, 1)
            dve.wait_ge(exps_ready, 1)
            dve.reduce_sum(total[:, :], exps[:, :, :], AX_X).then_inc(gating, 1)
            dve.wait_ge(gating, 14)
            dve.reciprocal(gate[:, :], total[:, :]).then_inc(gating, 1)
            dve.wait_ge(places_done, 1)
            dve.scalar_tensor_tensor(kept[:, :, :], rows_bank[0][0:S, 0:B * E].rearrange("p (b e) -> p b e", b=B), float(CAP),
                                     chosen[:, :, :], ALU.is_le, ALU.mult).then_inc(gating, 1)
            dve.wait_ge(gating, 16)
            dve.reduce_sum(total[:, :], kept[:, :, :], AX_X).then_inc(gating, 1)
            dve.wait_ge(gating, 17)
            dve.tensor_tensor(weight[:, :], gate[:, :], total[:, :], ALU.mult).then_inc(gating, 1)
            dve.wait_ge(gating, 18)
            dve.wait_ge(expert_read, B)

            def update(b):
                dve.scalar_tensor_tensor(row(keep.x, b), row(expert_out, b), weight[:, bass.ds(b, 1)], row(keep.x, b),
                                         ALU.mult, ALU.add).then_inc(updated, 1)

            update(0)
            with dve.Fori(1, B) as b:
                update(b)
                dve.wait_ge(updated, b)
                dve.bn_stats(row(keep.stats, b - 1), row(keep.x, b - 1))
            dve.wait_ge(updated, B)
            dve.bn_stats(keep.stats[:, B - 1, :], keep.x[:, B - 1, :])


def agent_attention(nc, keep, name, w):
    G = 4
    with ExitStack() as stack:
        scope = Scope(nc, stack, name)
        sb, psum, sem = scope.sb, scope.psum, scope.sem
        wq, wv = sb("wq", [128, DC, D]), sb("wv", [128, DC, D])
        wk_t, wv_t = sb("wk_t", [128, DC, D]), sb("wv_t", [128, DC, D])
        conv1, agent_w = sb("conv1", [128, DC]), sb("agent_w", [128, DC])
        normed, normed_t = sb("normed", [S, G, D]), sb("normed_t", [128, G, DC, S])
        agent, agents = sb("agent", [S, G]), sb("agents", [S, B])
        token_sum, channel_w = sb("token_sum", [128, DC, B]), sb("channel_w", [128, DC, B])
        key_sum, key_exp, key_probs = sb("key_sum", [B, D]), sb("key_exp", [B, D]), sb("key_probs", [B, D])
        key_probs_t = sb("key_probs_t", [128, DC, B])
        token_scores, token_rows = sb("token_scores", [S, B]), sb("token_rows", [B, S])
        token_exp, token_probs, token_weights = sb("token_exp", [B, S]), sb("token_probs", [B, S]), sb("token_weights", [S, B])
        stat = sb("stat", [B, 8])
        gathered = sb("gathered", [128, G, DC])
        own, own_exp, own_inverse, own_probs = (sb(n, [S, B]) for n in ("own", "own_exp", "own_inverse", "own_probs"))
        bank_a = [psum(f"bank_a{n}", [128, 512]) for n in range(G)]
        bank_b = [psum(f"bank_b{n}", [128, 512]) for n in range(G)]

        loaded = sem("loaded")
        agent_w_done, agent_w_ready = sem("agent_w_done"), sem("agent_w_ready")
        normed_ready, turned, turned_read = sem("normed_ready"), sem("turned"), sem("turned_read")
        agent_done, agent_ready, token_sum_done, token_sum_read = (
            sem(n) for n in ("agent_done", "agent_ready", "token_sum_done", "token_sum_read"))
        scores_done, scores_read = sem("scores_done"), sem("scores_read")
        gather_done, gather_read, value_done, updated = (sem(n) for n in ("gather_done", "gather_read", "value_done", "updated"))
        pe_step, dve_step, act_step, small_step = (sem(n) for n in ("pe_step", "dve_step", "act_step", "small_step"))
        block = stack.enter_context(nc.Block())

        @block.sync
        def _(sp):
            qkv, qkv_t = w["qkv"], w["qkv_t"]
            sp.dma_start(wq[:, :, :], qkv[0:D, :].rearrange("(c p) n -> p c n", p=128)).then_inc(loaded, 16)
            sp.dma_start(wv[:, :, :], qkv[2 * D:3 * D, :].rearrange("(c p) n -> p c n", p=128)).then_inc(loaded, 16)
            sp.dma_start(wk_t[:, :, :], qkv_t[:, D:2 * D].rearrange("(c p) n -> p c n", p=128)).then_inc(loaded, 16)
            sp.dma_start(wv_t[:, :, :], qkv_t[:, 2 * D:3 * D].rearrange("(c p) n -> p c n", p=128)).then_inc(loaded, 16)
            sp.dma_start(conv1[:, :], w["conv1"]).then_inc(loaded, 16)

        @block.tensor
        def _(pe):
            def turn(n, i, s):
                t = n * B + G * i + s
                pe.wait_ge(normed_ready, t + 1)
                reuse(pe, turned_read, t + 1 - G)
                for c in range(DC):
                    last = pe.transpose(bank_a[s][:, c * S:(c + 1) * S], normed[:, s, c * 128:(c + 1) * 128],
                                        keep.ident[0:S, 0:S])
                last.then_inc(turned, 1)

            def first_pass(i):
                for s in range(G):
                    turn(0, i, s)
                for s in range(G):
                    t = G * i + s
                    pe.wait_ge(turned_read, t + 1)
                    reuse(pe, token_sum_read, t + 1 - G)
                    for c in range(DC):
                        last = pe.matmul(bank_b[s][0:S, 0:1], normed_t[:, s, c, :], agent_w[:, c:c + 1], start=c == 0, stop=c == DC - 1)
                    last.then_inc(agent_done, 1)
                for s in range(G):
                    t = G * i + s
                    pe.wait_ge(agent_ready, t + 1)
                    for c in range(DC):
                        last = pe.matmul(bank_b[s][:, 8 + c:9 + c], normed[:, s, c * 128:(c + 1) * 128], agent[:, s:s + 1],
                                         start=True, stop=True)
                    last.then_inc(token_sum_done, 1)

            def second_pass(i):
                for s in range(G):
                    turn(1, i, s)
                for s in range(G):
                    t = G * i + s
                    pe.wait_ge(turned_read, B + t + 1)
                    reuse(pe, scores_read, t + 1 - G)
                    for c in range(DC):
                        last = pe.matmul(bank_b[s][0:S, 0:1], normed_t[:, s, c, :], channel_w[:, c, bass.ds(G * i + s, 1)],
                                         start=c == 0, stop=c == DC - 1)
                    last.then_inc(scores_done, 1)

            def third_pass(i):
                for s in range(G):
                    t = G * i + s
                    pe.wait_ge(normed_ready, 2 * B + t + 1)
                    reuse(pe, gather_read, t + 1 - G)
                    for c in range(DC):
                        last = pe.matmul(bank_a[s][:, c:c + 1], normed[:, s, c * 128:(c + 1) * 128],
                                         token_weights[:, bass.ds(G * i + s, 1)], start=True, stop=True)
                    last.then_inc(gather_done, 1)
                for s in range(G):
                    t = G * i + s
                    pe.wait_ge(gather_read, t + 1)
                    reuse(pe, updated, t + 1 - G)
                    for c in range(DC):
                        last = pe.matmul(bank_b[s][0:S, 0:D], gathered[:, s, c:c + 1].broadcast_to([128, S]), wv_t[:, c, :],
                                         start=c == 0, stop=c == DC - 1)
                    last.then_inc(value_done, 1)

            pe.wait_ge(loaded, 80)
            for m in range(DC):
                for c in range(DC):
                    last = pe.matmul(bank_a[0][:, m:m + 1], wq[:, c, m * 128:(m + 1) * 128], conv1[:, c:c + 1],
                                     start=c == 0, stop=c == DC - 1)
            last.then_inc(agent_w_done, 1)
            pe.wait_ge(agent_w_ready, 1)
            first_pass(0)
            with pe.Fori(1, B // G) as i:
                first_pass(i)

            pe.wait_ge(token_sum_read, B)
            for c in range(DC):
                last = pe.matmul(bank_a[0][0:B, 0:D], token_sum[:, c, :], wk_t[:, c, :], start=c == 0, stop=c == DC - 1)
            last.then_inc(pe_step, 1)
            pe.wait_ge(dve_step, 2)
            for c in range(DC):
                last = pe.transpose(bank_a[1][:, c * B:(c + 1) * B], key_probs[:, c * 128:(c + 1) * 128], keep.ident[0:B, 0:B])
            last.then_inc(pe_step, 1)
            pe.wait_ge(act_step, 2)
            for m in range(DC):
                for c in range(DC):
                    last = pe.matmul(bank_a[2][:, m * B:(m + 1) * B], wv[:, c, m * 128:(m + 1) * 128], key_probs_t[:, c, :],
                                     start=c == 0, stop=c == DC - 1)
            last.then_inc(pe_step, 1)
            pe.wait_ge(act_step, 3)
            second_pass(0)
            with pe.Fori(1, B // G) as i:
                second_pass(i)

            pe.wait_ge(scores_read, B)
            pe.transpose(bank_a[0][0:B, 0:S], token_scores[:, :], keep.ident[0:S, 0:S]).then_inc(pe_step, 1)
            pe.wait_ge(dve_step, 4)
            pe.transpose(bank_a[1][0:S, 0:B], token_probs[:, :], keep.ident[0:B, 0:B]).then_inc(pe_step, 1)
            pe.wait_ge(act_step, 5)
            third_pass(0)
            with pe.Fori(1, B // G) as i:
                third_pass(i)

        @block.scalar
        def _(act):
            def read_turned(n, i, s):
                t = n * B + G * i + s
                act.wait_ge(turned, t + 1)
                if n == 0:
                    reuse(act, agent_done, t + 1 - G)
                else:
                    act.wait_ge(agent_done, B)
                    reuse(act, scores_done, G * i + s + 1 - G)
                act.activation(normed_t[:, s, :, :].rearrange("p c s -> p (c s)"), bank_a[s][:, 0:DC * S],
                               ACT.Copy).then_inc(turned_read, 1)

            def first_pass(i):
                for s in range(G):
                    read_turned(0, i, s)
                for s in range(G):
                    t = G * i + s
                    act.wait_ge(agent_done, t + 1)
                    reuse(act, token_sum_done, t + 1 - G)
                    act.activation(agent[:, s:s + 1], bank_b[s][0:S, 0:1], ACT.Copy, scale=float(D) ** -0.5).then_inc(agent_ready, 1)
                for s in range(G):
                    t = G * i + s
                    act.wait_ge(token_sum_done, t + 1)
                    act.activation(agents[:, bass.ds(t, 1)], agent[:, s:s + 1], ACT.Copy)
                    act.activation(token_sum[:, :, bass.ds(t, 1)].rearrange("p c o -> p (c o)"), bank_b[s][:, 8:8 + DC],
                                   ACT.Copy).then_inc(token_sum_read, 1)

            def second_pass(i):
                for s in range(G):
                    read_turned(1, i, s)
                for s in range(G):
                    t = G * i + s
                    act.wait_ge(scores_done, t + 1)
                    act.activation(token_scores[:, bass.ds(t, 1)], bank_b[s][0:S, 0:1], ACT.Copy).then_inc(scores_read, 1)

            def third_pass(i):
                for s in range(G):
                    t = G * i + s
                    act.wait_ge(gather_done, t + 1)
                    reuse(act, value_done, t + 1 - G)
                    act.activation(gathered[:, s, :], bank_a[s][:, 0:DC], ACT.Copy).then_inc(gather_read, 1)

            act.wait_ge(agent_w_done, 1)
            act.activation(agent_w[:, :], bank_a[0][:, 0:DC], ACT.Copy).then_inc(agent_w_ready, 1)
            first_pass(0)
            with act.Fori(1, B // G) as i:
                first_pass(i)
            act.wait_ge(dve_step, 1)
            act.activation(key_exp[:, :], key_sum[:, :], ACT.Exp, bias=stat[:, 0:1], accum_out=stat[:, 1:2]).then_inc(act_step, 1)
            act.wait_ge(pe_step, 2)
            act.activation(key_probs_t[:, :, :].rearrange("p c b -> p (c b)"), bank_a[1][:, 0:DC * B], ACT.Copy).then_inc(act_step, 1)
            act.wait_ge(pe_step, 3)
            act.activation(channel_w[:, :, :].rearrange("p c b -> p (c b)"), bank_a[2][:, 0:DC * B], ACT.Copy).then_inc(act_step, 1)
            second_pass(0)
            with act.Fori(1, B // G) as i:
                second_pass(i)
            act.wait_ge(dve_step, 3)
            act.activation(token_exp[:, :], token_rows[:, :], ACT.Exp, bias=stat[:, 4:5], accum_out=stat[:, 5:6]).then_inc(act_step, 1)
            act.wait_ge(pe_step, 5)
            act.activation(token_weights[:, :], bank_a[1][0:S, 0:B], ACT.Copy).then_inc(act_step, 1)
            act.wait_ge(dve_step, 5)
            act.activation(own_exp[:, :], own[:, :], ACT.Exp).then_inc(act_step, 1)
            third_pass(0)
            with act.Fori(1, B // G) as i:
                third_pass(i)

        @block.vector
        def _(dve):
            def rows_in(n, i, s):
                t = n * B + G * i + s
                if n == 0:
                    reuse(dve, token_sum_done, t + 1 - G)
                elif n == 1:
                    if isinstance(i, int):
                        dve.wait_ge(token_sum_done, B)
                    reuse(dve, turned, t + 1 - G)
                else:
                    if isinstance(i, int):
                        dve.wait_ge(turned, 2 * B)
                    reuse(dve, gather_done, G * i + s + 1 - G)
                normalise(dve, keep, G * i + s, normed[:, s, :]).then_inc(normed_ready, 1)

            def rows_of(n, i):
                for s in range(G):
                    rows_in(n, i, s)

            def update(i):
                for s in range(G):
                    t = G * i + s
                    dve.wait_ge(value_done, t + 1)
                    dve.scalar_tensor_tensor(row(keep.x, t), bank_b[s][0:S, 0:D], own_probs[:, bass.ds(t, 1)], row(keep.x, t),
                                             ALU.mult, ALU.add).then_inc(updated, 1)
                for s in range(G):
                    t = G * i + s
                    dve.wait_ge(updated, t + 1)
                    dve.bn_stats(row(keep.stats, t), row(keep.x, t))

            rows_of(0, 0)
            with dve.Fori(1, B // G) as i:
                rows_of(0, i)

            def softmax(source, kept, exps, probs, at):
                dve.wait_ge(pe_step, 1 if at == 0 else 4)
                dve.reduce_max(stat[:, at + 2:at + 3], source, AX_X).then_inc(small_step, 1)
                dve.tensor_copy(kept, source).then_inc(small_step, 1)
                dve.wait_ge(small_step, 3 * (at > 0) + 2)
                dve.tensor_scalar(stat[:, at:at + 1], stat[:, at + 2:at + 3], -1.0, None, ALU.mult).then_inc(dve_step, 1)
                dve.wait_ge(act_step, 1 if at == 0 else 4)
                dve.reciprocal(stat[:, at + 3:at + 4], stat[:, at + 1:at + 2]).then_inc(small_step, 1)
                dve.wait_ge(small_step, 3 * (at > 0) + 3)
                dve.tensor_scalar(probs, exps, stat[:, at + 3:at + 4], None, ALU.mult).then_inc(dve_step, 1)

            softmax(bank_a[0][0:B, 0:D], key_sum[:, :], key_exp[:, :], key_probs[:, :], 0)
            rows_of(1, 0)
            with dve.Fori(1, B // G) as i:
                rows_of(1, i)
            softmax(bank_a[0][0:B, 0:S], token_rows[:, :], token_exp[:, :], token_probs[:, :], 4)
            dve.wait_ge(token_sum_read, B)
            dve.tensor_tensor(own[:, :], agents[:, :], agents[:, :], ALU.subtract).then_inc(dve_step, 1)
            dve.wait_ge(act_step, 6)
            dve.reciprocal(own_inverse[:, :], own_exp[:, :]).then_inc(small_step, 1)
            dve.wait_ge(small_step, 7)
            dve.tensor_tensor(own_probs[:, :], own_exp[:, :], own_inverse[:, :], ALU.mult).then_inc(small_step, 1)
            dve.wait_ge(small_step, 8)
            rows_of(2, 0)
            update(0)
            with dve.Fori(1, B // G) as i:
                rows_of(2, i)
                update(i)


def latent_moe(nc, keep, name, w):
    with ExitStack() as stack:
        scope = Scope(nc, stack, name)
        latent_t = scope.sb("latent_t", [128, DC, B, S])
        combine = scope.sb("combine", [S, B, 8])
        latent_attention(nc, keep, name + "a_", w, latent_t, combine)
        experts(nc, keep, name + "e_", w, latent_t, combine)


def latent_attention(nc, keep, name, w, latent_t, combine):
    E = 8
    LAT = H * KPH
    QUADS = H // 4
    VW = KPH + 1
    with ExitStack() as stack:
        scope = Scope(nc, stack, name)
        sb, psum, sem = scope.sb, scope.psum, scope.sem
        wq, wk, wv = (sb(n, [128, DC, LAT]) for n in ("wq", "wk", "wv"))
        wo, router = sb("wo", [LAT, D]), sb("router", [128, DC, E])
        bq, bk, bv, bo = sb("bq", [LAT, 1]), sb("bk", [LAT, 1]), sb("bv", [S, LAT]), sb("bo", [128, DC])
        router_b, ones, preference = sb("router_b", [1, E]), sb("ones", [1, S]), sb("preference", [S, E])
        own_rows = sb("own_rows", [LAT, H])
        plain_keys = sb("plain_keys", [LAT, 2, S])
        normed = sb("normed", [S, 2, D])
        normed_t = sb("normed_t", [128, 2, DC, S])
        queries = sb("queries", [LAT, 2, S])
        keys = sb("keys", [LAT, 2, H, S])
        values = sb("values", [S, 2, H, VW])
        top4 = sb("top4", [S, 2, 4])
        shifted, probs, probs_t = sb("shifted", [S, 2, 4, S]), sb("probs", [S, 2, 4, S]), sb("probs_t", [S, 2, 4, S])
        inverse, heads_out, heads_t = sb("inverse", [S, 2, H]), sb("heads_out", [S, 2, H, KPH]), sb("heads_t", [LAT, 2, S])
        latent = sb("latent", [128, 2, DC, S])
        logits = sb("logits", [S, B, E])
        exps, left, picked, first = (sb(n, [S, B, E]) for n in ("exps", "left", "picked", "first"))
        top, total = sb("top", [S, B]), sb("total", [S, B])
        qkv_bank = [psum(f"qkv_bank{n}", [128, 512]) for n in range(2)]
        score_bank = [psum(f"score_bank{n}", [128, 512]) for n in range(2)]
        turn_bank = [psum(f"turn_bank{n}", [128, 512]) for n in range(2)]
        heads_bank = [psum(f"heads_bank{n}", [128, 512]) for n in range(2)]
        heads_psum = [b[0:S, 0:H * VW].rearrange("p (h v) -> p h v", h=H) for b in heads_bank]
        heads_t_psum = [b[0:LAT, 160:160 + S] for b in heads_bank]
        latent_psum = [b[:, 272:272 + DC * S] for b in heads_bank]
        logits_psum = [b[0:S, 496:496 + E] for b in heads_bank]

        loaded, constants = sem("loaded"), sem("constants")
        normed_ready, turned, turned_read, residual_added = (sem(n) for n in ("normed_ready", "turned", "turned_read", "residual_added"))
        qkv_done, queries_ready, values_ready = (sem(n) for n in ("qkv_done", "queries_ready", "values_ready"))
        keys_ready = sem("keys_ready")
        inverse_ready, heads_out_ready, heads_turned, heads_t_ready = (
            sem(n) for n in ("inverse_ready", "heads_out_ready", "heads_turned", "heads_t_ready"))
        latent_done, latent_ready, latent_kept, logits_done, logits_read = (
            sem(n) for n in ("latent_done", "latent_ready", "latent_kept", "logits_done", "logits_read"))
        scores_done, max_ready, shifted_ready, probs_ready, probs_turned, probs_t_ready, weighed = (
            sem(n) for n in ("scores_done", "max_ready", "shifted_ready", "probs_ready", "probs_turned", "probs_t_ready", "weighed"))
        routing, exps_ready = sem("routing"), sem("exps_ready")
        block = stack.enter_context(nc.Block())
        LOADED = 16 * 11

        @block.sync
        def _(sp):
            for tile, source in ((wq, "m_wq"), (wk, "m_wk"), (wv, "m_wv"), (router, "m_router")):
                sp.dma_start(tile[:, :, :], w[source].rearrange("(c p) n -> p c n", p=128)).then_inc(loaded, 16)
            sp.dma_start(wo[:, :], w["m_wo"][0:LAT, :]).then_inc(loaded, 16)
            for tile, source in ((bq, "m_bq"), (bk, "m_bk"), (bo, "m_bo"), (own_rows, "own_latent_head")):
                sp.dma_start(tile[:, :], w[source]).then_inc(loaded, 16)
            sp.dma_start(bv[:, :], w["m_bv"].rearrange("(o n) -> o n", o=1).broadcast_to([S, LAT])).then_inc(loaded, 16)
            sp.dma_start(router_b[:, :], w["m_router_b"].rearrange("(o n) -> o n", o=1)).then_inc(loaded, 16)

        def all_batches(eng, batch):
            batch(0, 0, first=True)
            batch(0, 1)
            with eng.Fori(1, B // 2 - 1) as i:
                batch(i, 0)
                batch(i, 1)
            batch(B // 2 - 1, 0)
            batch(B // 2 - 1, 1, final=True)

        @block.gpsimd
        def _(pool):
            def spread_keys(t, s):
                pool.wait_ge(queries_ready, t + 1)
                reuse(pool, scores_done, QUADS * (t - 1))
                for j in range(QUADS):
                    heads = slice(4 * j, 4 * j + 4)
                    pool.tensor_tensor(keys[:, s, heads, :], plain_keys[:, s, :].unsqueeze(1).broadcast_to([LAT, 4, S]),
                                       own_rows[:, heads].unsqueeze(2).broadcast_to([LAT, 4, S]), ALU.mult).then_inc(keys_ready, 1)

            def keep_latent(t, s):
                pool.wait_ge(latent_ready, t + 1)
                pool.tensor_copy(latent_t[:, :, bass.ds(t, 1), :].rearrange("p c o s -> p c (o s)"),
                                 latent[:, s, :, :]).then_inc(latent_kept, 1)

            def batch(i, s, first=False, final=False):
                t = 2 * i + s
                if not final:
                    spread_keys(t + 1, 1 - s)
                if not first:
                    keep_latent(t - 1, 1 - s)

            pool.wait_ge(constants, 4)
            spread_keys(0, 0)
            all_batches(pool, batch)
            keep_latent(B - 1, 1)

        @block.tensor
        def _(pe):
            def score(t, s, j):
                n = QUADS * t + j
                if j == 0:
                    pe.wait_ge(queries_ready, t + 1)
                pe.wait_ge(keys_ready, n + 1)
                reuse(pe, shifted_ready, n - 1)
                pe.matmul(score_bank[j % 2][0:S, 0:4 * S], queries[:, s, :],
                          keys[:, s, 4 * j:4 * j + 4, :].rearrange("p r s -> p (r s)"), start=True, stop=True).then_inc(scores_done, 1)

            def turn(t, j):
                n = QUADS * t + j
                pe.wait_ge(probs_ready, n + 1)
                reuse(pe, probs_t_ready, n - 1)
                for r in range(4):
                    last = pe.transpose(turn_bank[j % 2][0:S, r * S:(r + 1) * S], probs[:, j % 2, r, :], keep.ident[0:S, 0:S])
                last.then_inc(probs_turned, 1)

            def weigh(t, s, j):
                n = QUADS * t + j
                if j == 0:
                    pe.wait_ge(values_ready, t + 1)
                    reuse(pe, logits_read, t - 1)
                pe.wait_ge(probs_t_ready, n + 1)
                for r in range(4):
                    last = pe.matmul(heads_psum[s][:, 4 * j + r, :], probs_t[:, j % 2, r, :], values[:, s, 4 * j + r, :],
                                     start=True, stop=True)
                last.then_inc(weighed, 1)

            def turn_rows(t, s):
                pe.wait_ge(normed_ready, t + 1)
                reuse(pe, values_ready, t - 1)
                for c in range(DC):
                    last = pe.transpose(qkv_bank[s][:, c * S:(c + 1) * S], normed[:, s, c * 128:(c + 1) * 128], keep.ident[0:S, 0:S])
                last.then_inc(turned, 1)

            def project(t, s):
                pe.wait_ge(turned_read, t + 1)
                for n, weights in enumerate((wq, wk)):
                    for c in range(DC):
                        pe.matmul(qkv_bank[s][:, n * S:(n + 1) * S], weights[:, c, :], normed_t[:, s, c, :], start=c == 0, stop=c == DC - 1)
                for c in range(DC):
                    last = pe.matmul(qkv_bank[s][0:S, 256:256 + LAT], normed_t[:, s, c, :], wv[:, c, :], start=c == 0, stop=c == DC - 1)
                last.then_inc(qkv_done, 1)

            def turn_heads(t, s):
                pe.wait_ge(heads_out_ready, t + 1)
                pe.transpose(heads_t_psum[s], heads_out[:, s, :, :].rearrange("p h v -> p (h v)"), keep.ident[0:S, 0:S]).then_inc(heads_turned, 1)

            def project_out(t, s):
                pe.wait_ge(heads_t_ready, t + 1)
                for c in range(DC):
                    last = pe.matmul(latent_psum[s][:, c * S:(c + 1) * S], wo[:, c * 128:(c + 1) * 128], heads_t[:, s, :],
                                     start=True, stop=True)
                last.then_inc(latent_done, 1)

            def route(t, s):
                pe.wait_ge(latent_ready, t + 1)
                pe.matmul(logits_psum[s], ones[:, :], router_b[:, :], start=True, stop=False)
                for c in range(DC):
                    last = pe.matmul(logits_psum[s], latent[:, s, c, :], router[:, c, :], start=False, stop=c == DC - 1)
                last.then_inc(logits_done, 1)

            def batch(i, s, first=False, final=False):
                t = 2 * i + s
                for j in range(QUADS):
                    if j + 2 < QUADS:
                        score(t, s, j + 2)
                    elif not final:
                        score(t + 1, 1 - s, j + 2 - QUADS)
                    turn(t, j)
                    if j == 0 and not final:
                        turn_rows(t + 1, 1 - s)
                    if j > 0:
                        weigh(t, s, j - 1)
                    elif not first:
                        weigh(t - 1, 1 - s, QUADS - 1)
                    if j == 0 and not final:
                        project(t + 1, 1 - s)
                    if not first:
                        if j == 1:
                            turn_heads(t - 1, 1 - s)
                        if j == 2:
                            project_out(t - 1, 1 - s)
                        if j == 3:
                            route(t - 1, 1 - s)

            pe.wait_ge(loaded, LOADED)
            pe.wait_ge(constants, 2)
            turn_rows(0, 0)
            project(0, 0)
            score(0, 0, 0)
            score(0, 0, 1)
            all_batches(pe, batch)
            weigh(B - 1, 1, QUADS - 1)
            turn_heads(B - 1, 1)
            project_out(B - 1, 1)
            route(B - 1, 1)

        @block.scalar
        def _(act):
            def exponentials(t, j):
                n = QUADS * t + j
                act.wait_ge(shifted_ready, n + 1)
                reuse(act, probs_turned, n - 1)
                act.activation(probs[:, j % 2, :, :], shifted[:, j % 2, :, :], ACT.Exp).then_inc(probs_ready, 1)

            def read_probs(t, j):
                n = QUADS * t + j
                act.wait_ge(probs_turned, n + 1)
                reuse(act, weighed, n - 1)
                act.activation(probs_t[:, j % 2, :, :].rearrange("p r s -> p (r s)"), turn_bank[j % 2][0:S, 0:4 * S],
                               ACT.Copy).then_inc(probs_t_ready, 1)

            def read_rows(t, s):
                act.wait_ge(turned, t + 1)
                reuse(act, qkv_done, t - 1)
                act.activation(normed_t[:, s, :, :].rearrange("p c s -> p (c s)"), qkv_bank[s][:, 0:DC * S], ACT.Copy).then_inc(turned_read, 1)

            def read_queries_and_keys(t, s):
                act.wait_ge(qkv_done, t + 1)
                reuse(act, scores_done, QUADS * (t - 1))
                reuse(act, keys_ready, QUADS * (t - 1))
                act.activation(plain_keys[:, s, :], qkv_bank[s][:, S:2 * S], ACT.Identity, bias=bk[:, :])
                act.activation(queries[:, s, :], qkv_bank[s][:, 0:S], ACT.Identity, bias=bq[:, :]).then_inc(queries_ready, 1)

            def read_heads(t, s):
                act.wait_ge(heads_turned, t + 1)
                reuse(act, latent_done, t - 1)
                act.activation(heads_t[:, s, :], heads_t_psum[s], ACT.Copy).then_inc(heads_t_ready, 1)

            def read_latent(t, s):
                act.wait_ge(latent_done, t + 1)
                reuse(act, latent_kept, t - 1)
                reuse(act, logits_done, t - 1)
                for c in range(DC):
                    last = act.activation(latent[:, s, c, :], latent_psum[s][:, c * S:(c + 1) * S], ACT.Identity, bias=bo[:, c:c + 1])
                last.then_inc(latent_ready, 1)

            def batch(i, s, first=False, final=False):
                t = 2 * i + s
                for j in range(QUADS):
                    if j + 2 < QUADS:
                        exponentials(t, j + 2)
                    elif not final:
                        exponentials(t + 1, j + 2 - QUADS)
                    read_probs(t, j)
                    if j == 0 and not final:
                        read_rows(t + 1, 1 - s)
                        read_queries_and_keys(t + 1, 1 - s)
                    if j == 1 and not first:
                        read_heads(t - 1, 1 - s)
                    if j == 2 and not first:
                        read_latent(t - 1, 1 - s)

            act.wait_ge(loaded, LOADED)
            read_rows(0, 0)
            read_queries_and_keys(0, 0)
            exponentials(0, 0)
            exponentials(0, 1)
            all_batches(act, batch)
            read_heads(B - 1, 1)
            read_latent(B - 1, 1)
            act.wait_ge(routing, 2)
            act.activation(exps[:, :, :], exps[:, :, :], ACT.Exp).then_inc(exps_ready, 1)

        @block.vector
        def _(dve):
            def shift(t, j):
                n = QUADS * t + j
                bank = score_bank[j % 2][0:S, 0:4 * S].rearrange("p (r s) -> p r s", r=4)
                dve.wait_ge(scores_done, n + 1)
                dve.reduce_max(top4[:, j % 2, :], bank, AX_X).then_inc(max_ready, 1)
                dve.wait_ge(max_ready, n + 1)
                reuse(dve, probs_ready, n - 1)
                dve.tensor_tensor(shifted[:, j % 2, :, :], bank, top4[:, j % 2, :].unsqueeze(2).broadcast_to([S, 4, S]),
                                  ALU.subtract).then_inc(shifted_ready, 1)

            def rows(t, s):
                reuse(dve, turned, t - 1)
                normalise(dve, keep, t, normed[:, s, :]).then_inc(normed_ready, 1)

            def add_residual(t, s):
                dve.wait_ge(normed_ready, t + 1)
                dve.tensor_tensor(row(keep.x, t), row(keep.x, t), normed[:, s, :], ALU.add)

            def read_values(t, s):
                dve.wait_ge(queries_ready, t + 1)
                reuse(dve, weighed, QUADS * (t - 1))
                dve.tensor_tensor(values[:, s, :, 0:KPH], qkv_bank[s][0:S, 256:256 + LAT].rearrange("p (h v) -> p h v", h=H),
                                  bv[:, :].rearrange("p (h v) -> p h v", h=H), ALU.add).then_inc(values_ready, 1)

            def divide_heads(t, s):
                dve.wait_ge(weighed, QUADS * (t + 1))
                dve.reciprocal(inverse[:, s, :], heads_psum[s][:, :, KPH]).then_inc(inverse_ready, 1)
                dve.wait_ge(inverse_ready, t + 1)
                reuse(dve, heads_turned, t - 1)
                dve.tensor_tensor(heads_out[:, s, :, :], heads_psum[s][:, :, 0:KPH],
                                  inverse[:, s, :].unsqueeze(2).broadcast_to([S, H, KPH]), ALU.mult).then_inc(heads_out_ready, 1)

            def read_logits(t, s):
                dve.wait_ge(logits_done, t + 1)
                dve.tensor_copy(row(logits, t), logits_psum[s]).then_inc(logits_read, 1)

            def batch(i, s, first=False, final=False):
                t = 2 * i + s
                for j in range(QUADS):
                    if j == 0 and not final:
                        rows(t + 1, 1 - s)
                    if j + 2 < QUADS:
                        shift(t, j + 2)
                    elif not final:
                        shift(t + 1, j + 2 - QUADS)
                    if j == 0 and not first:
                        divide_heads(t - 1, 1 - s)
                    if j == 0 and not final:
                        add_residual(t + 1, 1 - s)
                        read_values(t + 1, 1 - s)
                    if j == 3 and not first:
                        read_logits(t - 1, 1 - s)

            def wide(column):
                return column[:, :].unsqueeze(2).broadcast_to([S, B, E])

            def pick_best(source, out, steps):
                dve.reduce_max(top[:, :], source[:, :, :], AX_X).then_inc(routing, 1)
                dve.wait_ge(routing, steps + 1)
                dve.tensor_tensor(out[:, :, :], source[:, :, :], wide(top), ALU.is_ge).then_inc(routing, 1)
                dve.wait_ge(routing, steps + 2)
                dve.tensor_tensor(out[:, :, :], out[:, :, :], preference[:, :].unsqueeze(1).broadcast_to([S, B, E]), ALU.mult).then_inc(routing, 1)
                dve.wait_ge(routing, steps + 3)
                dve.reduce_max(top[:, :], out[:, :, :], AX_X).then_inc(routing, 1)
                dve.wait_ge(routing, steps + 4)
                dve.tensor_tensor(out[:, :, :], out[:, :, :], wide(top), ALU.is_equal).then_inc(routing, 1)
                dve.wait_ge(routing, steps + 5)

            dve.memset(ones[:, :], 1.0).then_inc(constants, 1)
            dve.memset(values[:, :, :, KPH:VW], 1.0).then_inc(constants, 1)
            for e in range(E):
                last = dve.memset(preference[:, e:e + 1], float(E - e))
            last.then_inc(constants, 1)
            dve.wait_ge(loaded, LOADED)
            dve.tensor_scalar(own_rows[:, :], own_rows[:, :], float(KPH) ** -0.5, None, ALU.mult).then_inc(constants, 1)
            rows(0, 0)
            add_residual(0, 0)
            read_values(0, 0)
            shift(0, 0)
            shift(0, 1)
            all_batches(dve, batch)
            divide_heads(B - 1, 1)
            read_logits(B - 1, 1)
            dve.wait_ge(logits_read, B)
            dve.reduce_max(top[:, :], logits[:, :, :], AX_X).then_inc(routing, 1)
            dve.wait_ge(routing, 1)
            dve.tensor_tensor(exps[:, :, :], logits[:, :, :], wide(top), ALU.subtract).then_inc(routing, 1)
            dve.wait_ge(exps_ready, 1)
            dve.reduce_sum(total[:, :], exps[:, :, :], AX_X).then_inc(routing, 1)
            dve.wait_ge(routing, 3)
            dve.reciprocal(total[:, :], total[:, :]).then_inc(routing, 1)
            dve.wait_ge(routing, 4)
            dve.tensor_tensor(exps[:, :, :], exps[:, :, :], wide(total), ALU.mult).then_inc(routing, 1)
            dve.wait_ge(routing, 5)
            pick_best(exps, first, 5)
            dve.scalar_tensor_tensor(left[:, :, :], first[:, :, :], -2.0, exps[:, :, :], ALU.mult, ALU.add).then_inc(routing, 1)
            dve.wait_ge(routing, 11)
            pick_best(left, picked, 11)
            dve.tensor_tensor(picked[:, :, :], picked[:, :, :], first[:, :, :], ALU.add).then_inc(routing, 1)
            dve.wait_ge(routing, 17)
            dve.tensor_tensor(picked[:, :, :], picked[:, :, :], exps[:, :, :], ALU.mult).then_inc(routing, 1)
            dve.wait_ge(routing, 18)
            dve.reduce_sum(total[:, :], picked[:, :, :], AX_X).then_inc(routing, 1)
            dve.wait_ge(routing, 19)
            dve.tensor_scalar(total[:, :], total[:, :], 1e-8, None, ALU.add).then_inc(routing, 1)
            dve.wait_ge(routing, 20)
            dve.reciprocal(total[:, :], total[:, :]).then_inc(routing, 1)
            dve.wait_ge(routing, 21)
            dve.tensor_tensor(picked[:, :, :], picked[:, :, :], wide(total), ALU.mult).then_inc(routing, 1)
            dve.wait_ge(routing, 22)
            dve.tensor_scalar(combine[:, :, :], picked[:, :, :], 0.3, None, ALU.mult)


def experts(nc, keep, name, w, latent_t, combine):
    E, G = 8, 4
    GROUPS = B // G
    T = G * S
    F = 512
    FC = F // 128
    with ExitStack() as stack:
        scope = Scope(nc, stack, name)
        sb, psum, sem = scope.sb, scope.psum, scope.sem
        w1, w2 = sb("w1", [128, E, DC, F]), sb("w2", [128, E, FC, D])
        b1, b2 = sb("b1", [128, E, FC]), sb("b2", [E, D])
        hidden = sb("hidden", [128, 2, FC, T])
        combine_here, combine_t = sb("combine_here", [S, G, E]), sb("combine_t", [E, G, S])
        hidden_bank = [psum(f"hidden_bank{n}", [128, 512]) for n in range(FC)]
        out_bank = [psum(f"out_bank{n}", [128, 512]) for n in range(G)]
        small_loaded = sem("small_loaded")
        expert_loaded = [sem(f"expert_loaded{e}") for e in range(E)]
        here_ready, combine_turned, combine_t_ready = sem("here_ready"), sem("combine_turned"), sem("combine_t_ready")
        hidden_done, hidden_ready = sem("hidden_done"), sem("hidden_ready")
        out_done = [sem(f"out_done{n}") for n in range(G)]
        out_read = [sem(f"out_read{n}") for n in range(G)]
        block = stack.enter_context(nc.Block())
        USES = E + 1

        @block.sync
        def _(sp):
            sp.dma_start(b1[:, :, :], w["m_b1"]).then_inc(small_loaded, 16)
            sp.dma_start(b2[:, :], w["m_b2"]).then_inc(small_loaded, 16)
            for e in range(E):
                sp.dma_start(w1[:, e, :, :], w["m_w1"][e].rearrange("(c p) n -> p c n", p=128)).then_inc(expert_loaded[e], 16)
                sp.dma_start(w2[:, e, :, :], w["m_w2"][e].rearrange("(c p) n -> p c n", p=128)).then_inc(expert_loaded[e], 16)

        @block.tensor
        def _(pe):
            def hide(g, e):
                if isinstance(g, int):
                    pe.wait_ge(expert_loaded[e], 32)
                for m in range(FC):
                    n = FC * (E * g + e) + m
                    reuse(pe, hidden_ready, n + 1 - FC)
                    for c in range(DC):
                        last = pe.matmul(hidden_bank[m][:, 0:T], w1[:, e, c, m * 128:(m + 1) * 128],
                                         latent_t[:, c, bass.ds(G * g, G), :].rearrange("p b s -> p (b s)"),
                                         start=c == 0, stop=c == DC - 1)
                    last.then_inc(hidden_done, 1)

            def unhide(g, e):
                for m in range(FC):
                    pe.wait_ge(hidden_ready, FC * (E * g + e) + m + 1)
                for b in range(G):
                    reuse(pe, out_read[b], USES * g + 1 + e)
                    for m in range(FC):
                        last = pe.matmul(out_bank[b][0:S, 0:D], hidden[:, e % 2, m, b * S:(b + 1) * S], w2[:, e, m, :],
                                         start=m == 0, stop=m == FC - 1)
                    last.then_inc(out_done[b], 1)

            def group(g):
                hide(g, 0)
                pe.wait_ge(here_ready, g + 1)
                for b in range(G):
                    reuse(pe, out_read[b], USES * g)
                    last = pe.transpose(out_bank[b][0:E, D:D + S], combine_here[:, b, :], keep.ident[0:S, 0:S])
                last.then_inc(combine_turned, 1)
                pe.wait_ge(combine_t_ready, g + 1)
                for b in range(G):
                    pe.matmul(out_bank[b][0:S, 0:D], combine_t[:, b, :], b2[:, :], start=True, stop=True).then_inc(out_done[b], 1)
                for e in range(E):
                    if e + 1 < E:
                        hide(g, e + 1)
                    unhide(g, e)

            pe.wait_ge(small_loaded, 32)
            group(0)
            with pe.Fori(1, GROUPS) as g:
                group(g)

        @block.scalar
        def _(act):
            def gelu(g, e):
                for m in range(FC):
                    n = FC * (E * g + e) + m
                    act.wait_ge(hidden_done, n + 1)
                    if e >= 2:
                        act.wait_ge(out_done[G - 1], USES * g + e)
                    else:
                        reuse(act, out_done[G - 1], 0 if isinstance(g, int) and g == 0 else USES * g - 1 + e)
                    act.activation(hidden[:, e % 2, m, :], hidden_bank[m][:, 0:T], ACT.Gelu, bias=b1[:, e, m:m + 1]).then_inc(hidden_ready, 1)

            def group(g):
                gelu(g, 0)
                act.wait_ge(combine_turned, g + 1)
                for b in range(G):
                    last = act.activation(combine_t[:, b, :], out_bank[b][0:E, D:D + S], ACT.Copy)
                last.then_inc(combine_t_ready, 1)
                for e in range(1, E):
                    gelu(g, e)

            act.wait_ge(small_loaded, 32)
            group(0)
            with act.Fori(1, GROUPS) as g:
                group(g)

        @block.vector
        def _(dve):
            def group(g):
                reuse(dve, combine_turned, g)
                for b in range(G):
                    reuse(dve, out_read[b], USES * g)
                dve.tensor_copy(combine_here[:, :, :], combine[:, bass.ds(G * g, G), :]).then_inc(here_ready, 1)
                for use in range(USES):
                    for b in range(G):
                        x_row = row(keep.x, G * g + b)
                        out = out_bank[b][0:S, 0:D]
                        dve.wait_ge(out_done[b], USES * g + use + 1)
                        reuse(dve, out_read[b], USES * g + use)
                        if use == 0:
                            dve.tensor_tensor(x_row, out, x_row, ALU.add).then_inc(out_read[b], 1)
                        else:
                            dve.scalar_tensor_tensor(x_row, out, combine_here[:, b, use - 1:use], x_row,
                                                     ALU.mult, ALU.add).then_inc(out_read[b], 1)

            group(0)
            with dve.Fori(1, GROUPS) as g:
                group(g)


def store_x(nc, keep, out):
    with ExitStack() as stack:
        stored = stack.enter_context(nc.semaphore("x_stored"))
        block = stack.enter_context(nc.Block())

        @block.sync
        def _(sp):
            sp.dma_start(out.rearrange("b s d -> s b d"), keep.x[:, :, :]).then_inc(stored, 16)
            sp.wait_ge(stored, 16)


class Keep:

    def __init__(self, nc, stack, ident_in):
        scope = Scope(nc, stack, "keep_")
        self.x = scope.sb("x", [S, B, D])
        self.stats = scope.sb("stats", [S, B, 6])
        self.moments = scope.sb("moments", [S, B, 2])
        self.rstd = scope.sb("rstd", [S, B])
        self.ident = scope.sb("ident", [128, 128])
        self.eps = scope.sb("eps", [128, 1])
        self.masked_score = scope.sb("masked_score", [128, 1])
        self.one = scope.sb("one", [128, 1])
        loaded = scope.sem("loaded")
        with nc.Block() as block:
            @block.sync
            def _(sp):
                sp.dma_start(self.ident[:, :], ident_in).then_inc(loaded, 16)
                sp.wait_ge(loaded, 16)

            @block.vector
            def _(dve):
                dve.memset(self.eps[:, :], EPS)
                dve.memset(self.one[:, :], 1.0)
                dve.memset(self.masked_score[:, :], -1e-9)


def decoder(nc, t, out):
    with ExitStack() as stack:
        keep = Keep(nc, stack, t["ident"])
        load_and_first_stats(nc, keep, t["x"])
        if 1 in PHASES:
            layernorm_scales(nc, keep, "n1_")
            mamba(nc, keep, "mb_", t)
        if 2 in PHASES:
            layernorm_scales(nc, keep, "n2_")
            cross_attention(nc, keep, "xa0_", t["ctx_t"], t["x0_wq_t"], t["x0_wk_t"], t["x0_wv_t"], t["x0_wo_t"],
                            t["x0_bq_cols"], t["x0_bk_cols"], t["x0_bv"], t["x0_bo"], t["own_head"],
                            t["mask"], t["mask_t"], None)
        if 3 in PHASES:
            layernorm_scales(nc, keep, "n3_")
            switch_ffn(nc, keep, "sf_", t)
        if 4 in PHASES:
            layernorm_scales(nc, keep, "n4_")
            agent_attention(nc, keep, "ag_", t)
        if 5 in PHASES:
            layernorm_scales(nc, keep, "n5_")
            cross_attention(nc, keep, "xa1_", t["ctx_t"], t["x1_wq_t"], t["x1_wk_t"], t["x1_wv_t"], t["x1_wo_t"],
                            None, None, None, t["x1_bo"], t["own_head"], None, None, t["key_mask"])
        if 6 in PHASES:
            layernorm_scales(nc, keep, "n6_")
            latent_moe(nc, keep, "lm_", t)
        store_x(nc, keep, out)


def kernel(**inputs):
    import concourse.bacc as bacc
    from concourse.bass_utils import run_bass_kernel_spmd

    a = {n: np.ascontiguousarray(v) for n, v in inputs.items()}

    def t_(v):
        return np.ascontiguousarray(np.swapaxes(v, -1, -2))

    def cols(v):
        return np.ascontiguousarray(v.reshape(-1, 128).T)

    own_head = np.kron(np.eye(128 // DK), np.ones((DK, 1))).astype(np.float32) * np.float32(DK ** -0.5)
    own_latent_head = np.kron(np.eye(H), np.ones((KPH, 1))).astype(np.float32)
    arrays = {
        "x": a["x"], "ident": np.eye(128, dtype=np.float32), "own_head": own_head, "own_latent_head": own_latent_head,
        "upto": np.triu(np.ones((S, S), np.float32)),
        "own_row": np.tile(np.kron(np.eye(32, dtype=np.float32)[:, 16:], np.ones((1, 128), np.float32)), (3, 1)),
        "ctx_t": t_(a["ctx_1024"]),
        "mask": a["mask_1x1xSxS2_if1"].reshape(S, SK), "mask_t": t_(a["mask_1x1xSxS2_if1"].reshape(S, SK)),
        "key_mask": a["mask_BxS2_bf1"].view(np.uint8),
        "x0_wq_t": t_(a["L0_xattn_wq"]), "x0_wk_t": t_(a["L0_xattn_wk"]), "x0_wv_t": t_(a["L0_xattn_wv"]),
        "x0_wo_t": t_(a["L0_xattn_wo"]), "x0_bq_cols": cols(a["L0_xattn_bq"]), "x0_bk_cols": cols(a["L0_xattn_bk"]),
        "x0_bv": a["L0_xattn_bv"], "x0_bo": a["L0_xattn_bo"],
        "x1_wq_t": t_(a["L1_xattn_Wq"]), "x1_wk_t": t_(a["L1_xattn_Wk"]), "x1_wv_t": t_(a["L1_xattn_Wv"]),
        "x1_wo_t": t_(a["L1_xattn_Wo"]), "x1_bo": a["L1_xattn_bo"],
        "w_in": a["L0_attn_W_in"], "conv": np.ascontiguousarray(a["L0_attn_dw_kernel"].reshape(4, 4, 128).transpose(2, 1, 0)),
        "pw": a["L0_attn_pw_kernel"], "conv_bias": cols(a["L0_attn_conv_bias"]),
        "w_x": a["L0_attn_W_x"], "w_dt": a["L0_attn_W_dt"], "b_dt": cols(a["L0_attn_b_dt"]),
        "a_log": np.ascontiguousarray(a["L0_attn_A_log"].reshape(4, 128, 8).transpose(1, 0, 2)),
        "skip": cols(a["L0_attn_D"]), "w_out": a["L0_attn_W_out"],
        "gate": a["L0_ffn_Wg"], "expert": a["L0_ffn_We"], "expert_bias": a["L0_ffn_be"],
        "qkv": a["L1_attn_w_qkv"], "qkv_t": t_(a["L1_attn_w_qkv"]), "conv1": cols(a["L1_attn_w_conv1"]),
        "m_wq": np.ascontiguousarray(a["L1_ffn_q_w"].reshape(D, H, DK)[:, :, :KPH].reshape(D, H * KPH)),
        "m_bq": np.ascontiguousarray(a["L1_ffn_q_b"].reshape(H, DK)[:, :KPH].reshape(H * KPH, 1)),
        "m_wk": a["L1_ffn_k_w"], "m_bk": cols(a["L1_ffn_k_b"]), "m_wv": a["L1_ffn_v_w"], "m_bv": a["L1_ffn_v_b"],
        "m_wo": a["L1_ffn_o_w"], "m_bo": cols(a["L1_ffn_o_b"]), "m_router": a["L1_ffn_router_w"],
        "m_router_b": a["L1_ffn_router_b"], "m_w1": a["L1_ffn_w1"],
        "m_b1": np.ascontiguousarray(a["L1_ffn_b1"].reshape(8, 4, 128).transpose(2, 0, 1)),
        "m_w2": a["L1_ffn_w2"], "m_b2": a["L1_ffn_b2"],
    }
    nc = bacc.Bacc("TRN2", target_bir_lowering=False, num_devices=1)
    tensors = {n: nc.dram_tensor(f"in_{n}", v.shape, mybir.dt.from_np(v.dtype), kind="ExternalInput").ap()
               for n, v in arrays.items()}
    out = nc.dram_tensor("out_x", (B, S, D), F32, kind="ExternalOutput").ap()
    decoder(nc, tensors, out)
    result = run_bass_kernel_spmd(nc, [{f"in_{n}": v for n, v in arrays.items()}], core_ids=[0])
    return result.results[0]["out_x"]
```
